# Optimizing a Trainium2 kernel written in Bass

```python
import numpy as np
import jax
import jax.numpy as jnp

def _softmax(x, axis=-1):
    return jax.nn.softmax(x, axis=axis)

def _gelu(x):
    return jax.nn.gelu(x, approximate=True)

def _silu(x):
    return jax.nn.silu(x)

def _sigmoid(x):
    return jax.nn.sigmoid(x)

def _layernorm(x, axis=-1, eps=1e-05):
    m = jnp.mean(x, axis=axis, keepdims=True)
    v = jnp.var(x, axis=axis, keepdims=True)
    return (x - m) / jnp.sqrt(v + eps)

def _scatter_add(tgt, idx, src, axis=0):
    return tgt.at[idx].add(src)

def _segment_sum(src, seg, n):
    return jax.ops.segment_sum(src, seg, n)
kernel_name = 'mk_prb_d2_jaxref_r4_8214af'

def setup_inputs(seed: int=0):
    np.random.seed(seed)
    _w = jnp.asarray

    def _L0_attn_setup():
        import jax, jax.numpy as jnp
        import numpy as np
        B, T, C = (4, 1024, 256)
        H = 16
        LS = 64
        EPS = 1e-06

        def rmsnorm(x, w):
            xf = x.astype(jnp.float32)
            y = xf * jax.lax.rsqrt(jnp.mean(xf * xf, axis=-1, keepdims=True) + EPS)
            return y.astype(x.dtype) * w
        key = jax.random.key(seed)
        k1, k2, k3 = jax.random.split(key, 3)
        x = jax.random.normal(k1, (B, T, C), dtype=jnp.float32)
        w_qkv = jax.random.normal(k2, (C, 3 * C), dtype=jnp.float32) * (1.0 / np.sqrt(C))
        ln_w = jnp.ones((C,), dtype=jnp.float32)
        w_proj = jax.random.normal(k3, (C, C), dtype=jnp.float32) * (1.0 / np.sqrt(C))
        return {'x': x, 'w_qkv': w_qkv, 'ln_w': ln_w, 'w_proj': w_proj}
    _L0_attn_in = _L0_attn_setup()

    def _L0_ffn_setup():
        import jax, jax.numpy as jnp
        import numpy as np
        D_MODEL = 256
        EXPERT_DIM = 256
        NUM_EXPERTS = 8
        TOP_K = 2
        B, T = (8, 1024)
        key = jax.random.key(seed)
        ks = jax.random.split(key, 5)
        scale_in = 1.0 / np.sqrt(D_MODEL)
        scale_h = 1.0 / np.sqrt(EXPERT_DIM)
        return {'x': jax.random.normal(ks[0], (B, T, D_MODEL), dtype=jnp.float32), 'gate_w': jax.random.normal(ks[1], (D_MODEL, NUM_EXPERTS), dtype=jnp.float32) * scale_in, 'gate_b': jnp.zeros((NUM_EXPERTS,), dtype=jnp.float32), 'w1': jax.random.normal(ks[2], (NUM_EXPERTS, D_MODEL, EXPERT_DIM), dtype=jnp.float32) * scale_in, 'b1': jnp.zeros((NUM_EXPERTS, EXPERT_DIM), dtype=jnp.float32), 'w2': jax.random.normal(ks[3], (NUM_EXPERTS, EXPERT_DIM, D_MODEL), dtype=jnp.float32) * scale_h, 'b2': jnp.zeros((NUM_EXPERTS, D_MODEL), dtype=jnp.float32)}
    _L0_ffn_in = _L0_ffn_setup()

    def _L1_attn_setup():
        import jax, jax.numpy as jnp
        import numpy as np
        B, N, D, H = (4, 1024, 256, 16)
        HD = D // H
        MLP = 4 * D

        def _ln(x, w, b):
            m = x.mean(-1, keepdims=True)
            v = x.var(-1, keepdims=True)
            return (x - m) / jnp.sqrt(v + 1e-05) * w + b
        key = jax.random.key(seed)
        ks = jax.random.split(key, 12)
        s = 1.0 / np.sqrt(D)
        sm = 1.0 / np.sqrt(MLP)
        return {'q_x': jax.random.normal(ks[0], (B, N, D), jnp.float32), 'ln1_w': jnp.ones((D,), jnp.float32), 'ln1_b': jnp.zeros((D,), jnp.float32), 'wq': jax.random.normal(ks[1], (D, D), jnp.float32) * s, 'bq': jnp.zeros((D,), jnp.float32), 'wk': jax.random.normal(ks[2], (D, D), jnp.float32) * s, 'bk': jnp.zeros((D,), jnp.float32), 'wv': jax.random.normal(ks[3], (D, D), jnp.float32) * s, 'bv': jnp.zeros((D,), jnp.float32), 'wo': jax.random.normal(ks[4], (D, D), jnp.float32) * s, 'bo': jnp.zeros((D,), jnp.float32), 'ln2_w': jnp.ones((D,), jnp.float32), 'ln2_b': jnp.zeros((D,), jnp.float32), 'fc_w': jax.random.normal(ks[5], (D, MLP), jnp.float32) * s, 'fc_b': jnp.zeros((MLP,), jnp.float32), 'proj_w': jax.random.normal(ks[6], (MLP, D), jnp.float32) * sm, 'proj_b': jnp.zeros((D,), jnp.float32)}
    _L1_attn_in = _L1_attn_setup()

    def _L1_ffn_setup():
        import jax, jax.numpy as jnp
        import numpy as np
        DIM = 256
        DEPTH = 2
        HEADS = 8
        DIM_HEAD = 64
        WINDOW = 128
        INNER = HEADS * DIM_HEAD
        HID = int(DIM * 4 * 2 / 3)
        B, N = (2, 2048)
        QK_SCALE = 8.0

        def shift_token(t):
            t1, t2 = jnp.split(t, 2, axis=-1)
            t2 = jnp.pad(t2, ((0, 0), (1, 0), (0, 0)))[:, :-1]
            return jnp.concatenate([t1, t2], axis=-1)

        def l2norm(t):
            return t / jnp.clip(jnp.linalg.norm(t, axis=-1, keepdims=True), 1e-12)

        def rotate_half(x):
            x1, x2 = jnp.split(x, 2, axis=-1)
            return jnp.concatenate([-x2, x1], axis=-1)

        def rotary_xpos(q, k):
            n = q.shape[-2]
            half_idx = jnp.arange(0, DIM_HEAD, 2, dtype=jnp.float32)
            inv_freq = 1.0 / 10000.0 ** (half_idx / DIM_HEAD)
            t = jnp.arange(n, dtype=jnp.float32)
            freqs = t[:, None] * inv_freq[None, :]
            freqs = jnp.concatenate([freqs, freqs], axis=-1)
            base = (half_idx + 0.4 * DIM_HEAD) / (1.4 * DIM_HEAD)
            power = (t - n // 2) / float(WINDOW // 2)
            scale = base[None, :] ** power[:, None]
            scale = jnp.concatenate([scale, scale], axis=-1)
            cos, sin = (jnp.cos(freqs), jnp.sin(freqs))
            q = q * cos * scale + rotate_half(q) * sin * scale
            k = k * cos / scale + rotate_half(k) * sin / scale
            return (q, k)

        def local_attention(q, k, v):
            b, h, n, d = q.shape
            w = n // WINDOW
            bq = q.reshape(b, h, w, WINDOW, d) * QK_SCALE
            bk = k.reshape(b, h, w, WINDOW, d)
            bv = v.reshape(b, h, w, WINDOW, d)

            def look_around(t):
                p = jnp.pad(t, ((0, 0), (0, 0), (1, 0), (0, 0), (0, 0)))
                return jnp.concatenate([p[:, :, :w], p[:, :, 1:]], axis=3)
            bk, bv = (look_around(bk), look_around(bv))
            bt = jnp.arange(n).reshape(w, WINDOW)
            btp = jnp.pad(bt, ((1, 0), (0, 0)), constant_values=-1)
            btk = jnp.concatenate([btp[:w], btp[1:]], axis=1)
            sim = jnp.einsum('bhwid,bhwjd->bhwij', bq, bk)
            i = bt[:, :, None]
            j = btk[:, None, :]
            mask = (i < j) | (i > j + WINDOW) | (j == -1)
            sim = jnp.where(mask, -jnp.finfo(sim.dtype).max, sim)
            attn = jax.nn.softmax(sim, axis=-1)
            out = jnp.einsum('bhwij,bhwjd->bhwid', attn, bv)
            return out.reshape(b, h, n, d)

        def _layer(x, wqkv, qs, ksc, wo, lg, lb, w1, b1, w2, b2):
            b, n, _ = x.shape
            h = shift_token(x)
            qkv = h @ wqkv
            q, k, v = jnp.split(qkv, 3, axis=-1)
            to_heads = lambda t: t.reshape(b, n, HEADS, DIM_HEAD).transpose(0, 2, 1, 3)
            q, k, v = (to_heads(q), to_heads(k), to_heads(v))
            q = l2norm(q) * qs
            k = l2norm(k) * ksc
            q, k = rotary_xpos(q, k)
            o = local_attention(q, k, v)
            o = o.transpose(0, 2, 1, 3).reshape(b, n, INNER)
            x = x + o @ wo
            h = shift_token(x)
            mu = h.mean(-1, keepdims=True)
            var = h.var(-1, keepdims=True)
            h = (h - mu) / jnp.sqrt(var + 1e-05) * lg + lb
            h = h @ w1 + b1
            a, g = jnp.split(h, 2, axis=-1)
            h = a * jax.nn.gelu(g, approximate=False)
            x = x + h @ w2 + b2
            return x
        key = jax.random.key(seed)
        ks = jax.random.split(key, 6)
        return {'x': jax.random.normal(ks[0], (B, N, DIM), jnp.float32), 'wqkv': jax.random.normal(ks[1], (DEPTH, DIM, 3 * INNER), jnp.float32) * 0.02, 'q_scale': jnp.ones((DEPTH, DIM_HEAD), jnp.float32), 'k_scale': jnp.ones((DEPTH, DIM_HEAD), jnp.float32), 'wo': jax.random.normal(ks[2], (DEPTH, INNER, DIM), jnp.float32) * 0.02, 'ln_g': jnp.ones((DEPTH, DIM), jnp.float32), 'ln_b': jnp.zeros((DEPTH, DIM), jnp.float32), 'w1': jax.random.normal(ks[3], (DEPTH, DIM, 2 * HID), jnp.float32) * 0.02, 'b1': jnp.zeros((DEPTH, 2 * HID), jnp.float32), 'w2': jax.random.normal(ks[4], (DEPTH, HID, DIM), jnp.float32) * 0.02, 'b2': jnp.zeros((DEPTH, DIM), jnp.float32)}
    _L1_ffn_in = _L1_ffn_setup()
    _d = {'L0_attn_x': _L0_attn_in['x'], 'L0_attn_w_qkv': _L0_attn_in['w_qkv'], 'L0_attn_ln_w': _L0_attn_in['ln_w'], 'L0_attn_w_proj': _L0_attn_in['w_proj'], 'L0_ffn_gate_w': _L0_ffn_in['gate_w'], 'L0_ffn_gate_b': _L0_ffn_in['gate_b'], 'L0_ffn_w1': _L0_ffn_in['w1'], 'L0_ffn_b1': _L0_ffn_in['b1'], 'L0_ffn_w2': _L0_ffn_in['w2'], 'L0_ffn_b2': _L0_ffn_in['b2'], 'L1_attn_ln1_w': _L1_attn_in['ln1_w'], 'L1_attn_ln1_b': _L1_attn_in['ln1_b'], 'L1_attn_wq': _L1_attn_in['wq'], 'L1_attn_bq': _L1_attn_in['bq'], 'L1_attn_wk': _L1_attn_in['wk'], 'L1_attn_bk': _L1_attn_in['bk'], 'L1_attn_wv': _L1_attn_in['wv'], 'L1_attn_bv': _L1_attn_in['bv'], 'L1_attn_wo': _L1_attn_in['wo'], 'L1_attn_bo': _L1_attn_in['bo'], 'L1_attn_ln2_w': _L1_attn_in['ln2_w'], 'L1_attn_ln2_b': _L1_attn_in['ln2_b'], 'L1_attn_fc_w': _L1_attn_in['fc_w'], 'L1_attn_fc_b': _L1_attn_in['fc_b'], 'L1_attn_proj_w': _L1_attn_in['proj_w'], 'L1_attn_proj_b': _L1_attn_in['proj_b'], 'L1_ffn_wqkv': _L1_ffn_in['wqkv'], 'L1_ffn_q_scale': _L1_ffn_in['q_scale'], 'L1_ffn_k_scale': _L1_ffn_in['k_scale'], 'L1_ffn_wo': _L1_ffn_in['wo'], 'L1_ffn_ln_g': _L1_ffn_in['ln_g'], 'L1_ffn_ln_b': _L1_ffn_in['ln_b'], 'L1_ffn_w1': _L1_ffn_in['w1'], 'L1_ffn_b1': _L1_ffn_in['b1'], 'L1_ffn_w2': _L1_ffn_in['w2'], 'L1_ffn_b2': _L1_ffn_in['b2']}
    _x0 = _d['L0_attn_x']
    _d['L0_attn_x'] = jax.random.normal(jax.random.fold_in(jax.random.key(seed), 1), (1, 4096, 256), dtype=_x0.dtype)
    del _x0
    return _d

def reference(L0_attn_x, L0_attn_w_qkv, L0_attn_ln_w, L0_attn_w_proj, L0_ffn_gate_w, L0_ffn_gate_b, L0_ffn_w1, L0_ffn_b1, L0_ffn_w2, L0_ffn_b2, L1_attn_ln1_w, L1_attn_ln1_b, L1_attn_wq, L1_attn_bq, L1_attn_wk, L1_attn_bk, L1_attn_wv, L1_attn_bv, L1_attn_wo, L1_attn_bo, L1_attn_ln2_w, L1_attn_ln2_b, L1_attn_fc_w, L1_attn_fc_b, L1_attn_proj_w, L1_attn_proj_b, L1_ffn_wqkv, L1_ffn_q_scale, L1_ffn_k_scale, L1_ffn_wo, L1_ffn_ln_g, L1_ffn_ln_b, L1_ffn_w1, L1_ffn_b1, L1_ffn_w2, L1_ffn_b2):

    def _L0_attn_ref(x, w_qkv, ln_w, w_proj):
        import jax, jax.numpy as jnp
        import numpy as np
        B, T, C = (4, 1024, 256)
        H = 16
        LS = 64
        EPS = 1e-06

        def rmsnorm(x, w):
            xf = x.astype(jnp.float32)
            y = xf * jax.lax.rsqrt(jnp.mean(xf * xf, axis=-1, keepdims=True) + EPS)
            return y.astype(x.dtype) * w
        Bx, Tx, Cx = x.shape
        ng = Tx // LS
        hd = Cx // H
        xg = x.reshape(Bx, ng, LS, Cx)
        qkv = jnp.einsum('bglc,cd->bgld', xg, w_qkv)
        q, k, v = jnp.split(qkv, 3, axis=-1)
        q = rmsnorm(q, ln_w)
        k = rmsnorm(k, ln_w)
        q = q.reshape(Bx, ng, LS, H, hd).transpose(0, 1, 3, 2, 4)
        k = k.reshape(Bx, ng, LS, H, hd).transpose(0, 1, 3, 2, 4)
        v = v.reshape(Bx, ng, LS, H, hd).transpose(0, 1, 3, 2, 4)
        scale = 1.0 / np.sqrt(hd)
        att = jnp.einsum('bghqd,bghkd->bghqk', q, k) * scale
        causal = jnp.tril(jnp.ones((LS, LS), dtype=bool))
        att = jnp.where(causal, att, -jnp.finfo(att.dtype).max)
        att = jax.nn.softmax(att, axis=-1)
        y = jnp.einsum('bghqk,bghkd->bghqd', att, v)
        y = y.transpose(0, 1, 3, 2, 4).reshape(Bx, Tx, Cx)
        return jnp.einsum('btc,cd->btd', y, w_proj)

    def _L0_ffn_ref(x, gate_w, gate_b, w1, b1, w2, b2):
        import jax, jax.numpy as jnp
        import numpy as np
        D_MODEL = 256
        EXPERT_DIM = 256
        NUM_EXPERTS = 8
        TOP_K = 2
        B, T = (8, 1024)
        b, t, d = x.shape
        xf = x.reshape(b * t, d)
        scores = xf @ gate_w + gate_b
        topk_s, topk_i = jax.lax.top_k(scores, TOP_K)
        n = xf.shape[0]
        comb = jnp.zeros_like(scores).at[jnp.arange(n)[:, None], topk_i].add(topk_s)
        h = jnp.maximum(jnp.einsum('nd,edh->neh', xf, w1) + b1, 0.0)
        eo = jnp.einsum('neh,ehd->ned', h, w2) + b2
        out = jnp.einsum('ne,ned->nd', comb, eo)
        return out.reshape(b, t, d)

    def _L1_attn_ref(q_x, ln1_w, ln1_b, wq, bq, wk, bk, wv, bv, wo, bo, ln2_w, ln2_b, fc_w, fc_b, proj_w, proj_b):
        import jax, jax.numpy as jnp
        import numpy as np
        B, N, D, H = (4, 1024, 256, 16)
        HD = D // H
        MLP = 4 * D

        def _ln(x, w, b):
            m = x.mean(-1, keepdims=True)
            v = x.var(-1, keepdims=True)
            return (x - m) / jnp.sqrt(v + 1e-05) * w + b
        b, n, c = q_x.shape
        xn = _ln(q_x, ln1_w, ln1_b)
        q = (xn @ wq + bq).reshape(b, n, H, HD).transpose(0, 2, 1, 3)
        k = (xn @ wk + bk).reshape(b, n, H, HD).transpose(0, 2, 1, 3)
        v = (xn @ wv + bv).reshape(b, n, H, HD).transpose(0, 2, 1, 3)
        fq = jax.nn.elu(q) + 1.0
        fk = jax.nn.elu(k) + 1.0
        kv = jnp.einsum('bhnd,bhne->bnde', fk, v)
        qkv = jnp.einsum('bhnd,bnde->bhne', fq, kv)
        k_sum = fk.sum(axis=1)
        qk = jnp.einsum('bhnd,bnd->bhn', fq, k_sum)
        attn = qkv / (qk[..., None] + 1e-06)
        attn = attn.transpose(0, 2, 1, 3).reshape(b, n, c)
        attn = attn @ wo + bo
        x = q_x + attn
        h = _ln(x, ln2_w, ln2_b)
        h = jax.nn.gelu(h @ fc_w + fc_b, approximate=False)
        return x + (h @ proj_w + proj_b)

    def _L1_ffn_ref(x, wqkv, q_scale, k_scale, wo, ln_g, ln_b, w1, b1, w2, b2):
        import jax, jax.numpy as jnp
        import numpy as np
        DIM = 256
        DEPTH = 2
        HEADS = 8
        DIM_HEAD = 64
        WINDOW = 128
        INNER = HEADS * DIM_HEAD
        HID = int(DIM * 4 * 2 / 3)
        B, N = (2, 2048)
        QK_SCALE = 8.0

        def shift_token(t):
            t1, t2 = jnp.split(t, 2, axis=-1)
            t2 = jnp.pad(t2, ((0, 0), (1, 0), (0, 0)))[:, :-1]
            return jnp.concatenate([t1, t2], axis=-1)

        def l2norm(t):
            return t / jnp.clip(jnp.linalg.norm(t, axis=-1, keepdims=True), 1e-12)

        def rotate_half(x):
            x1, x2 = jnp.split(x, 2, axis=-1)
            return jnp.concatenate([-x2, x1], axis=-1)

        def rotary_xpos(q, k):
            n = q.shape[-2]
            half_idx = jnp.arange(0, DIM_HEAD, 2, dtype=jnp.float32)
            inv_freq = 1.0 / 10000.0 ** (half_idx / DIM_HEAD)
            t = jnp.arange(n, dtype=jnp.float32)
            freqs = t[:, None] * inv_freq[None, :]
            freqs = jnp.concatenate([freqs, freqs], axis=-1)
            base = (half_idx + 0.4 * DIM_HEAD) / (1.4 * DIM_HEAD)
            power = (t - n // 2) / float(WINDOW // 2)
            scale = base[None, :] ** power[:, None]
            scale = jnp.concatenate([scale, scale], axis=-1)
            cos, sin = (jnp.cos(freqs), jnp.sin(freqs))
            q = q * cos * scale + rotate_half(q) * sin * scale
            k = k * cos / scale + rotate_half(k) * sin / scale
            return (q, k)

        def local_attention(q, k, v):
            b, h, n, d = q.shape
            w = n // WINDOW
            bq = q.reshape(b, h, w, WINDOW, d) * QK_SCALE
            bk = k.reshape(b, h, w, WINDOW, d)
            bv = v.reshape(b, h, w, WINDOW, d)

            def look_around(t):
                p = jnp.pad(t, ((0, 0), (0, 0), (1, 0), (0, 0), (0, 0)))
                return jnp.concatenate([p[:, :, :w], p[:, :, 1:]], axis=3)
            bk, bv = (look_around(bk), look_around(bv))
            bt = jnp.arange(n).reshape(w, WINDOW)
            btp = jnp.pad(bt, ((1, 0), (0, 0)), constant_values=-1)
            btk = jnp.concatenate([btp[:w], btp[1:]], axis=1)
            sim = jnp.einsum('bhwid,bhwjd->bhwij', bq, bk)
            i = bt[:, :, None]
            j = btk[:, None, :]
            mask = (i < j) | (i > j + WINDOW) | (j == -1)
            sim = jnp.where(mask, -jnp.finfo(sim.dtype).max, sim)
            attn = jax.nn.softmax(sim, axis=-1)
            out = jnp.einsum('bhwij,bhwjd->bhwid', attn, bv)
            return out.reshape(b, h, n, d)

        def _layer(x, wqkv, qs, ksc, wo, lg, lb, w1, b1, w2, b2):
            b, n, _ = x.shape
            h = shift_token(x)
            qkv = h @ wqkv
            q, k, v = jnp.split(qkv, 3, axis=-1)
            to_heads = lambda t: t.reshape(b, n, HEADS, DIM_HEAD).transpose(0, 2, 1, 3)
            q, k, v = (to_heads(q), to_heads(k), to_heads(v))
            q = l2norm(q) * qs
            k = l2norm(k) * ksc
            q, k = rotary_xpos(q, k)
            o = local_attention(q, k, v)
            o = o.transpose(0, 2, 1, 3).reshape(b, n, INNER)
            x = x + o @ wo
            h = shift_token(x)
            mu = h.mean(-1, keepdims=True)
            var = h.var(-1, keepdims=True)
            h = (h - mu) / jnp.sqrt(var + 1e-05) * lg + lb
            h = h @ w1 + b1
            a, g = jnp.split(h, 2, axis=-1)
            h = a * jax.nn.gelu(g, approximate=False)
            x = x + h @ w2 + b2
            return x
        for l in range(DEPTH):
            x = _layer(x, wqkv[l], q_scale[l], k_scale[l], wo[l], ln_g[l], ln_b[l], w1[l], b1[l], w2[l], b2[l])
        return x
    x = L0_attn_x
    xn = _layernorm(x, axis=-1)
    x = x + _L0_attn_ref(xn, L0_attn_w_qkv, L0_attn_ln_w, L0_attn_w_proj) + _L0_ffn_ref(xn, L0_ffn_gate_w, L0_ffn_gate_b, L0_ffn_w1, L0_ffn_b1, L0_ffn_w2, L0_ffn_b2)
    xn = _layernorm(x, axis=-1)
    x = x + _L1_attn_ref(xn, L1_attn_ln1_w, L1_attn_ln1_b, L1_attn_wq, L1_attn_bq, L1_attn_wk, L1_attn_bk, L1_attn_wv, L1_attn_bv, L1_attn_wo, L1_attn_bo, L1_attn_ln2_w, L1_attn_ln2_b, L1_attn_fc_w, L1_attn_fc_b, L1_attn_proj_w, L1_attn_proj_b) + _L1_ffn_ref(xn, L1_ffn_wqkv, L1_ffn_q_scale, L1_ffn_k_scale, L1_ffn_wo, L1_ffn_ln_g, L1_ffn_ln_b, L1_ffn_w1, L1_ffn_b1, L1_ffn_w2, L1_ffn_b2)
    return x

_drawn_inputs = setup_inputs


def setup_inputs(seed=0):
    import zlib

    import numpy as np

    out = dict(_drawn_inputs(seed))
    spreads = {'L0_attn_ln_w': (1.0, 0.2),
     'L0_ffn_gate_b': (0.0, 0.1),
     'L0_ffn_b1': (0.0, 0.1),
     'L0_ffn_b2': (0.0, 0.1),
     'L1_attn_ln1_w': (1.0, 0.6),
     'L1_attn_ln1_b': (0.0, 2.0),
     'L1_attn_bq': (0.0, 2.0),
     'L1_attn_bk': (0.0, 2.0),
     'L1_attn_bv': (0.0, 2.0),
     'L1_attn_bo': (0.0, 0.8),
     'L1_attn_ln2_w': (1.0, 0.6),
     'L1_attn_ln2_b': (0.0, 2.0),
     'L1_attn_fc_b': (0.0, 2.0),
     'L1_attn_proj_b': (0.0, 1.361),
     'L1_ffn_q_scale': (1.0, 0.6),
     'L1_ffn_k_scale': (1.0, 0.6),
     'L1_ffn_ln_g': (1.0, 0.6),
     'L1_ffn_ln_b': (0.0, 0.8),
     'L1_ffn_b1': (0.0, 0.8),
     'L1_ffn_b2': (0.0, 0.421)}
    factors = {'L1_attn_wq': 29.394,
     'L1_attn_wk': 13.767,
     'L1_ffn_wqkv': 4.068,
     'L1_ffn_wo': 4.069,
     'L1_ffn_w1': 4.369,
     'L1_ffn_w2': 4.347}
    for name, (base, spread) in spreads.items():
        noise = np.random.default_rng([zlib.crc32(name.encode()), seed]).standard_normal(out[name].shape)
        drawn = base * np.exp(spread * noise) if base else spread * noise
        out[name] = jnp.asarray(drawn.astype(out[name].dtype))
    for name, factor in factors.items():
        out[name] = (out[name] * factor).astype(out[name].dtype)
    return out
```

```python
from contextlib import ExitStack

import concourse.bass as bass
from concourse import mybir

F32 = mybir.dt.float32
BF16 = mybir.dt.bfloat16
U32 = mybir.dt.uint32
ALU = mybir.AluOpType
ACT = mybir.ActivationFunctionType
AX = mybir.AxisListType.X

P = 128
C = 256
NCH = C // P
NT = 4096
SUBS = 4
BT = SUBS * P
NB = NT // BT
H16, D16 = 16, 16
NE, ED = 8, 256
MLP = 1024
H8, D64 = 8, 64
INNER = D64 * H8
HID = 682
HCH = (HID + P - 1) // P
EPS_LN, EPS_RMS = 1e-5, 1e-6
NORM_FLOOR = 1e-24
QK_SCALE = 8.0
PADDED = ("xn1", "xm0", "xl1", "xm1")


class Ring:

    def __init__(self, banks, sem, order):
        n = len(banks)
        self.banks = banks
        self.full_sems = [sem(f"bank{b}_full") for b in range(n)]
        self.free_sems = [sem(f"bank{b}_free") for b in range(n)]
        self.at = {tag: (u % n, u // n) for u, tag in enumerate(order)}
        self.per = [len(range(b, len(order), n)) for b in range(n)]

    def bank(self, tag):
        return self.banks[self.at[tag][0]]

    def full(self, tag):
        return self.full_sems[self.at[tag][0]]

    def free(self, tag):
        return self.free_sems[self.at[tag][0]]

    def space(self, tag, i):
        b, k = self.at[tag]
        return self.free_sems[b], i * self.per[b] + (k + 1)

    def data(self, tag, i):
        b, k = self.at[tag]
        return self.full_sems[b], i * self.per[b] + (k + 1)

    def copied(self, tag, i):
        b, k = self.at[tag]
        return self.free_sems[b], i * self.per[b] + (k + 2)

    def open(self, eng):
        for s in self.free_sems:
            eng.sem_inc(s, 1)


def blocks_loop(eng, body):
    with eng.Fori(0, NB - 1) as i:
        body(i, True)
    body(NB - 1, False)


def token_rows(ap, i, first=0, c0=0, c1=C):
    return ap[bass.ds(i * BT + first, BT), c0:c1].rearrange("(s p) c -> p s c", p=P)


def nth(i, s):
    return i * SUBS + (s + 1)


def row_stats(dve, x, st, mv):
    for s in range(SUBS):
        dve.bn_stats(st[:, s, :], x[:, s, :])
    dve.drain()
    for s in range(SUBS):
        r = dve.bn_aggr(mv[:, s, :], st[:, s, :])
    return r


def inverse_root(pool, out, x, eps, neghalf):
    pool.tensor_tensor(out, x, eps, ALU.add)
    pool.drain()
    return pool.tensor_tensor(out, out, neghalf, ALU.pow)


def normalise(dve, xn, x, mv, rs):
    for s in range(SUBS):
        r = dve.tensor_scalar(xn[:, s, :], x[:, s, :], mv[:, s, 0:1], rs[:, s:s + 1], ALU.subtract, ALU.mult)
    return r


def turn_block(pe, ring, tags, i, x, ident):
    for c, tag in enumerate(tags):
        pe.wait_ge(*ring.space(tag, i))
        for s in range(SUBS):
            mm = pe.transpose(ring.bank(tag)[:, s * P:(s + 1) * P], x[:, s, c * P:(c + 1) * P], ident[:, :])
        mm.then_inc(ring.full(tag), 1)


def chunks(ap):
    return ap.rearrange("(c p) n -> p c n", p=P)


def column(ap):
    return ap.rearrange("(c p) -> p c", p=P)


def build(nc, t_in, out, scratch):
    stack = ExitStack()
    with stack:
        def sb(name, shape, dt=F32):
            return stack.enter_context(nc.sbuf_tensor(name, shape, dt))

        semaphores = {}

        def sems(prefix):
            def sem(name):
                if prefix + name not in semaphores:
                    semaphores[prefix + name] = stack.enter_context(nc.semaphore(prefix + name))
                return semaphores[prefix + name]
            return sem

        def clear(prefixes):
            with nc.Block() as block:

                @block.gpsimd
                def _(pool):
                    for name, s in semaphores.items():
                        if name.startswith(prefixes):
                            pool.sem_clear(s)

        used = []

        def buffers(ctx, prefix):
            used.append(prefix)
            turn = f"{prefix}{used.count(prefix)}_"
            return lambda name, shape, dt=F32: ctx.enter_context(nc.sbuf_tensor(turn + name, shape, dt))

        stack.enter_context(nc.allow_non_contiguous_dma(reason="biases, a column per partition: a few KB"))
        banks = [stack.enter_context(nc.psum_tensor(f"bank{b}", [P, 512], F32)) for b in range(4)]
        wide = stack.enter_context(nc.psum_tensor("wide", [P, 4, 512], F32))
        shared = {
            "ident": sb("ident", [P, P]),
            "identb": sb("identb", [P, P], BF16),
            "neghalf": sb("neghalf", [P, 2 * H8]),
            "eps_ln": sb("eps_ln", [P, SUBS]),
            "eps_rms": sb("eps_rms", [P, 2]),
        }
        local = [local_weights(sb, sems(f"w{n}_"), t_in, n) for n in range(2)]
        load_constants(nc, sb, sems("c_"), shared, t_in, scratch)
        first_stage(nc, buffers, sems("a_"), banks, wide, shared, t_in, scratch, local)
        linear = linear_weights(sb, sems("wl_"), t_in)
        for n, (src, mid, dst) in enumerate((("xn1", "xm0", "xl1"), ("xl1", "xm1", "xl2"))):
            local_attention(nc, buffers, sems("d_"), banks, wide, shared, t_in, scratch, local[n], src, mid,
                            [linear] if n == 0 else [])
            local_ffn(nc, buffers, sems("f_"), banks, wide, shared, t_in, scratch, local[n], mid, dst)
            if n == 0:
                clear(("d_", "f_"))
        linear_stage(nc, buffers, sems("l_"), banks, wide, shared, t_in, scratch, linear, out)


def local_weights(sb, sem, t_in, n):
    w = {"loaded": sem("loaded"), "loads": []}

    def add(name, shape, src):
        w[name] = sb(f"{name}_{n}", shape)
        if src is not None:
            w["loads"].append((w[name], src))

    full = HID // P * P
    add("wqkv", [P, NCH, 3 * INNER], chunks(t_in["L1_ffn_wqkv"][n]))
    add("wo", [P, INNER // P, C], chunks(t_in["L1_ffn_wo"][n]))
    add("w1", [P, NCH, 2 * HID], chunks(t_in["L1_ffn_w1"][n]))
    add("w2", [P, HCH, C], None)
    w["loads"].append((w["w2"][:, 0:HID // P, :], chunks(t_in["L1_ffn_w2"][n, 0:full])))
    w["loads"].append((w["w2"][0:HID - full, HID // P, :], t_in["L1_ffn_w2"][n, full:HID]))
    add("b1", [P, 2, HCH], None)
    for t in range(2):
        a = t * HID
        w["loads"].append((w["b1"][:, t, 0:HID // P], column(t_in["L1_ffn_b1"][n, a:a + full])))
        w["loads"].append((w["b1"][0:HID - full, t, HID // P:HCH],
                           t_in["L1_ffn_b1"][n, a + full:a + HID].rearrange("(p a) -> p a", a=1)))
    add("b2", [P, C], t_in["L1_ffn_b2"][n].partition_broadcast(P))
    add("lg", [P, NCH], column(t_in["L1_ffn_ln_g"][n]))
    add("lb", [P, NCH], column(t_in["L1_ffn_ln_b"][n]))
    for name in ("q_scale", "k_scale"):
        add(name, [P, D64], t_in[f"L1_ffn_{name}"][n].partition_broadcast(P))
        add(name + "_turned", [P, D64], None)
        for a in range(2):
            other = slice((1 - a) * D64 // 2, (2 - a) * D64 // 2)
            w["loads"].append((w[name + "_turned"][:, a * D64 // 2:(a + 1) * D64 // 2],
                               t_in[f"L1_ffn_{name}"][n, other].partition_broadcast(P)))
    return w


def linear_weights(sb, sem, t_in):
    w = {"loaded": sem("loaded"), "loads": []}
    w["wqkv"] = sb("l_wqkv", [P, NCH, 3 * C])
    w["bqkv"] = sb("l_bqkv", [P, 3 * C])
    for k, name in enumerate("qkv"):
        w["loads"].append((w["wqkv"][:, :, k * C:(k + 1) * C], chunks(t_in[f"L1_attn_w{name}"])))
        w["loads"].append((w["bqkv"][:, k * C:(k + 1) * C], t_in[f"L1_attn_b{name}"].partition_broadcast(P)))
    for name, shape, src in (
        ("wo", [P, NCH, C], chunks(t_in["L1_attn_wo"])),
        ("fc", [P, NCH, MLP], chunks(t_in["L1_attn_fc_w"])),
        ("proj", [P, MLP // P, C], chunks(t_in["L1_attn_proj_w"])),
        ("fcb", [P, MLP // P], column(t_in["L1_attn_fc_b"])),
        ("bo", [P, C], t_in["L1_attn_bo"].partition_broadcast(P)),
        ("projb", [P, C], t_in["L1_attn_proj_b"].partition_broadcast(P)),
        ("g1", [P, NCH], column(t_in["L1_attn_ln1_w"])),
        ("o1", [P, NCH], column(t_in["L1_attn_ln1_b"])),
        ("g2", [P, NCH], column(t_in["L1_attn_ln2_w"])),
        ("o2", [P, NCH], column(t_in["L1_attn_ln2_b"])),
    ):
        w[name] = sb("l_" + name, shape)
        w["loads"].append((w[name], src))
    return w


def whole(t):
    return t if isinstance(t, bass.AP) else t[tuple(slice(None) for _ in t.shape)]


def load_constants(nc, sb, sem, shared, t_in, scratch):
    zrow = sb("zrow", [1, C])
    loaded, zeroed, stored = sem("loaded"), sem("zeroed"), sem("stored")
    with nc.Block() as block:

        @block.sync
        def _(sp):
            sp.dma_start(shared["ident"][:, :], t_in["k_ident"]).then_inc(loaded, 16)
            sp.wait_ge(zeroed, 1)
            for name in PADDED:
                sp.dma_start(scratch[name][0:1, :], zrow[:, :]).then_inc(stored, 16)
            sp.wait_ge(stored, 16 * len(PADDED))

        @block.vector
        def _(dve):
            dve.memset(zrow[:, :], 0.0).then_inc(zeroed, 1)
            for name, value in (("neghalf", -0.5), ("eps_ln", EPS_LN), ("eps_rms", EPS_RMS)):
                dve.memset(shared[name][:, :], value)
            dve.wait_ge(loaded, 16)
            dve.tensor_copy(shared["identb"][:, :], shared["ident"][:, :])
            dve.drain()


def first_stage(nc, buffers, sem, banks, wide, shared, t_in, scratch, later):
    ctx = ExitStack()
    with ctx:
        sb = buffers(ctx, "a_")
        ident, identb, neghalf = shared["ident"], shared["identb"], shared["neghalf"]
        wqkv = sb("wqkv", [P, NCH, 3 * C])
        wproj = sb("wproj", [P, NCH, C])
        w1 = sb("w1", [P, NE, NCH, ED])
        w2 = sb("w2", [P, NE, ED // P, C])
        gw = sb("gw", [P, NCH, NE])
        gb = sb("gb", [P, NE])
        b1 = sb("b1", [P, NE, ED // P])
        b2 = sb("b2", [NE, C])
        lnw = sb("lnw", [P, C])
        iota = sb("iota", [P, NE])
        maskf = sb("maskf", [P, P])
        mask = sb("mask", [P, 4, P], BF16)
        xin = sb("xin", [P, SUBS, C])
        st = sb("st", [P, SUBS, 6])
        mv = sb("mv", [P, SUBS, 2])
        rs = sb("rs", [P, SUBS])
        xn = sb("xn", [P, SUBS, C])
        xT = sb("xT", [P, NCH, BT])
        xres = sb("xres", [P, SUBS, C])
        acc = sb("acc", [P, SUBS, C])
        st2 = sb("st2", [P, SUBS, 6])
        mv2 = sb("mv2", [P, SUBS, 2])
        rs2 = sb("rs2", [P, SUBS])
        xn1 = sb("xn1", [P, SUBS, C])
        score = sb("score", [P, SUBS, NE])
        top = sb("top", [P, SUBS, 8])
        topi = sb("topi", [P, SUBS, 8], U32)
        topf = sb("topf", [P, SUBS, 8])
        pick = sb("pick", [P, 2, SUBS, NE])
        comb = sb("comb", [P, SUBS, NE])
        combT = sb("combT", [NE, BT])
        sq = sb("sq", [P, 2, C])
        ss = sb("ss", [P, 2])
        rr = sb("rr", [P, 2])
        qk = sb("qk", [P, 2, H16, 32])
        v = sb("v", [P, 2, C])
        qkT = sb("qkT", [P, 2, 4, P])
        mx = sb("mx", [P, H16])
        nm = sb("nm", [P, H16])
        probs = sb("probs", [P, 4, 4, P])
        den = sb("den", [P, H16])
        rden = sb("rden", [P, H16])
        pT = sb("pT", [P, 4, 4, P])
        y = sb("y", [P, C])
        yT = sb("yT", [P, NCH, P])
        hT = sb("hT", [P, 2, ED // P, BT])

        order = ["xT0", "xT1", "gate", "qk0", "v0", "h0_0", "h0_1", "cT", "tq0", "tk0", "eo0_0", "eo0_1"]
        for s in range(SUBS):
            e = 2 * s + 1
            order += [f"h{e}_0", f"h{e}_1", f"eo{e}_0", f"eo{e}_1"]
            if s + 1 < SUBS:
                order += [f"qk{s + 1}", f"v{s + 1}", f"h{e + 1}_0", f"h{e + 1}_1"]
            order += [f"pv{s}"]
            if s + 1 < SUBS:
                order += [f"tq{s + 1}", f"tk{s + 1}", f"eo{e + 1}_0", f"eo{e + 1}_1"]
            order += [f"yT{s}", f"proj{s}"]
        ring = Ring(banks, sem, order)

        w_loaded, setup_done = sem("w_loaded"), sem("setup_done")
        x_loaded, res_loaded, res_used = sem("x_loaded"), sem("res_loaded"), sem("res_used")
        stats_ready, rs_ready, xn_ready = sem("stats_ready"), sem("rs_ready"), sem("xn_ready")
        comb_ready = sem("comb_ready")
        ss_ready, rr_ready = sem("ss_ready"), sem("rr_ready")
        scores_done, max_ready, probs_ready = sem("scores_done"), sem("max_ready"), sem("probs_ready")
        turned, pT_act, pT_dve = sem("turned"), sem("pT_act"), sem("pT_dve")
        y_ready = sem("y_ready")
        acc_ready, stats2_ready, rs2_ready, xn1_ready = (
            sem("acc_ready"), sem("stats2_ready"), sem("rs2_ready"), sem("xn1_ready"))
        stored = sem("stored")

        weights = (
            (gw[:, :, :], chunks(t_in["L0_ffn_gate_w"])),
            (wqkv[:, :, :], chunks(t_in["L0_attn_w_qkv"])),
            (gb[:, :], t_in["L0_ffn_gate_b"].partition_broadcast(P)),
            (lnw[:, :], t_in["L0_attn_ln_w"].partition_broadcast(P)),
            (b1[:, :, :], t_in["L0_ffn_b1"].rearrange("e (m p) -> p e m", p=P)),
            (b2[:, :], t_in["L0_ffn_b2"]),
            (iota[:, :], t_in["k_iota"].partition_broadcast(P)),
            (maskf[:, :], t_in["k_mask_group"]),
            (wproj[:, :, :], chunks(t_in["L0_attn_w_proj"])),
        ) + tuple(
            (dst[:, a:a + 4, :, :], src[a:a + 4].rearrange("e (c p) n -> p e c n", p=P))
            for a in (0, 4) for dst, src in ((w1, t_in["L0_ffn_w1"]), (w2, t_in["L0_ffn_w2"]))
        )

        with nc.Block() as block:

            @block.sync
            def _(sp):
                def load_x(i):
                    sp.dma_start(xin[:, :, :], token_rows(t_in["x"], i)).then_inc(x_loaded, 16)

                def load_res(i):
                    sp.dma_start(xres[:, :, :], token_rows(t_in["x"], i)).then_inc(res_loaded, 16)

                ring.open(sp)
                sp.sem_inc(stored, 32)
                load_x(0)
                load_res(0)
                for dst, src in weights:
                    sp.dma_start(dst, src).then_inc(w_loaded, 16)
                for group in later:
                    for dst, src in group["loads"]:
                        sp.dma_start(whole(dst), src).then_inc(group["loaded"], 16)

                def body(i, more):
                    if more:
                        sp.wait_ge(xn_ready, i + 1)
                        load_x(i + 1)
                        sp.wait_ge(res_used, i + 1)
                        load_res(i + 1)
                    sp.wait_ge(acc_ready, i + 1)
                    sp.dma_start(token_rows(scratch["x1"], i), acc[:, :, :]).then_inc(stored, 16)
                    sp.wait_ge(xn1_ready, i + 1)
                    sp.dma_start(token_rows(scratch["xn1"], i, 1), xn1[:, :, :]).then_inc(stored, 16)

                blocks_loop(sp, body)
                sp.wait_ge(stored, 32 * (NB + 1))

            @block.gpsimd
            def _(pool):
                def front(i):
                    pool.wait_ge(stats_ready, i + 1)
                    inverse_root(pool, rs[:, :], mv[:, :, 1], shared["eps_ln"][:, :], neghalf[:, 0:SUBS]).then_inc(rs_ready, 1)

                def rms(i, s):
                    pool.wait_ge(ss_ready, nth(i, s))
                    inverse_root(pool, rr[:, :], ss[:, :], shared["eps_rms"][:, :], neghalf[:, 0:2]).then_inc(rr_ready, 1)

                def body(i, more):
                    rms(i, 0)
                    rms(i, 1)
                    rms(i, 2)
                    if more:
                        front(i + 1)
                    rms(i, 3)
                    pool.wait_ge(stats2_ready, i + 1)
                    inverse_root(pool, rs2[:, :], mv2[:, :, 1], shared["eps_ln"][:, :], neghalf[:, 0:SUBS])\
                        .then_inc(rs2_ready, 1)

                front(0)
                blocks_loop(pool, body)

            @block.tensor
            def _(pe):
                def gate(i):
                    pe.wait_ge(*ring.space("gate", i))
                    o = ring.bank("gate")
                    for s in range(SUBS):
                        for c in range(NCH):
                            mm = pe.matmul(o[:, s * NE:(s + 1) * NE], xT[:, c, s * P:(s + 1) * P], gw[:, c, :],
                                           start=c == 0, stop=c == NCH - 1)
                    mm.then_inc(ring.full("gate"), 1)

                def qkv(i, s):
                    for tag, a, b in ((f"qk{s}", 0, 2 * C), (f"v{s}", 2 * C, 3 * C)):
                        pe.wait_ge(*ring.space(tag, i))
                        for c in range(NCH):
                            mm = pe.matmul(ring.bank(tag)[:, 0:b - a], xT[:, c, s * P:(s + 1) * P], wqkv[:, c, a:b],
                                           start=c == 0, stop=c == NCH - 1)
                        mm.then_inc(ring.full(tag), 1)

                def turn_qk(i, s):
                    pe.wait_ge(*ring.copied(f"qk{s}", i))
                    for t, tag in enumerate((f"tq{s}", f"tk{s}")):
                        pe.wait_ge(*ring.space(tag, i))
                        for g in range(4):
                            mm = pe.transpose(ring.bank(tag)[:, g * P:(g + 1) * P],
                                              qk[:, t, 4 * g:4 * g + 4, :].rearrange("p a b -> p (a b)"), ident[:, :])
                        mm.then_inc(ring.full(tag), 1)

                def expert_in(i, e):
                    for m in range(ED // P):
                        tag = f"h{e}_{m}"
                        pe.wait_ge(*ring.space(tag, i))
                        for c in range(NCH):
                            mm = pe.matmul(ring.bank(tag)[:, :], w1[:, e, c, m * P:(m + 1) * P], xT[:, c, :],
                                           start=c == 0, stop=c == NCH - 1)
                        mm.then_inc(ring.full(tag), 1)

                def expert_out(i, e):
                    for m in range(ED // P):
                        pe.wait_ge(*ring.copied(f"h{e}_{m}", i))
                    for n in range(2):
                        tag = f"eo{e}_{n}"
                        pe.wait_ge(*ring.space(tag, i))
                        for s in (2 * n, 2 * n + 1):
                            for m in range(ED // P):
                                mm = pe.matmul(ring.bank(tag)[:, (s % 2) * C:(s % 2 + 1) * C],
                                               hT[:, e % 2, m, s * P:(s + 1) * P],
                                               w2[:, e, m, :], start=m == 0, stop=m == ED // P - 1)
                        mm.then_inc(ring.full(tag), 1)

                def turn_comb(i):
                    pe.wait_ge(comb_ready, i + 1)
                    pe.wait_ge(*ring.space("cT", i))
                    for s in range(SUBS):
                        mm = pe.transpose(ring.bank("cT")[0:NE, s * P:(s + 1) * P], comb[:, s, :], ident[:, :])
                    mm.then_inc(ring.full("cT"), 1)

                def scores(i, s):
                    pe.wait_ge(*ring.copied(f"tq{s}", i))
                    pe.wait_ge(*ring.copied(f"tk{s}", i))
                    for j in range(4):
                        pe.matmul(wide[:, j, :], identb[:, :], mask[:, :, :].rearrange("p a b -> p (a b)"),
                                  start=True, stop=False)
                    for g in range(4):
                        for j in range(4):
                            r = slice(32 * j, 32 * j + D16)
                            mm = pe.matmul(wide[:, j, g * P:(g + 1) * P], qkT[r, 0, g, :], qkT[r, 1, g, :],
                                           start=False, stop=g == 3)
                    mm.then_inc(scores_done, 1)

                def turn_probs(i, s):
                    pe.wait_ge(probs_ready, nth(i, s))
                    for j in range(4):
                        for g in range(4):
                            mm = pe.transpose(wide[:, j, g * P:(g + 1) * P], probs[:, j, g, :], ident[:, :])
                    mm.then_inc(turned, 1)

                def values(i, s):
                    tag = f"pv{s}"
                    pe.wait_ge(pT_act, nth(i, s))
                    pe.wait_ge(pT_dve, nth(i, s))
                    pe.wait_ge(*ring.copied(f"v{s}", i))
                    pe.wait_ge(*ring.space(tag, i))
                    for j in range(4):
                        for g in range(4):
                            h = slice((4 * g + j) * D16, (4 * g + j + 1) * D16)
                            mm = pe.matmul(ring.bank(tag)[:, h], pT[:, j, g, :], v[:, s % 2, h], start=True, stop=True)
                    mm.then_inc(ring.full(tag), 1)

                def project(i, s):
                    pe.wait_ge(y_ready, nth(i, s))
                    pe.wait_ge(*ring.space(f"yT{s}", i))
                    for c in range(NCH):
                        mm = pe.transpose(ring.bank(f"yT{s}")[:, c * P:(c + 1) * P], y[:, c * P:(c + 1) * P], ident[:, :])
                    mm.then_inc(ring.full(f"yT{s}"), 1)
                    o = ring.bank(f"proj{s}")
                    pe.wait_ge(*ring.space(f"proj{s}", i))
                    if s == 0:
                        pe.wait_ge(*ring.copied("cT", i))
                    pe.matmul(o[:, 0:C], combT[:, s * P:(s + 1) * P], b2[:, :], start=True, stop=False)
                    pe.wait_ge(*ring.copied(f"yT{s}", i))
                    for c in range(NCH):
                        mm = pe.matmul(o[:, 0:C], yT[:, c, :], wproj[:, c, :], start=False, stop=c == NCH - 1)
                    mm.then_inc(ring.full(f"proj{s}"), 1)

                def body(i, more):
                    pe.wait_ge(xn_ready, i + 1)
                    turn_block(pe, ring, ("xT0", "xT1"), i, xn, ident)
                    for tag in ("xT0", "xT1"):
                        pe.wait_ge(*ring.copied(tag, i))
                    gate(i)
                    qkv(i, 0)
                    expert_in(i, 0)
                    turn_comb(i)
                    turn_qk(i, 0)
                    expert_out(i, 0)
                    for s in range(SUBS):
                        e = 2 * s + 1
                        scores(i, s)
                        expert_in(i, e)
                        expert_out(i, e)
                        turn_probs(i, s)
                        if s + 1 < SUBS:
                            qkv(i, s + 1)
                            expert_in(i, e + 1)
                        values(i, s)
                        if s + 1 < SUBS:
                            turn_qk(i, s + 1)
                            expert_out(i, e + 1)
                        project(i, s)

                pe.wait_ge(w_loaded, 16 * len(weights))
                pe.wait_ge(setup_done, 2)
                blocks_loop(pe, body)

            @block.scalar
            def _(act):
                def squares(i, s):
                    act.wait_ge(*ring.data(f"qk{s}", i))
                    for t in range(2):
                        r = act.activation(sq[:, t, :], ring.bank(f"qk{s}")[:, t * C:(t + 1) * C], ACT.Square,
                                           scale=C ** -0.5, accum_out=ss[:, t:t + 1])
                    r.then_inc(ss_ready, 1)

                def copy(i, tag, dst, src):
                    act.wait_ge(*ring.data(tag, i))
                    act.copy(dst, src).then_inc(ring.free(tag), 1)

                def hidden(i, e):
                    if e >= 2:
                        act.wait_ge(*ring.data(f"eo{e - 2}_1", i))
                    for m in range(ED // P):
                        tag = f"h{e}_{m}"
                        act.wait_ge(*ring.data(tag, i))
                        act.activation(hT[:, e % 2, m, :], ring.bank(tag)[:, :], ACT.Relu, bias=b1[:, e, m:m + 1])\
                           .then_inc(ring.free(tag), 1)

                def exponentials(i, s):
                    act.wait_ge(max_ready, nth(i, s))
                    for j in range(4):
                        for g in range(4):
                            n = 4 * j + g
                            r = act.activation(probs[:, j, g, :], wide[:, j, g * P:(g + 1) * P], ACT.Exp,
                                               bias=nm[:, n:n + 1], scale=D16 ** -0.5, accum_out=den[:, n:n + 1])
                    r.then_inc(probs_ready, 1)

                def keep_turned(i, s):
                    act.wait_ge(turned, nth(i, s))
                    act.copy(pT[:, 2:4, :, :].rearrange("p a b c -> p (a b c)"),
                             wide[:, 2:4, :].rearrange("p a b -> p (a b)")).then_inc(pT_act, 1)

                def body(i, more):
                    for c in range(NCH):
                        copy(i, f"xT{c}", xT[:, c, :], ring.bank(f"xT{c}")[:, :])
                    squares(i, 0)
                    copy(i, "v0", v[:, 0, :], ring.bank("v0")[:, 0:C])
                    hidden(i, 0)
                    copy(i, "tq0", qkT[:, 0, :, :].rearrange("p a b -> p (a b)"), ring.bank("tq0")[:, :])
                    for s in range(SUBS):
                        e = 2 * s + 1
                        hidden(i, e)
                        exponentials(i, s)
                        keep_turned(i, s)
                        if s + 1 < SUBS:
                            squares(i, s + 1)
                            copy(i, f"v{s + 1}", v[:, (s + 1) % 2, :], ring.bank(f"v{s + 1}")[:, 0:C])
                            hidden(i, e + 1)
                            tag = f"tq{s + 1}"
                            copy(i, tag, qkT[:, 0, :, :].rearrange("p a b -> p (a b)"), ring.bank(tag)[:, :])
                        tag = f"yT{s}"
                        copy(i, tag, yT[:, :, :].rearrange("p a b -> p (a b)"), ring.bank(tag)[:, 0:C])

                act.wait_ge(w_loaded, 16 * len(weights))
                blocks_loop(act, body)

            @block.vector
            def _(dve):
                def front_stats(i):
                    dve.wait_ge(x_loaded, 16 * (i + 1))
                    row_stats(dve, xin, st, mv).then_inc(stats_ready, 1)

                def front_norm(i):
                    dve.wait_ge(rs_ready, i + 1)
                    normalise(dve, xn, xin, mv, rs).then_inc(xn_ready, 1)

                def combination(i):
                    dve.wait_ge(*ring.data("gate", i))
                    dve.tensor_tensor(score[:, :, :], ring.bank("gate")[:, 0:SUBS * NE].rearrange("p (s e) -> p s e", s=SUBS),
                                      gb[:, :].unsqueeze(1).broadcast_to([P, SUBS, NE]), ALU.add)\
                       .then_inc(ring.free("gate"), 1)
                    dve.drain()
                    for s in range(SUBS):
                        dve.max(top[:, s, :], score[:, s, :])
                    dve.drain()
                    for s in range(SUBS):
                        dve.max_index(topi[:, s, :], top[:, s, :], score[:, s, :])
                    dve.drain()
                    dve.tensor_copy(topf[:, :, :], topi[:, :, :])
                    dve.drain()
                    for s in range(SUBS):
                        for t in range(2):
                            dve.tensor_scalar(pick[:, t, s, :], iota[:, :], topf[:, s, t:t + 1], top[:, s, t:t + 1],
                                              ALU.is_equal, ALU.mult)
                    dve.drain()
                    dve.tensor_tensor(comb[:, :, :], pick[:, 0, :, :], pick[:, 1, :, :], ALU.add).then_inc(comb_ready, 1)

                def norm_qk(i, s):
                    tag = f"qk{s}"
                    dve.wait_ge(rr_ready, nth(i, s))
                    dve.wait_ge(*ring.data(tag, i))
                    for t in range(2):
                        r = dve.scalar_tensor_tensor(
                            out=qk[:, t, :, 0:D16],
                            in0=ring.bank(tag)[:, t * C:(t + 1) * C].rearrange("p (h d) -> p h d", h=H16),
                            scalar=rr[:, t:t + 1], in1=lnw[:, :].rearrange("p (h d) -> p h d", h=H16),
                            op0=ALU.mult, op1=ALU.mult)
                    r.then_inc(ring.free(tag), 1)

                def copy(i, tag, dst, src):
                    dve.wait_ge(*ring.data(tag, i))
                    dve.tensor_copy(dst, src).then_inc(ring.free(tag), 1)

                def add_expert(i, e):
                    dve.drain()
                    if e == 0:
                        dve.wait_ge(res_loaded, 16 * (i + 1))
                        dve.wait_ge(stored, (i + 1) * 32)
                    for s in range(SUBS):
                        tag = f"eo{e}_{s // 2}"
                        if s % 2 == 0:
                            dve.wait_ge(*ring.data(tag, i))
                        r = dve.scalar_tensor_tensor(
                            out=acc[:, s, :], in0=ring.bank(tag)[:, (s % 2) * C:(s % 2 + 1) * C],
                            scalar=comb[:, s, e:e + 1], in1=(acc if e else xres)[:, s, :], op0=ALU.mult, op1=ALU.add)
                        if s % 2 == 1:
                            r.then_inc(ring.free(tag), 1)
                    if e == 0:
                        dve.drain().then_inc(res_used, 1)

                def maxima(i, s):
                    dve.wait_ge(scores_done, nth(i, s))
                    dve.tensor_reduce(mx[:, :], wide[:, :, :].rearrange("p j (g k) -> p (j g) k", g=4), AX, ALU.max)
                    dve.drain()
                    dve.tensor_scalar(nm[:, :], mx[:, :], -(D16 ** -0.5), None, ALU.mult).then_inc(max_ready, 1)

                def keep_turned(i, s):
                    dve.wait_ge(turned, nth(i, s))
                    dve.tensor_copy(pT[:, 0:2, :, :].rearrange("p a b c -> p (a b c)"),
                                    wide[:, 0:2, :].rearrange("p a b -> p (a b)")).then_inc(pT_dve, 1)
                    dve.reciprocal(rden[:, :], den[:, :])
                    dve.drain()

                def outputs(i, s):
                    tag = f"pv{s}"
                    dve.wait_ge(*ring.data(tag, i))
                    dve.tensor_tensor(
                        y[:, :].rearrange("p (g j e) -> p j g e", g=4, j=4),
                        ring.bank(tag)[:, 0:C].rearrange("p (g j e) -> p j g e", g=4, j=4),
                        rden[:, :].rearrange("p (j g) -> p j g", j=4).unsqueeze(3).broadcast_to([P, 4, 4, D16]),
                        ALU.mult).then_inc(ring.free(tag), 1)
                    dve.drain().then_inc(y_ready, 1)

                def body(i, more):
                    combination(i)
                    norm_qk(i, 0)
                    copy(i, "cT", combT[:, :], ring.bank("cT")[0:NE, :])
                    copy(i, "tk0", qkT[:, 1, :, :].rearrange("p a b -> p (a b)"), ring.bank("tk0")[:, :])
                    add_expert(i, 0)
                    for s in range(SUBS):
                        e = 2 * s + 1
                        maxima(i, s)
                        add_expert(i, e)
                        keep_turned(i, s)
                        if s + 1 < SUBS:
                            norm_qk(i, s + 1)
                        if more and s == 1:
                            front_stats(i + 1)
                        outputs(i, s)
                        if s + 1 < SUBS:
                            tag = f"tk{s + 1}"
                            copy(i, tag, qkT[:, 1, :, :].rearrange("p a b -> p (a b)"), ring.bank(tag)[:, :])
                            add_expert(i, e + 1)
                        if more and s == 2:
                            front_norm(i + 1)
                        tag = f"proj{s}"
                        dve.drain()
                        dve.wait_ge(*ring.data(tag, i))
                        dve.tensor_tensor(acc[:, s, :], ring.bank(tag)[:, 0:C], acc[:, s, :], ALU.add)\
                           .then_inc(ring.free(tag), 1)
                    dve.drain().then_inc(acc_ready, 1)
                    row_stats(dve, acc, st2, mv2).then_inc(stats2_ready, 1)
                    dve.wait_ge(rs2_ready, i + 1)
                    normalise(dve, xn1, acc, mv2, rs2).then_inc(xn1_ready, 1)

                dve.memset(qk[:, :, :, :], 0.0).then_inc(setup_done, 1)
                dve.wait_ge(w_loaded, 16 * len(weights))
                dve.tensor_copy(mask[:, :, :], maskf[:, :].unsqueeze(1).broadcast_to([P, 4, P])).then_inc(setup_done, 1)
                dve.drain()
                front_stats(0)
                front_norm(0)
                blocks_loop(dve, body)


def shifted_loads(sp, dst, src, i, loaded):
    sp.dma_start(dst[:, :, 0:P], token_rows(src, i, 1, 0, P)).then_inc(loaded, 16)
    sp.dma_start(dst[:, :, P:C], token_rows(src, i, 0, P, C)).then_inc(loaded, 16)


def local_attention(nc, buffers, sem, banks, wide, shared, t_in, scratch, w, src, dst, prefetch):
    ctx = ExitStack()
    with ctx:
        sb = buffers(ctx, "d_")
        ident, identb, neghalf = shared["ident"], shared["identb"], shared["neghalf"]
        maskf = sb("maskf", [P, 2, 2 * P])
        mask = sb("mask", [P, 2, 2, 2 * P], BF16)
        xin = sb("xin", [P, SUBS, C])
        xT = sb("xT", [P, NCH, BT])
        xres = sb("xres", [P, SUBS, C])
        xout = sb("xout", [P, SUBS, C])
        rotary = sb("rotary", [P, SUBS, 4, D64 // 2])
        turn = sb("turn", [P, SUBS, 4, D64])
        junk = sb("junk", [P, 2, INNER])
        ss = sb("ss", [P, 2, H8])
        rr = sb("rr", [P, 2, 2, H8])
        rot = sb("rot", [P, 2, 2, INNER])
        qk = sb("qk", [P, 2, INNER])
        qT = sb("qT", [P, H8 // 2, P])
        kT = sb("kT", [P, H8 // 2, SUBS + 1, P])
        v = sb("v", [P, SUBS + 1, INNER])
        mx = sb("mx", [P, H8])
        scale = sb("scale", [P, H8])
        nm = sb("nm", [P, H8])
        probs = sb("probs", [P, 4, 2, 2 * P])
        den = sb("den", [P, H8])
        rden = sb("rden", [P, H8])
        pT = sb("pT", [P, 4, 4, P])
        o = sb("o", [P, INNER])
        oT = sb("oT", [P, INNER // P, P])

        order = ["xT0", "xT1"]
        for s in range(SUBS):
            order += [f"{t}{s}" for t in ("q", "k", "v", "tq", "tk")]
        ring = Ring(banks[0:3], sem, order)
        order = []
        for s in range(SUBS):
            order += [f"pv{s}", f"oT{s}", f"wo{s}"]
        out_ring = Ring(banks[3:4], lambda name: sem("out_" + name), order)

        def ahead(i, s, n, last):
            return (i, s + n) if s + n < SUBS else None if last else (i + 1, s + n - SUBS)

        def staggered(eng, body):
            body(0, True, False)
            with eng.Fori(1, NB - 1) as i:
                body(i, False, False)
            body(NB - 1, False, True)

        def place(h):
            pair, odd = h // 2, h % 2
            return 2 * odd + pair // 2, pair % 2

        setup_loaded, setup_done = sem("setup_loaded"), sem("setup_done")
        x_loaded, x_used, res_loaded, rotary_loaded = (
            sem("x_loaded"), sem("x_used"), sem("res_loaded"), sem("rotary_loaded"))
        turn_ready, mask_ready, before_ready = sem("turn_ready"), sem("mask_ready"), sem("before_ready")
        squared, ss_ready, rr_ready = sem("squared"), sem("ss_ready"), sem("rr_ready")
        parts_ready, qk_ready = sem("parts_ready"), sem("qk_ready")
        scores_done, max_ready, probs_ready = sem("scores_done"), sem("max_ready"), sem("probs_ready")
        turned, pT_act, pT_dve = sem("turned"), sem("pT_act"), sem("pT_dve")
        o_ready, xout_ready, stored = sem("o_ready"), sem("xout_ready"), sem("stored")

        with nc.Block() as block:

            @block.sync
            def _(sp):
                def load(i):
                    shifted_loads(sp, xin, scratch[src], i, x_loaded)

                def load_rotary(i):
                    sp.dma_start(rotary[:, :, :, :],
                                 t_in["k_rotary"][bass.ds(i * BT, BT), :, :].rearrange("(s p) a d -> p s (a d)", p=P))\
                      .then_inc(rotary_loaded, 16)

                def load_res(i):
                    sp.dma_start(xres[:, :, :], token_rows(scratch[src], i, 1)).then_inc(res_loaded, 16)

                ring.open(sp)
                out_ring.open(sp)
                sp.sem_inc(stored, 16)
                load(0)
                load_rotary(0)
                load_res(0)
                sp.dma_start(maskf[:, :, :], t_in["k_mask_local"]).then_inc(setup_loaded, 16)
                for group in prefetch:
                    for d, a in group["loads"]:
                        sp.dma_start(whole(d), a).then_inc(group["loaded"], 16)

                def body(i, more):
                    if more:
                        sp.wait_ge(*ring.data("xT1", i))
                        load(i + 1)
                        sp.wait_ge(turn_ready, i + 1)
                        load_rotary(i + 1)
                    sp.wait_ge(xout_ready, i + 1)
                    if more:
                        load_res(i + 1)
                    sp.dma_start(token_rows(scratch[dst], i, 1), xout[:, :, :]).then_inc(stored, 16)

                blocks_loop(sp, body)
                sp.wait_ge(stored, 16 * (NB + 1))

            @block.gpsimd
            def _(pool):
                def tables(i):
                    for t, name in enumerate(("q_scale", "k_scale")):
                        for a, (table, scales) in enumerate(((2 * t, w[name]), (2 * t + 1, w[name + "_turned"]))):
                            r = pool.tensor_tensor(
                                turn[:, :, 2 * t + a, :].rearrange("p s (a d) -> p s a d", a=2),
                                rotary[:, :, table, :].unsqueeze(2).broadcast_to([P, SUBS, 2, D64 // 2]),
                                scales[:, :].rearrange("p (a d) -> p a d", a=2).unsqueeze(1)
                                            .broadcast_to([P, SUBS, 2, D64 // 2]), ALU.mult)
                    return r

                def roots(i, s):
                    pool.wait_ge(ss_ready, nth(i, s))
                    pool.tensor_tensor(rr[:, s % 2, :, :].rearrange("p a b -> p (a b)"), ss[:, :, :].rearrange("p a b -> p (a b)"),
                                       neghalf[:, :], ALU.pow).then_inc(rr_ready, 1)

                def rotate(i, s):
                    pool.wait_ge(parts_ready, nth(i, s))
                    pool.tensor_tensor(qk[:, :, :], rot[:, :, 0, :], rot[:, :, 1, :], ALU.add)
                    pool.drain()
                    pool.tensor_tensor(qk[:, 1, :].rearrange("p (h d) -> p h d", h=H8),
                                       qk[:, 1, :].rearrange("p (h d) -> p h d", h=H8),
                                       rr[:, s % 2, 1, :].unsqueeze(2).broadcast_to([P, H8, D64]), ALU.mult).then_inc(qk_ready, 1)

                def body(i, more):
                    for s in range(SUBS):
                        if s == 0:
                            pool.wait_ge(rotary_loaded, 16 * (i + 1))
                            tables(i).then_inc(turn_ready, 1)
                        roots(i, s)
                        rotate(i, s)

                pool.memset(kT[:, :, 0, :], 0.0)
                pool.memset(v[:, 0, :], 0.0).then_inc(before_ready, 1)
                pool.wait_ge(w["loaded"], 16 * len(w["loads"]))
                for name in ("q_scale_turned", "k_scale_turned"):
                    r = pool.tensor_scalar(w[name][:, 0:D64 // 2], w[name][:, 0:D64 // 2], -1.0, None, ALU.mult)
                pool.drain()
                blocks_loop(pool, body)

            @block.tensor
            def _(pe):
                def channels(i, s, n):
                    tag = f"{'qkv'[n]}{s}"
                    pe.wait_ge(*ring.space(tag, i))
                    for c in range(NCH):
                        mm = pe.matmul(ring.bank(tag)[:, :], xT[:, c, s * P:(s + 1) * P],
                                       w["wqkv"][:, c, n * INNER:(n + 1) * INNER], start=c == 0, stop=c == NCH - 1)
                    mm.then_inc(ring.full(tag), 1)

                def turn_x(i):
                    pe.wait_ge(x_loaded, 32 * (i + 1))
                    turn_block(pe, ring, ("xT0", "xT1"), i, xin, ident)

                def turn_qk(i, s):
                    pe.wait_ge(qk_ready, nth(i, s))
                    for t, tag in enumerate((f"tq{s}", f"tk{s}")):
                        pe.wait_ge(*ring.space(tag, i))
                        for g in range(INNER // P):
                            mm = pe.transpose(ring.bank(tag)[:, g * P:(g + 1) * P], qk[:, t, g * P:(g + 1) * P], ident[:, :])
                        mm.then_inc(ring.full(tag), 1)

                def scores(i, s):
                    pe.wait_ge(*ring.copied(f"tq{s}", i))
                    pe.wait_ge(*ring.copied(f"tk{s}", i))
                    if s == 0:
                        pe.wait_ge(mask_ready, i + 1)
                    for b in range(4):
                        pe.matmul(wide[:, b, :], identb[:, :], mask[:, int(s == 0), :, :].rearrange("p a b -> p (a b)"),
                                  start=True, stop=False)
                    for pair in (0, 2, 1, 3):
                        for odd in range(2):
                            h = 2 * pair + odd
                            b, half = place(h)
                            r = slice(D64 * odd, D64 * (odd + 1))
                            mm = pe.matmul(wide[:, b, half * 2 * P:(half + 1) * 2 * P], qT[r, pair, :],
                                           kT[r, pair, s:s + 2, :].rearrange("p a b -> p (a b)"),
                                           start=False, stop=half == 1)
                    mm.then_inc(scores_done, 1)

                def turn_probs(i, s):
                    pe.wait_ge(probs_ready, nth(i, s))
                    for b in range(4):
                        for g in range(4):
                            mm = pe.transpose(wide[:, b, g * P:(g + 1) * P],
                                              probs[:, b, g // 2, (g % 2) * P:(g % 2 + 1) * P], ident[:, :])
                    mm.then_inc(turned, 1)

                def values(i, s):
                    tag = f"pv{s}"
                    pe.wait_ge(pT_act, nth(i, s))
                    pe.wait_ge(pT_dve, nth(i, s))
                    pe.wait_ge(*ring.copied(f"v{s}", i))
                    pe.wait_ge(*out_ring.space(tag, i))
                    for h in range(H8):
                        b, half = place(h)
                        cols = slice(h * D64, (h + 1) * D64)
                        for k in range(2):
                            mm = pe.matmul(out_ring.bank(tag)[:, cols], pT[:, b, 2 * half + k, :], v[:, s + k, cols],
                                           start=k == 0, stop=k == 1)
                    mm.then_inc(out_ring.full(tag), 1)

                def turn_o(i, s):
                    tag = f"oT{s}"
                    pe.wait_ge(o_ready, nth(i, s))
                    pe.wait_ge(*out_ring.space(tag, i))
                    for g in range(INNER // P):
                        mm = pe.transpose(out_ring.bank(tag)[:, g * P:(g + 1) * P], o[:, g * P:(g + 1) * P], ident[:, :])
                    mm.then_inc(out_ring.full(tag), 1)

                def project(i, s):
                    tag = f"wo{s}"
                    pe.wait_ge(*out_ring.space(tag, i))
                    for g in range(INNER // P):
                        mm = pe.matmul(out_ring.bank(tag)[:, 0:C], oT[:, g, :], w["wo"][:, g, :],
                                       start=g == 0, stop=g == INNER // P - 1)
                    mm.then_inc(out_ring.full(tag), 1)

                def body(i, first, last):
                    for s in range(SUBS):
                        one, two = ahead(i, s, 1, last), ahead(i, s, 2, last)
                        before = (i, s - 1) if s else None if first else (i - 1, SUBS - 1)
                        scores(i, s)
                        if one:
                            turn_qk(*one)
                        if two and s == 2:
                            turn_x(i + 1)
                        if before:
                            turn_o(*before)
                        if two and s != 2:
                            channels(*two, 0)
                        if before:
                            project(*before)
                        if two and s == 2:
                            for tag in ("xT0", "xT1"):
                                pe.wait_ge(*ring.copied(tag, i + 1))
                            channels(*two, 0)
                        if two:
                            channels(*two, 1)
                        turn_probs(i, s)
                        if two:
                            channels(*two, 2)
                        values(i, s)

                pe.wait_ge(w["loaded"], 16 * len(w["loads"]))
                pe.wait_ge(before_ready, 1)
                turn_x(0)
                for tag in ("xT0", "xT1"):
                    pe.wait_ge(*ring.copied(tag, 0))
                for n in range(3):
                    channels(0, 0, n)
                turn_qk(0, 0)
                for n in range(3):
                    channels(0, 1, n)
                staggered(pe, body)
                turn_o(NB - 1, SUBS - 1)
                project(NB - 1, SUBS - 1)

            @block.scalar
            def _(act):
                def copy(i, tag, dst, src, ring=ring):
                    act.wait_ge(*ring.data(tag, i))
                    act.copy(dst, src).then_inc(ring.free(tag), 1)

                def copy_x(i):
                    for c in range(NCH):
                        copy(i, f"xT{c}", xT[:, c, :], ring.bank(f"xT{c}")[:, :])

                def copy_q(i, s):
                    copy(i, f"tq{s}", qT[:, :, :].rearrange("p a b -> p (a b)"), ring.bank(f"tq{s}")[:, :])

                def copy_v(i, s):
                    copy(i, f"v{s}", v[:, s + 1, :], ring.bank(f"v{s}")[:, :])

                def copy_o(i, s):
                    tag = f"oT{s}"
                    copy(i, tag, oT[:, :, :].rearrange("p a b -> p (a b)"), out_ring.bank(tag)[:, :], out_ring)

                def squares(i, s):
                    for t in range(2):
                        tag = f"{'qk'[t]}{s}"
                        act.wait_ge(*ring.data(tag, i))
                        r = act.activation(junk[:, t, :], ring.bank(tag)[:, :], ACT.Square)
                    r.then_inc(squared, 1)

                def exponentials(i, s):
                    act.wait_ge(max_ready, nth(i, s))
                    for h in range(H8):
                        b, half = place(h)
                        r = act.activation(probs[:, b, half, :], wide[:, b, half * 2 * P:(half + 1) * 2 * P], ACT.Exp,
                                           bias=nm[:, h:h + 1], scale=scale[:, h:h + 1], accum_out=den[:, h:h + 1])
                    r.then_inc(probs_ready, 1)

                def keep_turned(i, s):
                    act.wait_ge(turned, nth(i, s))
                    act.copy(pT[:, 2:4, :, :].rearrange("p a b c -> p (a b c)"),
                             wide[:, 2:4, :].rearrange("p a b -> p (a b)")).then_inc(pT_act, 1)

                def body(i, first, last):
                    for s in range(SUBS):
                        one, two = ahead(i, s, 1, last), ahead(i, s, 2, last)
                        before = (i, s - 1) if s else None if first else (i - 1, SUBS - 1)
                        if one:
                            copy_q(*one)
                        if two and s == 2:
                            copy_x(i + 1)
                        if before:
                            copy_o(*before)
                        exponentials(i, s)
                        keep_turned(i, s)
                        if two:
                            squares(*two)
                            copy_v(*two)
                        if s == SUBS - 1 and not last:
                            act.copy(v[:, 0, :], v[:, SUBS, :])

                act.wait_ge(before_ready, 1)
                copy_x(0)
                squares(0, 0)
                copy_v(0, 0)
                copy_q(0, 0)
                squares(0, 1)
                copy_v(0, 1)
                staggered(act, body)
                copy_o(NB - 1, SUBS - 1)

            @block.vector
            def _(dve):
                def copy(i, tag, dst, src):
                    dve.wait_ge(*ring.data(tag, i))
                    dve.tensor_copy(dst, src).then_inc(ring.free(tag), 1)

                def rotate(i, s):
                    dve.wait_ge(squared, nth(i, s))
                    dve.tensor_reduce(ss[:, :, :], junk[:, :, :].rearrange("p t (h d) -> p t h d", h=H8), AX, ALU.add)
                    dve.drain()
                    dve.tensor_scalar(ss[:, :, :], ss[:, :, :], NORM_FLOOR, None, ALU.max).then_inc(ss_ready, 1)
                    if s == 0:
                        dve.wait_ge(turn_ready, i + 1)
                    half = D64 // 2
                    for t in range(2):
                        tag = f"{'qk'[t]}{s}"
                        dve.wait_ge(*ring.data(tag, i))
                        x = ring.bank(tag)[:, :].rearrange("p (h d) -> p h d", h=H8)
                        cos = rot[:, t, 0, :].rearrange("p (h d) -> p h d", h=H8)
                        sin = rot[:, t, 1, :].rearrange("p (h d) -> p h d", h=H8)
                        dve.tensor_tensor(cos, x, turn[:, s, 2 * t, :].unsqueeze(1).broadcast_to([P, H8, D64]), ALU.mult)
                        for a in range(2):
                            here, there = slice(a * half, (a + 1) * half), slice((1 - a) * half, (2 - a) * half)
                            r = dve.tensor_tensor(
                                sin[:, :, here], x[:, :, there],
                                turn[:, s, 2 * t + 1, here].unsqueeze(1).broadcast_to([P, H8, half]), ALU.mult)
                        r.then_inc(ring.free(tag), 1)
                    dve.drain().then_inc(parts_ready, 1)

                def maxima(i, s):
                    dve.wait_ge(scores_done, nth(i, s))
                    dve.tensor_reduce(mx[:, :].rearrange("p (pair odd) -> p odd pair", odd=2),
                                      wide[:, :, :].rearrange("p (o b) (a k) -> p o (b a) k", o=2, a=2), AX, ALU.max)
                    dve.tensor_scalar(scale[:, :], rr[:, s % 2, 0, :], QK_SCALE, None, ALU.mult)
                    dve.drain()
                    dve.scalar_tensor_tensor(out=nm[:, :], in0=mx[:, :], scalar=-1.0, in1=scale[:, :],
                                             op0=ALU.mult, op1=ALU.mult).then_inc(max_ready, 1)

                def keep_turned(i, s):
                    dve.wait_ge(turned, nth(i, s))
                    dve.tensor_copy(pT[:, 0:2, :, :].rearrange("p a b c -> p (a b c)"),
                                    wide[:, 0:2, :].rearrange("p a b -> p (a b)")).then_inc(pT_dve, 1)
                    dve.reciprocal(rden[:, :], den[:, :])
                    dve.drain()

                def outputs(i, s):
                    tag = f"pv{s}"
                    dve.wait_ge(*out_ring.data(tag, i))
                    dve.tensor_tensor(o[:, :].rearrange("p (h d) -> p h d", h=H8),
                                      out_ring.bank(tag)[:, :].rearrange("p (h d) -> p h d", h=H8),
                                      rden[:, :].unsqueeze(2).broadcast_to([P, H8, D64]), ALU.mult)\
                       .then_inc(out_ring.free(tag), 1)
                    dve.drain().then_inc(o_ready, 1)

                def keys(i, s):
                    tag = f"tk{s}"
                    copy(i, tag, kT[:, :, s + 1, :], ring.bank(tag)[:, :].rearrange("p (a b) -> p a b", a=H8 // 2))

                def add(i, s):
                    if s == 0:
                        dve.wait_ge(res_loaded, 16 * (i + 1))
                        dve.wait_ge(stored, 16 * (i + 1))
                    tag = f"wo{s}"
                    dve.wait_ge(*out_ring.data(tag, i))
                    dve.tensor_tensor(xout[:, s, :], out_ring.bank(tag)[:, 0:C], xres[:, s, :], ALU.add)\
                       .then_inc(out_ring.free(tag), 1)
                    if s == SUBS - 1:
                        dve.drain().then_inc(xout_ready, 1)

                def body(i, first, last):
                    for s in range(SUBS):
                        one, two = ahead(i, s, 1, last), ahead(i, s, 2, last)
                        before = (i, s - 1) if s else None if first else (i - 1, SUBS - 1)
                        maxima(i, s)
                        if s == 0:
                            dve.tensor_copy(mask[:, 1, :, :], mask[:, 0, :, :]).then_inc(mask_ready, 1)
                        if s == SUBS - 1 and not last:
                            dve.tensor_copy(kT[:, :, 0, :], kT[:, :, SUBS, :])
                        if one:
                            keys(*one)
                        if before:
                            add(*before)
                        keep_turned(i, s)
                        if two:
                            rotate(*two)
                        outputs(i, s)

                dve.wait_ge(setup_loaded, 16)
                dve.wait_ge(before_ready, 1)
                for n in range(2):
                    r = dve.tensor_copy(mask[:, n, :, :], maskf[:, n, :].unsqueeze(1).broadcast_to([P, 2, 2 * P]))
                r.then_inc(mask_ready, 1)
                rotate(0, 0)
                keys(0, 0)
                rotate(0, 1)
                staggered(dve, body)
                add(NB - 1, SUBS - 1)


def local_ffn(nc, buffers, sem, banks, wide, shared, t_in, scratch, w, src, dst):
    ctx = ExitStack()
    with ctx:
        sb = buffers(ctx, "f_")
        ident, neghalf = shared["ident"], shared["neghalf"]
        xin = sb("xin", [P, SUBS, C])
        st = sb("st", [P, SUBS, 6])
        mv = sb("mv", [P, SUBS, 2])
        rs = sb("rs", [P, SUBS])
        xn = sb("xn", [P, SUBS, C])
        xT = sb("xT", [P, NCH, BT])
        xres = sb("xres", [P, SUBS, C])
        xb = sb("xb", [P, SUBS, C])
        xout = sb("xout", [P, SUBS, C])
        gate = sb("gate", [P, 2, BT])
        u = sb("u", [P, HCH, BT])

        order = ["xT0", "xT1"]
        for m in range(HCH):
            order += [f"g{m}", f"a{m}"]
        order += [f"y{s}" for s in range(SUBS)]
        ring = Ring(banks, sem, order)
        rows = [min(P, HID - m * P) for m in range(HCH)]

        x_loaded, res_loaded, stored = sem("x_loaded"), sem("res_loaded"), sem("stored")
        stats_ready, rs_ready, xn_ready = sem("stats_ready"), sem("rs_ready"), sem("xn_ready")
        xb_ready, gate_ready, xout_ready = sem("xb_ready"), sem("gate_ready"), sem("xout_ready")

        with nc.Block() as block:

            @block.sync
            def _(sp):
                def load(i):
                    shifted_loads(sp, xin, scratch[src], i, x_loaded)

                def load_res(i):
                    sp.dma_start(xres[:, :, :], token_rows(scratch[src], i, 1)).then_inc(res_loaded, 16)

                ring.open(sp)
                sp.sem_inc(stored, 16)
                load(0)
                load_res(0)

                def body(i, more):
                    if more:
                        sp.wait_ge(xn_ready, i + 1)
                        load(i + 1)
                        sp.wait_ge(xb_ready, i + 1)
                        load_res(i + 1)
                    sp.wait_ge(xout_ready, i + 1)
                    rows_out = token_rows(scratch[dst], i, int(dst in PADDED))
                    sp.dma_start(rows_out, xout[:, :, :]).then_inc(stored, 16)

                blocks_loop(sp, body)
                sp.wait_ge(stored, 16 * (NB + 1))

            @block.gpsimd
            def _(pool):
                def front(i):
                    pool.wait_ge(stats_ready, i + 1)
                    inverse_root(pool, rs[:, :], mv[:, :, 1], shared["eps_ln"][:, :], neghalf[:, 0:SUBS]).then_inc(rs_ready, 1)

                def body(i, more):
                    pool.wait_ge(res_loaded, 16 * (i + 1))
                    pool.tensor_tensor(xb[:, :, :], xres[:, :, :], w["b2"][:, :].unsqueeze(1).broadcast_to([P, SUBS, C]),
                                       ALU.add).then_inc(xb_ready, 1)
                    if more:
                        front(i + 1)
                        pool.wait_ge(xout_ready, i + 1)

                front(0)
                pool.wait_ge(w["loaded"], 16 * len(w["loads"]))
                blocks_loop(pool, body)

            @block.tensor
            def _(pe):
                def body(i, more):
                    pe.wait_ge(xn_ready, i + 1)
                    turn_block(pe, ring, ("xT0", "xT1"), i, xn, ident)
                    for tag in ("xT0", "xT1"):
                        pe.wait_ge(*ring.copied(tag, i))
                    for m, r in enumerate(rows):
                        for tag, first in ((f"g{m}", HID + m * P), (f"a{m}", m * P)):
                            pe.wait_ge(*ring.space(tag, i))
                            for c in range(NCH):
                                mm = pe.matmul(ring.bank(tag)[0:r, :], w["w1"][:, c, first:first + r], xT[:, c, :],
                                               start=c == 0, stop=c == NCH - 1)
                            mm.then_inc(ring.full(tag), 1)
                    for s in range(SUBS):
                        pe.wait_ge(*ring.space(f"y{s}", i))
                        for m, r in enumerate(rows):
                            if s == 0:
                                pe.wait_ge(*ring.copied(f"a{m}", i))
                            mm = pe.matmul(ring.bank(f"y{s}")[:, 0:C], u[0:r, m, s * P:(s + 1) * P], w["w2"][0:r, m, :],
                                           start=m == 0, stop=m == HCH - 1)
                        mm.then_inc(ring.full(f"y{s}"), 1)

                pe.wait_ge(w["loaded"], 16 * len(w["loads"]))
                blocks_loop(pe, body)

            @block.scalar
            def _(act):
                def body(i, more):
                    for c in range(NCH):
                        tag = f"xT{c}"
                        act.wait_ge(*ring.data(tag, i))
                        act.activation(xT[:, c, :], ring.bank(tag)[:, :], ACT.Identity, bias=w["lb"][:, c:c + 1],
                                       scale=w["lg"][:, c:c + 1]).then_inc(ring.free(tag), 1)
                    for m, r in enumerate(rows):
                        tag = f"g{m}"
                        if m >= 2:
                            act.wait_ge(*ring.copied(f"a{m - 2}", i))
                        act.wait_ge(*ring.data(tag, i))
                        act.activation(gate[0:r, m % 2, :], ring.bank(tag)[0:r, :], ACT.Gelu,
                                       bias=w["b1"][0:r, 1, m:m + 1]).then_inc(ring.free(tag), 1)

                act.wait_ge(w["loaded"], 16 * len(w["loads"]))
                blocks_loop(act, body)

            @block.vector
            def _(dve):
                def front_stats(i):
                    dve.wait_ge(x_loaded, 32 * (i + 1))
                    row_stats(dve, xin, st, mv).then_inc(stats_ready, 1)

                def front_norm(i):
                    dve.wait_ge(rs_ready, i + 1)
                    normalise(dve, xn, xin, mv, rs).then_inc(xn_ready, 1)

                def body(i, more):
                    for m, r in enumerate(rows):
                        dve.wait_ge(*ring.copied(f"g{m}", i))
                        dve.wait_ge(*ring.data(f"a{m}", i))
                        dve.scalar_tensor_tensor(out=u[0:r, m, :], in0=ring.bank(f"a{m}")[0:r, :],
                                                 scalar=w["b1"][0:r, 0, m:m + 1], in1=gate[0:r, m % 2, :],
                                                 op0=ALU.add, op1=ALU.mult).then_inc(ring.free(f"a{m}"), 1)
                        if more and m == 1:
                            front_stats(i + 1)
                        if more and m == 3:
                            front_norm(i + 1)
                    dve.wait_ge(xb_ready, i + 1)
                    dve.wait_ge(stored, 16 * (i + 1))
                    for s in range(SUBS):
                        dve.wait_ge(*ring.data(f"y{s}", i))
                        dve.tensor_tensor(xout[:, s, :], ring.bank(f"y{s}")[:, 0:C], xb[:, s, :], ALU.add)\
                           .then_inc(ring.free(f"y{s}"), 1)
                    dve.drain().then_inc(xout_ready, 1)

                dve.wait_ge(w["loaded"], 16 * len(w["loads"]))
                front_stats(0)
                front_norm(0)
                blocks_loop(dve, body)


def linear_stage(nc, buffers, sem, banks, wide, shared, t_in, scratch, w, out):
    ctx = ExitStack()
    with ctx:
        sb = buffers(ctx, "l_")
        ident, neghalf, eps = shared["ident"], shared["neghalf"], shared["eps_ln"]
        xin = sb("xin", [P, SUBS, C])
        st = sb("st", [P, SUBS, 6])
        mv = sb("mv", [P, SUBS, 2])
        rs = sb("rs", [P, SUBS])
        xn = sb("xn", [P, SUBS, C])
        xT = sb("xT", [P, NCH, BT])
        xb = sb("xb", [P, SUBS, C])
        x1 = sb("x1", [P, SUBS, C])
        xl = sb("xl", [P, SUBS, C])
        base = sb("base", [P, SUBS, C])
        z = sb("z", [P, 2 * C])
        neg = sb("neg", [P, 2 * C])
        pos = sb("pos", [P, 2 * C])
        ez = sb("ez", [P, 2 * C])
        f = sb("f", [P, 2, C])
        v = sb("v", [P, C])
        prod = sb("prod", [P, C, D16])
        kv = sb("kv", [P, D16, D16])
        ksum = sb("ksum", [P, D16])
        num = sb("num", [P, C])
        dprod = sb("dprod", [P, H16, D16])
        den = sb("den", [P, H16])
        y = sb("y", [P, 2, C])
        yT = sb("yT", [P, NCH, P])
        x2 = sb("x2", [P, SUBS, C])
        st2 = sb("st2", [P, 6])
        mv2 = sb("mv2", [P, 2])
        rs2 = sb("rs2", [P, 1])
        xn2 = sb("xn2", [P, C])
        x2T = sb("x2T", [P, NCH, BT])
        hT = sb("hT", [P, MLP // P, BT])
        rest = sb("rest", [P, SUBS, C])
        total = sb("total", [P, SUBS, C])

        order = ["xT0", "xT1", "qk0", "v0", "qk1", "v1"]
        for s in range(SUBS):
            order += [f"yT{s}", f"wo{s}", f"x2T{s}"]
            if s + 2 < SUBS:
                order += [f"qk{s + 2}", f"v{s + 2}"]
        ring = Ring(banks, sem, order)
        mlp_order = [f"h{m}" for m in range(MLP // P)] + [f"p{s}" for s in range(SUBS)]
        mlp_ring = Ring([wide[:, b, :] for b in range(4)], lambda name: sem("mlp_" + name), mlp_order)

        x_loaded, rest_loaded, stored = sem("x_loaded"), sem("rest_loaded"), sem("stored")
        stats_ready, rs_ready, xn_ready = sem("stats_ready"), sem("rs_ready"), sem("xn_ready")
        xb_ready, base_ready, rest_ready = sem("xb_ready"), sem("base_ready"), sem("rest_ready")
        z_ready, elu_ready, y_ready = sem("z_ready"), sem("elu_ready"), sem("y_ready")
        stats2_ready, rs2_ready, xn2_ready = sem("stats2_ready"), sem("rs2_ready"), sem("xn2_ready")
        added, total_ready = sem("added"), sem("total_ready")

        def staggered(eng, body):
            body(None, 0)
            with eng.Fori(0, NB - 1) as i:
                body(i, i + 1)
            body(NB - 1, None)

        with nc.Block() as block:

            @block.sync
            def _(sp):
                def load_x(b):
                    sp.dma_start(xin[:, :, :], token_rows(scratch["xn1"], b, 1)).then_inc(x_loaded, 16)

                def load_rest(b):
                    sp.dma_start(x1[:, :, :], token_rows(scratch["x1"], b)).then_inc(rest_loaded, 16)
                    sp.dma_start(xl[:, :, :], token_rows(scratch["xl2"], b)).then_inc(rest_loaded, 16)

                ring.open(sp)
                mlp_ring.open(sp)
                sp.sem_inc(stored, 16)
                load_x(0)
                load_rest(0)

                def body(i, more):
                    if more:
                        sp.wait_ge(xn_ready, i + 1)
                        sp.wait_ge(xb_ready, i + 1)
                        load_x(i + 1)
                        sp.wait_ge(base_ready, i + 1)
                        load_rest(i + 1)
                    sp.wait_ge(total_ready, i + 1)
                    sp.dma_start(token_rows(out, i), total[:, :, :]).then_inc(stored, 16)

                blocks_loop(sp, body)
                sp.wait_ge(stored, 16 * (NB + 1))

            @block.gpsimd
            def _(pool):
                def wide_bias(name):
                    return w[name][:, :].unsqueeze(1).broadcast_to([P, SUBS, C])

                def body(i, b):
                    if b is None:
                        return
                    pool.wait_ge(stats_ready, b + 1)
                    inverse_root(pool, rs[:, :], mv[:, :, 1], eps[:, :], neghalf[:, 0:SUBS]).then_inc(rs_ready, 1)
                    if i is not None:
                        pool.wait_ge(stats2_ready, nth(i, SUBS - 1))
                    pool.tensor_tensor(xb[:, :, :], xin[:, :, :], wide_bias("bo"), ALU.add).then_inc(xb_ready, 1)
                    pool.wait_ge(rest_loaded, 32 * (b + 1))
                    pool.tensor_tensor(base[:, :, :], x1[:, :, :], xl[:, :, :], ALU.add)
                    pool.drain()
                    pool.tensor_tensor(base[:, :, :], base[:, :, :], wide_bias("projb"), ALU.add).then_inc(base_ready, 1)
                    for s in range(SUBS):
                        pool.wait_ge(stats2_ready, nth(b, s))
                        inverse_root(pool, rs2[:, :], mv2[:, 1:2], eps[:, 0:1], neghalf[:, 0:1]).then_inc(rs2_ready, 1)
                        if i is not None:
                            pool.wait_ge(added, nth(i, s))
                        pool.tensor_tensor(rest[:, s, :], base[:, s, :], x2[:, s, :], ALU.add).then_inc(rest_ready, 1)
                    pool.drain()

                pool.wait_ge(w["loaded"], 16 * len(w["loads"]))
                staggered(pool, body)

            @block.tensor
            def _(pe):
                def qkv(b, s):
                    for tag, lo, hi in ((f"qk{s}", 0, 2 * C), (f"v{s}", 2 * C, 3 * C)):
                        pe.wait_ge(*ring.space(tag, b))
                        for c in range(NCH):
                            mm = pe.matmul(ring.bank(tag)[:, 0:hi - lo], xT[:, c, s * P:(s + 1) * P],
                                           w["wqkv"][:, c, lo:hi], start=c == 0, stop=c == NCH - 1)
                        mm.then_inc(ring.full(tag), 1)

                def turn(b, tag, x):
                    pe.wait_ge(*ring.space(tag, b))
                    for c in range(NCH):
                        mm = pe.transpose(ring.bank(tag)[:, c * P:(c + 1) * P], x[:, c * P:(c + 1) * P], ident[:, :])
                    mm.then_inc(ring.full(tag), 1)

                def finish(b, s):
                    pe.wait_ge(y_ready, nth(b, s))
                    turn(b, f"yT{s}", y[:, s % 2, :])
                    pe.wait_ge(*ring.space(f"wo{s}", b))
                    pe.wait_ge(*ring.copied(f"yT{s}", b))
                    for c in range(NCH):
                        mm = pe.matmul(ring.bank(f"wo{s}")[:, 0:C], yT[:, c, :], w["wo"][:, c, :],
                                       start=c == 0, stop=c == NCH - 1)
                    mm.then_inc(ring.full(f"wo{s}"), 1)
                    pe.wait_ge(xn2_ready, nth(b, s))
                    turn(b, f"x2T{s}", xn2)

                def mlp_in(i, ms):
                    for m in ms:
                        pe.wait_ge(*mlp_ring.space(f"h{m}", i))
                        for c in range(NCH):
                            mm = pe.matmul(mlp_ring.bank(f"h{m}"), w["fc"][:, c, m * P:(m + 1) * P], x2T[:, c, :],
                                           start=c == 0, stop=c == NCH - 1)
                        mm.then_inc(mlp_ring.full(f"h{m}"), 1)

                def mlp_out(i, s):
                    pe.wait_ge(*mlp_ring.space(f"p{s}", i))
                    for m in range(MLP // P):
                        if s == 0:
                            pe.wait_ge(*mlp_ring.copied(f"h{m}", i))
                        mm = pe.matmul(mlp_ring.bank(f"p{s}")[:, 0:C], hT[:, m, s * P:(s + 1) * P], w["proj"][:, m, :],
                                       start=m == 0, stop=m == MLP // P - 1)
                    mm.then_inc(mlp_ring.full(f"p{s}"), 1)

                def body(i, b):
                    half = MLP // P // 2
                    if i is not None:
                        pe.wait_ge(*ring.copied(f"x2T{SUBS - 1}", i))
                        mlp_in(i, range(half))
                    if b is not None:
                        pe.wait_ge(xn_ready, b + 1)
                        turn_block(pe, ring, ("xT0", "xT1"), b, xn, ident)
                        for tag in ("xT0", "xT1"):
                            pe.wait_ge(*ring.copied(tag, b))
                        qkv(b, 0)
                    if i is not None:
                        mlp_in(i, range(half, 2 * half))
                    if b is not None:
                        qkv(b, 1)
                    for s in range(SUBS):
                        if i is not None:
                            mlp_out(i, s)
                        if b is not None:
                            finish(b, s)
                            if s + 2 < SUBS:
                                qkv(b, s + 2)

                pe.wait_ge(w["loaded"], 16 * len(w["loads"]))
                staggered(pe, body)

            @block.scalar
            def _(act):
                def affine(b, tag, dst, src, scale, bias):
                    for c in range(NCH):
                        r = act.activation(dst(c), src(c), ACT.Identity, bias=bias[:, c:c + 1], scale=scale[:, c:c + 1])
                    return r

                def elu(b, s):
                    act.wait_ge(z_ready, nth(b, s))
                    act.activation(neg[:, :], z[:, :], ACT.Relu, scale=-1.0)
                    act.activation(pos[:, :], z[:, :], ACT.Relu)
                    act.drain()
                    act.activation(ez[:, :], neg[:, :], ACT.Exp, scale=-1.0).then_inc(elu_ready, 1)

                def finish(b, s):
                    tag = f"yT{s}"
                    act.wait_ge(*ring.data(tag, b))
                    act.copy(yT[:, :, :].rearrange("p a b -> p (a b)"), ring.bank(tag)[:, 0:C]).then_inc(ring.free(tag), 1)
                    tag = f"x2T{s}"
                    act.wait_ge(*ring.data(tag, b))
                    for c in range(NCH):
                        r = act.activation(x2T[:, c, s * P:(s + 1) * P], ring.bank(tag)[:, c * P:(c + 1) * P],
                                           ACT.Identity, bias=w["o2"][:, c:c + 1], scale=w["g2"][:, c:c + 1])
                    r.then_inc(ring.free(tag), 1)

                def gelu(i, ms):
                    for m in ms:
                        tag = f"h{m}"
                        act.wait_ge(*mlp_ring.data(tag, i))
                        act.activation(hT[:, m, :], mlp_ring.bank(tag), ACT.Gelu, bias=w["fcb"][:, m:m + 1])\
                           .then_inc(mlp_ring.free(tag), 1)

                def body(i, b):
                    half = MLP // P // 2
                    if i is not None:
                        gelu(i, range(half))
                    if b is not None:
                        for c in range(NCH):
                            tag = f"xT{c}"
                            act.wait_ge(*ring.data(tag, b))
                            act.activation(xT[:, c, :], ring.bank(tag)[:, :], ACT.Identity, bias=w["o1"][:, c:c + 1],
                                           scale=w["g1"][:, c:c + 1]).then_inc(ring.free(tag), 1)
                        elu(b, 0)
                    if i is not None:
                        gelu(i, range(half, 2 * half))
                    if b is not None:
                        elu(b, 1)
                        for s in range(SUBS):
                            finish(b, s)
                            if s + 2 < SUBS:
                                elu(b, s + 2)

                act.wait_ge(w["loaded"], 16 * len(w["loads"]))
                staggered(act, body)

            @block.vector
            def _(dve):
                def attention(b, s):
                    dve.wait_ge(*ring.data(f"qk{s}", b))
                    dve.tensor_tensor(z[:, :], ring.bank(f"qk{s}")[:, :], w["bqkv"][:, 0:2 * C], ALU.add)\
                       .then_inc(ring.free(f"qk{s}"), 1)
                    dve.wait_ge(*ring.data(f"v{s}", b))
                    dve.tensor_tensor(v[:, :], ring.bank(f"v{s}")[:, 0:C], w["bqkv"][:, 2 * C:3 * C], ALU.add)\
                       .then_inc(ring.free(f"v{s}"), 1)
                    dve.drain().then_inc(z_ready, 1)
                    dve.wait_ge(elu_ready, nth(b, s))
                    dve.tensor_tensor(f[:, :, :].rearrange("p a b -> p (a b)"), ez[:, :], pos[:, :], ALU.add)
                    dve.drain()
                    fq = f[:, 0, :].rearrange("p (h d) -> p h d", h=H16)
                    fk = f[:, 1, :].rearrange("p (h d) -> p d h", h=H16)
                    vt = v[:, :].rearrange("p (h e) -> p e h", h=H16)
                    cube = prod[:, :, :].rearrange("p (a b) c -> p a b c", a=D16)
                    shape = [P, D16, D16, D16]
                    dve.tensor_reduce(ksum[:, :], fk, AX, ALU.add)
                    dve.tensor_tensor(cube, fk.unsqueeze(2).broadcast_to(shape), vt.unsqueeze(1).broadcast_to(shape), ALU.mult)
                    dve.drain()
                    dve.tensor_reduce(kv[:, :, :].rearrange("p a b -> p (a b)"), prod[:, :, :], AX, ALU.add)
                    dve.tensor_tensor(dprod[:, :, :], fq, ksum[:, :].unsqueeze(1).broadcast_to([P, H16, D16]), ALU.mult)
                    dve.drain()
                    dve.tensor_tensor(cube, fq.unsqueeze(2).broadcast_to(shape),
                                      kv[:, :, :].rearrange("p d e -> p e d").unsqueeze(1).broadcast_to(shape), ALU.mult)
                    dve.tensor_reduce(den[:, :], dprod[:, :, :], AX, ALU.add)
                    dve.drain()
                    dve.tensor_reduce(num[:, :], prod[:, :, :], AX, ALU.add)
                    dve.tensor_scalar(den[:, :], den[:, :], 1e-6, None, ALU.add)
                    dve.drain()
                    dve.reciprocal(den[:, :], den[:, :])
                    dve.drain()
                    dve.tensor_tensor(y[:, s % 2, :].rearrange("p (h e) -> p h e", h=H16),
                                      num[:, :].rearrange("p (h e) -> p h e", h=H16),
                                      den[:, :].unsqueeze(2).broadcast_to([P, H16, D16]), ALU.mult).then_inc(y_ready, 1)

                def finish(b, s):
                    if s == 0:
                        dve.wait_ge(xb_ready, b + 1)
                    dve.wait_ge(*ring.data(f"wo{s}", b))
                    dve.tensor_tensor(x2[:, s, :], ring.bank(f"wo{s}")[:, 0:C], xb[:, s, :], ALU.add)\
                       .then_inc(ring.free(f"wo{s}"), 1)
                    dve.drain()
                    dve.bn_stats(st2[:, :], x2[:, s, :])
                    dve.drain()
                    dve.bn_aggr(mv2[:, :], st2[:, :]).then_inc(stats2_ready, 1)
                    dve.wait_ge(rs2_ready, nth(b, s))
                    dve.tensor_scalar(xn2[:, :], x2[:, s, :], mv2[:, 0:1], rs2[:, 0:1], ALU.subtract, ALU.mult)\
                       .then_inc(xn2_ready, 1)

                def add(i, s):
                    if s == 0:
                        dve.wait_ge(stored, 16 * (i + 1))
                    dve.wait_ge(rest_ready, nth(i, s))
                    dve.wait_ge(*mlp_ring.data(f"p{s}", i))
                    dve.tensor_tensor(total[:, s, :], mlp_ring.bank(f"p{s}")[:, 0:C], rest[:, s, :], ALU.add)\
                       .then_inc(mlp_ring.free(f"p{s}"), 1)
                    dve.drain().then_inc(added, 1)

                def body(i, b):
                    if b is not None:
                        dve.wait_ge(x_loaded, 16 * (b + 1))
                        row_stats(dve, xin, st, mv).then_inc(stats_ready, 1)
                        dve.wait_ge(rs_ready, b + 1)
                        normalise(dve, xn, xin, mv, rs).then_inc(xn_ready, 1)
                        attention(b, 0)
                        attention(b, 1)
                    for s in range(SUBS):
                        if i is not None:
                            add(i, s)
                        if b is not None:
                            finish(b, s)
                            if s + 2 < SUBS:
                                attention(b, s + 2)
                    if i is not None:
                        dve.drain().then_inc(total_ready, 1)

                dve.wait_ge(w["loaded"], 16 * len(w["loads"]))
                staggered(dve, body)


_INS = ['L0_attn_x', 'L0_attn_w_qkv', 'L0_attn_ln_w', 'L0_attn_w_proj', 'L0_ffn_gate_w', 'L0_ffn_gate_b', 'L0_ffn_w1',
        'L0_ffn_b1', 'L0_ffn_w2', 'L0_ffn_b2', 'L1_attn_ln1_w', 'L1_attn_ln1_b', 'L1_attn_wq', 'L1_attn_bq',
        'L1_attn_wk', 'L1_attn_bk', 'L1_attn_wv', 'L1_attn_bv', 'L1_attn_wo', 'L1_attn_bo', 'L1_attn_ln2_w',
        'L1_attn_ln2_b', 'L1_attn_fc_w', 'L1_attn_fc_b', 'L1_attn_proj_w', 'L1_attn_proj_b', 'L1_ffn_wqkv',
        'L1_ffn_q_scale', 'L1_ffn_k_scale', 'L1_ffn_wo', 'L1_ffn_ln_g', 'L1_ffn_ln_b', 'L1_ffn_w1', 'L1_ffn_b1',
        'L1_ffn_w2', 'L1_ffn_b2']


def shape_constants():
    import numpy as np

    masked = np.float32(-1e30)
    q, k = np.arange(P)[:, None], np.arange(P)[None, :]
    group = 64
    local = np.concatenate([q <= k, k <= q], axis=1)
    first = np.concatenate([np.zeros((P, P), bool), k <= q], axis=1)
    half = np.arange(0, D64, 2, dtype=np.float32)
    freq = (np.float32(1.0) / np.float32(10000.0) ** (half / np.float32(D64))).astype(np.float32)
    t = np.arange(NT, dtype=np.float32)
    angle = (t[:, None] * freq[None, :]).astype(np.float32)
    base = ((half + np.float32(0.4 * D64)) / np.float32(1.4 * D64)).astype(np.float32)
    power = ((t - NT // 2) / np.float32(P // 2)).astype(np.float32)
    scale = (base[None, :] ** power[:, None]).astype(np.float32)
    cos, sin = np.cos(angle), np.sin(angle)
    return {
        "k_ident": np.eye(P, dtype=np.float32),
        "k_iota": np.arange(NE, dtype=np.float32),
        "k_mask_group": np.where((k <= q) & (k // group == q // group), np.float32(0), masked),
        "k_mask_local": np.stack([np.where(m, np.float32(0), masked) for m in (local, first)], axis=1),
        "k_rotary": np.stack([cos * scale, sin * scale, cos / scale, sin / scale], axis=1).astype(np.float32),
    }


def kernel(**inputs):
    import numpy as _np
    import concourse.bacc as _bacc
    from concourse.bass_utils import run_bass_kernel_spmd as _run

    nc = _bacc.Bacc("TRN2", target_bir_lowering=False, num_devices=1)
    arrays, t_in = {}, {}
    for name in _INS:
        a = _np.ascontiguousarray(inputs[name])
        if name == 'L0_attn_x':
            name, a = 'x', a.reshape(NT, C)
        arrays[f"in_{name}"] = a
        t_in[name] = nc.dram_tensor(f"in_{name}", a.shape, mybir.dt.from_np(a.dtype), kind="ExternalInput").ap()
    for name, a in shape_constants().items():
        arrays[name] = a
        t_in[name] = nc.dram_tensor(name, a.shape, F32, kind="ExternalInput").ap()
    out = nc.dram_tensor("out_0_dram", (1, NT, C), F32, kind="ExternalOutput").ap()
    scratch = {name: nc.dram_tensor(f"s_{name}", (NT + (name in PADDED), C), F32).ap()
               for name in ("x1", "xl2") + PADDED}
    build(nc, t_in, out[0], scratch)
    r = _run(nc, [arrays], core_ids=[0])
    return r.results[0]["out_0_dram"]
```

```python
from contextlib import ExitStack

import concourse.bass as bass
from concourse import mybir

F32 = mybir.dt.float32
BF16 = mybir.dt.bfloat16
U32 = mybir.dt.uint32
ALU = mybir.AluOpType
ACT = mybir.ActivationFunctionType
AX = mybir.AxisListType.X

P = 128
C = 256
NCH = C // P
NT = 4096
SUBS = 4
BT = SUBS * P
NB = NT // BT
H16, D16 = 16, 16
NE, ED = 8, 256
MLP = 1024
H8, D64 = 8, 64
INNER = D64 * H8
HID = 682
HCH = (HID + P - 1) // P
EPS_LN, EPS_RMS = 1e-5, 1e-6
NORM_FLOOR = 1e-24
QK_SCALE = 8.0
PADDED = ("xn1", "xm0", "xl1", "xm1")


class Ring:

    def __init__(self, banks, sem, order):
        n = len(banks)
        self.banks = banks
        self.full_sems = [sem(f"bank{b}_full") for b in range(n)]
        self.free_sems = [sem(f"bank{b}_free") for b in range(n)]
        self.at = {tag: (u % n, u // n) for u, tag in enumerate(order)}
        self.per = [len(range(b, len(order), n)) for b in range(n)]

    def bank(self, tag):
        return self.banks[self.at[tag][0]]

    def full(self, tag):
        return self.full_sems[self.at[tag][0]]

    def free(self, tag):
        return self.free_sems[self.at[tag][0]]

    def space(self, tag, i):
        b, k = self.at[tag]
        return self.free_sems[b], i * self.per[b] + (k + 1)

    def data(self, tag, i):
        b, k = self.at[tag]
        return self.full_sems[b], i * self.per[b] + (k + 1)

    def copied(self, tag, i):
        b, k = self.at[tag]
        return self.free_sems[b], i * self.per[b] + (k + 2)

    def open(self, eng):
        for s in self.free_sems:
            eng.sem_inc(s, 1)


def blocks_loop(eng, body):
    with eng.Fori(0, NB - 1) as i:
        body(i, True)
    body(NB - 1, False)


def token_rows(ap, i, first=0, c0=0, c1=C):
    return ap[bass.ds(i * BT + first, BT), c0:c1].rearrange("(s p) c -> p s c", p=P)


def nth(i, s):
    return i * SUBS + (s + 1)


def row_stats(dve, x, st, mv):
    for s in range(SUBS):
        dve.bn_stats(st[:, s, :], x[:, s, :])
    dve.drain()
    for s in range(SUBS):
        r = dve.bn_aggr(mv[:, s, :], st[:, s, :])
    return r


def inverse_root(pool, out, x, eps, neghalf):
    pool.tensor_tensor(out, x, eps, ALU.add)
    pool.drain()
    return pool.tensor_tensor(out, out, neghalf, ALU.pow)


def normalise(dve, xn, x, mv, rs):
    for s in range(SUBS):
        r = dve.tensor_scalar(xn[:, s, :], x[:, s, :], mv[:, s, 0:1], rs[:, s:s + 1], ALU.subtract, ALU.mult)
    return r


def turn_block(pe, ring, tags, i, x, ident):
    for c, tag in enumerate(tags):
        pe.wait_ge(*ring.space(tag, i))
        for s in range(SUBS):
            mm = pe.transpose(ring.bank(tag)[:, s * P:(s + 1) * P], x[:, s, c * P:(c + 1) * P], ident[:, :])
        mm.then_inc(ring.full(tag), 1)


def chunks(ap):
    return ap.rearrange("(c p) n -> p c n", p=P)


def column(ap):
    return ap.rearrange("(c p) -> p c", p=P)


def build(nc, t_in, out, scratch):
    stack = ExitStack()
    with stack:
        def sb(name, shape, dt=F32):
            return stack.enter_context(nc.sbuf_tensor(name, shape, dt))

        semaphores = {}

        def sems(prefix):
            def sem(name):
                if prefix + name not in semaphores:
                    semaphores[prefix + name] = stack.enter_context(nc.semaphore(prefix + name))
                return semaphores[prefix + name]
            return sem

        def clear(prefixes):
            with nc.Block() as block:

                @block.gpsimd
                def _(pool):
                    for name, s in semaphores.items():
                        if name.startswith(prefixes):
                            pool.sem_clear(s)

        used = []

        def buffers(ctx, prefix):
            used.append(prefix)
            turn = f"{prefix}{used.count(prefix)}_"
            return lambda name, shape, dt=F32: ctx.enter_context(nc.sbuf_tensor(turn + name, shape, dt))

        stack.enter_context(nc.allow_non_contiguous_dma(reason="biases, a column per partition: a few KB"))
        banks = [stack.enter_context(nc.psum_tensor(f"bank{b}", [P, 512], F32)) for b in range(4)]
        wide = stack.enter_context(nc.psum_tensor("wide", [P, 4, 512], F32))
        shared = {
            "ident": sb("ident", [P, P]),
            "identb": sb("identb", [P, P], BF16),
            "neghalf": sb("neghalf", [P, 2 * H8]),
            "eps_ln": sb("eps_ln", [P, SUBS]),
            "eps_rms": sb("eps_rms", [P, 2]),
        }
        local = [local_weights(sb, sems(f"w{n}_"), t_in, n) for n in range(2)]
        load_constants(nc, sb, sems("c_"), shared, t_in, scratch)
        first_stage(nc, buffers, sems("a_"), banks, wide, shared, t_in, scratch, local)
        linear = linear_weights(sb, sems("wl_"), t_in)
        for n, (src, mid, dst) in enumerate((("xn1", "xm0", "xl1"), ("xl1", "xm1", "xl2"))):
            local_attention(nc, buffers, sems("d_"), banks, wide, shared, t_in, scratch, local[n], src, mid,
                            [linear] if n == 0 else [])
            local_ffn(nc, buffers, sems("f_"), banks, wide, shared, t_in, scratch, local[n], mid, dst)
            if n == 0:
                clear(("d_", "f_"))
        linear_stage(nc, buffers, sems("l_"), banks, wide, shared, t_in, scratch, linear,
                     [layer["wo"] for layer in local], out)


def local_weights(sb, sem, t_in, n):
    w = {"loaded": sem("loaded"), "loads": []}

    def add(name, shape, src):
        w[name] = sb(f"{name}_{n}", shape)
        if src is not None:
            w["loads"].append((w[name], src))

    full = HID // P * P
    add("wqkv", [P, NCH, 3 * INNER], chunks(t_in["L1_ffn_wqkv"][n]))
    add("wo", [P, INNER // P, C], chunks(t_in["L1_ffn_wo"][n]))
    add("w1", [P, NCH, 2 * HID], chunks(t_in["L1_ffn_w1"][n]))
    add("w2", [P, HCH, C], None)
    w["loads"].append((w["w2"][:, 0:HID // P, :], chunks(t_in["L1_ffn_w2"][n, 0:full])))
    w["loads"].append((w["w2"][0:HID - full, HID // P, :], t_in["L1_ffn_w2"][n, full:HID]))
    add("b1", [P, 2, HCH], None)
    for t in range(2):
        a = t * HID
        w["loads"].append((w["b1"][:, t, 0:HID // P], column(t_in["L1_ffn_b1"][n, a:a + full])))
        w["loads"].append((w["b1"][0:HID - full, t, HID // P:HCH],
                           t_in["L1_ffn_b1"][n, a + full:a + HID].rearrange("(p a) -> p a", a=1)))
    add("b2", [P, C], t_in["L1_ffn_b2"][n].partition_broadcast(P))
    add("lg", [P, NCH], column(t_in["L1_ffn_ln_g"][n]))
    add("lb", [P, NCH], column(t_in["L1_ffn_ln_b"][n]))
    for name in ("q_scale", "k_scale"):
        add(name, [P, D64], t_in[f"L1_ffn_{name}"][n].partition_broadcast(P))
        add(name + "_turned", [P, D64], None)
        for a in range(2):
            other = slice((1 - a) * D64 // 2, (2 - a) * D64 // 2)
            w["loads"].append((w[name + "_turned"][:, a * D64 // 2:(a + 1) * D64 // 2],
                               t_in[f"L1_ffn_{name}"][n, other].partition_broadcast(P)))
    return w


def linear_weights(sb, sem, t_in):
    w = {"loaded": sem("loaded"), "loads": []}
    w["wqkv"] = sb("l_wqkv", [P, NCH, 3 * C])
    w["bqkv"] = sb("l_bqkv", [P, 3 * C])
    for k, name in enumerate("qkv"):
        w["loads"].append((w["wqkv"][:, :, k * C:(k + 1) * C], chunks(t_in[f"L1_attn_w{name}"])))
        w["loads"].append((w["bqkv"][:, k * C:(k + 1) * C], t_in[f"L1_attn_b{name}"].partition_broadcast(P)))
    for name, shape, src in (
        ("wo", [P, NCH, C], chunks(t_in["L1_attn_wo"])),
        ("fc", [P, NCH, MLP], chunks(t_in["L1_attn_fc_w"])),
        ("proj", [P, MLP // P, C], chunks(t_in["L1_attn_proj_w"])),
        ("fcb", [P, MLP // P], column(t_in["L1_attn_fc_b"])),
        ("bo", [P, C], t_in["L1_attn_bo"].partition_broadcast(P)),
        ("projb", [P, C], t_in["L1_attn_proj_b"].partition_broadcast(P)),
        ("g1", [P, NCH], column(t_in["L1_attn_ln1_w"])),
        ("o1", [P, NCH], column(t_in["L1_attn_ln1_b"])),
        ("g2", [P, NCH], column(t_in["L1_attn_ln2_w"])),
        ("o2", [P, NCH], column(t_in["L1_attn_ln2_b"])),
    ):
        w[name] = sb("l_" + name, shape)
        w["loads"].append((w[name], src))
    return w


def whole(t):
    return t if isinstance(t, bass.AP) else t[tuple(slice(None) for _ in t.shape)]


def load_constants(nc, sb, sem, shared, t_in, scratch):
    zrow = sb("zrow", [1, C])
    loaded, zeroed, stored = sem("loaded"), sem("zeroed"), sem("stored")
    with nc.Block() as block:

        @block.sync
        def _(sp):
            sp.dma_start(shared["ident"][:, :], t_in["k_ident"]).then_inc(loaded, 16)
            sp.wait_ge(zeroed, 1)
            for name in PADDED:
                sp.dma_start(scratch[name][0:1, :], zrow[:, :]).then_inc(stored, 16)
            sp.wait_ge(stored, 16 * len(PADDED))

        @block.vector
        def _(dve):
            dve.memset(zrow[:, :], 0.0).then_inc(zeroed, 1)
            for name, value in (("neghalf", -0.5), ("eps_ln", EPS_LN), ("eps_rms", EPS_RMS)):
                dve.memset(shared[name][:, :], value)
            dve.wait_ge(loaded, 16)
            dve.tensor_copy(shared["identb"][:, :], shared["ident"][:, :])
            dve.drain()


def first_stage(nc, buffers, sem, banks, wide, shared, t_in, scratch, later):
    ctx = ExitStack()
    with ctx:
        sb = buffers(ctx, "a_")
        ident, identb, neghalf = shared["ident"], shared["identb"], shared["neghalf"]
        wqkv = sb("wqkv", [P, NCH, 3 * C])
        wproj = sb("wproj", [P, NCH, C])
        w1 = sb("w1", [P, NE, NCH, ED])
        w2 = sb("w2", [P, NE, ED // P, C])
        gw = sb("gw", [P, NCH, NE])
        gb = sb("gb", [P, NE])
        b1 = sb("b1", [P, NE, ED // P])
        b2 = sb("b2", [NE, C])
        lnw = sb("lnw", [P, C])
        iota = sb("iota", [P, NE])
        maskf = sb("maskf", [P, P])
        mask = sb("mask", [P, 4, P], BF16)
        xin = sb("xin", [P, SUBS, C])
        st = sb("st", [P, SUBS, 6])
        mv = sb("mv", [P, SUBS, 2])
        rs = sb("rs", [P, SUBS])
        xn = sb("xn", [P, SUBS, C])
        xT = sb("xT", [P, NCH, BT])
        xres = sb("xres", [P, SUBS, C])
        acc = sb("acc", [P, SUBS, C])
        st2 = sb("st2", [P, SUBS, 6])
        mv2 = sb("mv2", [P, SUBS, 2])
        rs2 = sb("rs2", [P, SUBS])
        xn1 = sb("xn1", [P, SUBS, C])
        score = sb("score", [P, SUBS, NE])
        top = sb("top", [P, SUBS, 8])
        topi = sb("topi", [P, SUBS, 8], U32)
        topf = sb("topf", [P, SUBS, 8])
        pick = sb("pick", [P, 2, SUBS, NE])
        comb = sb("comb", [P, SUBS, NE])
        combT = sb("combT", [NE, BT])
        sq = sb("sq", [P, 2, C])
        ss = sb("ss", [P, 2])
        rr = sb("rr", [P, 2])
        qk = sb("qk", [P, 2, H16, 32])
        v = sb("v", [P, 2, C])
        qkT = sb("qkT", [P, 2, 4, P])
        mx = sb("mx", [P, H16])
        nm = sb("nm", [P, H16])
        probs = sb("probs", [P, 4, 4, P])
        den = sb("den", [P, H16])
        rden = sb("rden", [P, H16])
        pT = sb("pT", [P, 4, 4, P])
        y = sb("y", [P, C])
        yT = sb("yT", [P, NCH, P])
        hT = sb("hT", [P, 2, ED // P, BT])

        order = ["xT0", "xT1", "gate", "qk0", "v0", "h0_0", "h0_1", "cT", "tq0", "tk0", "eo0_0", "eo0_1"]
        for s in range(SUBS):
            e = 2 * s + 1
            order += [f"h{e}_0", f"h{e}_1", f"eo{e}_0", f"eo{e}_1"]
            if s + 1 < SUBS:
                order += [f"qk{s + 1}", f"v{s + 1}", f"h{e + 1}_0", f"h{e + 1}_1"]
            order += [f"pv{s}"]
            if s + 1 < SUBS:
                order += [f"tq{s + 1}", f"tk{s + 1}", f"eo{e + 1}_0", f"eo{e + 1}_1"]
            order += [f"yT{s}", f"proj{s}"]
        ring = Ring(banks, sem, order)

        w_loaded, setup_done = sem("w_loaded"), sem("setup_done")
        x_loaded, res_loaded, res_used = sem("x_loaded"), sem("res_loaded"), sem("res_used")
        stats_ready, rs_ready, xn_ready = sem("stats_ready"), sem("rs_ready"), sem("xn_ready")
        comb_ready = sem("comb_ready")
        ss_ready, rr_ready = sem("ss_ready"), sem("rr_ready")
        scores_done, max_ready, probs_ready = sem("scores_done"), sem("max_ready"), sem("probs_ready")
        turned, pT_act, pT_dve = sem("turned"), sem("pT_act"), sem("pT_dve")
        y_ready = sem("y_ready")
        acc_ready, stats2_ready, rs2_ready, xn1_ready = (
            sem("acc_ready"), sem("stats2_ready"), sem("rs2_ready"), sem("xn1_ready"))
        stored = sem("stored")

        weights = (
            (gw[:, :, :], chunks(t_in["L0_ffn_gate_w"])),
            (wqkv[:, :, :], chunks(t_in["L0_attn_w_qkv"])),
            (gb[:, :], t_in["L0_ffn_gate_b"].partition_broadcast(P)),
            (lnw[:, :], t_in["L0_attn_ln_w"].partition_broadcast(P)),
            (b1[:, :, :], t_in["L0_ffn_b1"].rearrange("e (m p) -> p e m", p=P)),
            (b2[:, :], t_in["L0_ffn_b2"]),
            (iota[:, :], t_in["k_iota"].partition_broadcast(P)),
            (maskf[:, :], t_in["k_mask_group"]),
            (wproj[:, :, :], chunks(t_in["L0_attn_w_proj"])),
        ) + tuple(
            (dst[:, a:a + 4, :, :], src[a:a + 4].rearrange("e (c p) n -> p e c n", p=P))
            for a in (0, 4) for dst, src in ((w1, t_in["L0_ffn_w1"]), (w2, t_in["L0_ffn_w2"]))
        )

        with nc.Block() as block:

            @block.sync
            def _(sp):
                def load_x(i):
                    sp.dma_start(xin[:, :, :], token_rows(t_in["x"], i)).then_inc(x_loaded, 16)

                def load_res(i):
                    sp.dma_start(xres[:, :, :], token_rows(t_in["x"], i)).then_inc(res_loaded, 16)

                ring.open(sp)
                sp.sem_inc(stored, 32)
                load_x(0)
                load_res(0)
                for dst, src in weights:
                    sp.dma_start(dst, src).then_inc(w_loaded, 16)
                for group in later:
                    for dst, src in group["loads"]:
                        sp.dma_start(whole(dst), src).then_inc(group["loaded"], 16)

                def body(i, more):
                    if more:
                        sp.wait_ge(xn_ready, i + 1)
                        load_x(i + 1)
                        sp.wait_ge(res_used, i + 1)
                        load_res(i + 1)
                    sp.wait_ge(acc_ready, i + 1)
                    sp.dma_start(token_rows(scratch["x1"], i), acc[:, :, :]).then_inc(stored, 16)
                    sp.wait_ge(xn1_ready, i + 1)
                    sp.dma_start(token_rows(scratch["xn1"], i, 1), xn1[:, :, :]).then_inc(stored, 16)

                blocks_loop(sp, body)
                sp.wait_ge(stored, 32 * (NB + 1))

            @block.gpsimd
            def _(pool):
                def front(i):
                    pool.wait_ge(stats_ready, i + 1)
                    inverse_root(pool, rs[:, :], mv[:, :, 1], shared["eps_ln"][:, :], neghalf[:, 0:SUBS]).then_inc(rs_ready, 1)

                def rms(i, s):
                    pool.wait_ge(ss_ready, nth(i, s))
                    inverse_root(pool, rr[:, :], ss[:, :], shared["eps_rms"][:, :], neghalf[:, 0:2]).then_inc(rr_ready, 1)

                def body(i, more):
                    rms(i, 0)
                    rms(i, 1)
                    rms(i, 2)
                    if more:
                        front(i + 1)
                    rms(i, 3)
                    pool.wait_ge(stats2_ready, i + 1)
                    inverse_root(pool, rs2[:, :], mv2[:, :, 1], shared["eps_ln"][:, :], neghalf[:, 0:SUBS])\
                        .then_inc(rs2_ready, 1)

                front(0)
                blocks_loop(pool, body)

            @block.tensor
            def _(pe):
                def gate(i):
                    pe.wait_ge(*ring.space("gate", i))
                    o = ring.bank("gate")
                    for s in range(SUBS):
                        for c in range(NCH):
                            mm = pe.matmul(o[:, s * NE:(s + 1) * NE], xT[:, c, s * P:(s + 1) * P], gw[:, c, :],
                                           start=c == 0, stop=c == NCH - 1)
                    mm.then_inc(ring.full("gate"), 1)

                def qkv(i, s):
                    for tag, a, b in ((f"qk{s}", 0, 2 * C), (f"v{s}", 2 * C, 3 * C)):
                        pe.wait_ge(*ring.space(tag, i))
                        for c in range(NCH):
                            mm = pe.matmul(ring.bank(tag)[:, 0:b - a], xT[:, c, s * P:(s + 1) * P], wqkv[:, c, a:b],
                                           start=c == 0, stop=c == NCH - 1)
                        mm.then_inc(ring.full(tag), 1)

                def turn_qk(i, s):
                    pe.wait_ge(*ring.copied(f"qk{s}", i))
                    for t, tag in enumerate((f"tq{s}", f"tk{s}")):
                        pe.wait_ge(*ring.space(tag, i))
                        for g in range(4):
                            mm = pe.transpose(ring.bank(tag)[:, g * P:(g + 1) * P],
                                              qk[:, t, 4 * g:4 * g + 4, :].rearrange("p a b -> p (a b)"), ident[:, :])
                        mm.then_inc(ring.full(tag), 1)

                def expert_in(i, e):
                    for m in range(ED // P):
                        tag = f"h{e}_{m}"
                        pe.wait_ge(*ring.space(tag, i))
                        for c in range(NCH):
                            mm = pe.matmul(ring.bank(tag)[:, :], w1[:, e, c, m * P:(m + 1) * P], xT[:, c, :],
                                           start=c == 0, stop=c == NCH - 1)
                        mm.then_inc(ring.full(tag), 1)

                def expert_out(i, e):
                    for m in range(ED // P):
                        pe.wait_ge(*ring.copied(f"h{e}_{m}", i))
                    for n in range(2):
                        tag = f"eo{e}_{n}"
                        pe.wait_ge(*ring.space(tag, i))
                        for s in (2 * n, 2 * n + 1):
                            for m in range(ED // P):
                                mm = pe.matmul(ring.bank(tag)[:, (s % 2) * C:(s % 2 + 1) * C],
                                               hT[:, e % 2, m, s * P:(s + 1) * P],
                                               w2[:, e, m, :], start=m == 0, stop=m == ED // P - 1)
                        mm.then_inc(ring.full(tag), 1)

                def turn_comb(i):
                    pe.wait_ge(comb_ready, i + 1)
                    pe.wait_ge(*ring.space("cT", i))
                    for s in range(SUBS):
                        mm = pe.transpose(ring.bank("cT")[0:NE, s * P:(s + 1) * P], comb[:, s, :], ident[:, :])
                    mm.then_inc(ring.full("cT"), 1)

                def scores(i, s):
                    pe.wait_ge(*ring.copied(f"tq{s}", i))
                    pe.wait_ge(*ring.copied(f"tk{s}", i))
                    for j in range(4):
                        pe.matmul(wide[:, j, :], identb[:, :], mask[:, :, :].rearrange("p a b -> p (a b)"),
                                  start=True, stop=False)
                    for g in range(4):
                        for j in range(4):
                            r = slice(32 * j, 32 * j + D16)
                            mm = pe.matmul(wide[:, j, g * P:(g + 1) * P], qkT[r, 0, g, :], qkT[r, 1, g, :],
                                           start=False, stop=g == 3)
                    mm.then_inc(scores_done, 1)

                def turn_probs(i, s):
                    pe.wait_ge(probs_ready, nth(i, s))
                    for j in range(4):
                        for g in range(4):
                            mm = pe.transpose(wide[:, j, g * P:(g + 1) * P], probs[:, j, g, :], ident[:, :])
                    mm.then_inc(turned, 1)

                def values(i, s):
                    tag = f"pv{s}"
                    pe.wait_ge(pT_act, nth(i, s))
                    pe.wait_ge(pT_dve, nth(i, s))
                    pe.wait_ge(*ring.copied(f"v{s}", i))
                    pe.wait_ge(*ring.space(tag, i))
                    for j in range(4):
                        for g in range(4):
                            h = slice((4 * g + j) * D16, (4 * g + j + 1) * D16)
                            mm = pe.matmul(ring.bank(tag)[:, h], pT[:, j, g, :], v[:, s % 2, h], start=True, stop=True)
                    mm.then_inc(ring.full(tag), 1)

                def project(i, s):
                    pe.wait_ge(y_ready, nth(i, s))
                    pe.wait_ge(*ring.space(f"yT{s}", i))
                    for c in range(NCH):
                        mm = pe.transpose(ring.bank(f"yT{s}")[:, c * P:(c + 1) * P], y[:, c * P:(c + 1) * P], ident[:, :])
                    mm.then_inc(ring.full(f"yT{s}"), 1)
                    o = ring.bank(f"proj{s}")
                    pe.wait_ge(*ring.space(f"proj{s}", i))
                    if s == 0:
                        pe.wait_ge(*ring.copied("cT", i))
                    pe.matmul(o[:, 0:C], combT[:, s * P:(s + 1) * P], b2[:, :], start=True, stop=False)
                    pe.wait_ge(*ring.copied(f"yT{s}", i))
                    for c in range(NCH):
                        mm = pe.matmul(o[:, 0:C], yT[:, c, :], wproj[:, c, :], start=False, stop=c == NCH - 1)
                    mm.then_inc(ring.full(f"proj{s}"), 1)

                def body(i, more):
                    pe.wait_ge(xn_ready, i + 1)
                    turn_block(pe, ring, ("xT0", "xT1"), i, xn, ident)
                    for tag in ("xT0", "xT1"):
                        pe.wait_ge(*ring.copied(tag, i))
                    gate(i)
                    qkv(i, 0)
                    expert_in(i, 0)
                    turn_comb(i)
                    turn_qk(i, 0)
                    expert_out(i, 0)
                    for s in range(SUBS):
                        e = 2 * s + 1
                        scores(i, s)
                        expert_in(i, e)
                        expert_out(i, e)
                        turn_probs(i, s)
                        if s + 1 < SUBS:
                            qkv(i, s + 1)
                            expert_in(i, e + 1)
                        values(i, s)
                        if s + 1 < SUBS:
                            turn_qk(i, s + 1)
                            expert_out(i, e + 1)
                        project(i, s)

                pe.wait_ge(w_loaded, 16 * len(weights))
                pe.wait_ge(setup_done, 2)
                blocks_loop(pe, body)

            @block.scalar
            def _(act):
                def squares(i, s):
                    act.wait_ge(*ring.data(f"qk{s}", i))
                    for t in range(2):
                        r = act.activation(sq[:, t, :], ring.bank(f"qk{s}")[:, t * C:(t + 1) * C], ACT.Square,
                                           scale=C ** -0.5, accum_out=ss[:, t:t + 1])
                    r.then_inc(ss_ready, 1)

                def copy(i, tag, dst, src):
                    act.wait_ge(*ring.data(tag, i))
                    act.copy(dst, src).then_inc(ring.free(tag), 1)

                def hidden(i, e):
                    if e >= 2:
                        act.wait_ge(*ring.data(f"eo{e - 2}_1", i))
                    for m in range(ED // P):
                        tag = f"h{e}_{m}"
                        act.wait_ge(*ring.data(tag, i))
                        act.activation(hT[:, e % 2, m, :], ring.bank(tag)[:, :], ACT.Relu, bias=b1[:, e, m:m + 1])\
                           .then_inc(ring.free(tag), 1)

                def exponentials(i, s):
                    act.wait_ge(max_ready, nth(i, s))
                    for j in range(4):
                        for g in range(4):
                            n = 4 * j + g
                            r = act.activation(probs[:, j, g, :], wide[:, j, g * P:(g + 1) * P], ACT.Exp,
                                               bias=nm[:, n:n + 1], scale=D16 ** -0.5, accum_out=den[:, n:n + 1])
                    r.then_inc(probs_ready, 1)

                def keep_turned(i, s):
                    act.wait_ge(turned, nth(i, s))
                    act.copy(pT[:, 2:4, :, :].rearrange("p a b c -> p (a b c)"),
                             wide[:, 2:4, :].rearrange("p a b -> p (a b)")).then_inc(pT_act, 1)

                def body(i, more):
                    for c in range(NCH):
                        copy(i, f"xT{c}", xT[:, c, :], ring.bank(f"xT{c}")[:, :])
                    squares(i, 0)
                    copy(i, "v0", v[:, 0, :], ring.bank("v0")[:, 0:C])
                    hidden(i, 0)
                    copy(i, "tq0", qkT[:, 0, :, :].rearrange("p a b -> p (a b)"), ring.bank("tq0")[:, :])
                    for s in range(SUBS):
                        e = 2 * s + 1
                        hidden(i, e)
                        exponentials(i, s)
                        keep_turned(i, s)
                        if s + 1 < SUBS:
                            squares(i, s + 1)
                            copy(i, f"v{s + 1}", v[:, (s + 1) % 2, :], ring.bank(f"v{s + 1}")[:, 0:C])
                            hidden(i, e + 1)
                            tag = f"tq{s + 1}"
                            copy(i, tag, qkT[:, 0, :, :].rearrange("p a b -> p (a b)"), ring.bank(tag)[:, :])
                        tag = f"yT{s}"
                        copy(i, tag, yT[:, :, :].rearrange("p a b -> p (a b)"), ring.bank(tag)[:, 0:C])

                act.wait_ge(w_loaded, 16 * len(weights))
                blocks_loop(act, body)

            @block.vector
            def _(dve):
                def front_stats(i):
                    dve.wait_ge(x_loaded, 16 * (i + 1))
                    row_stats(dve, xin, st, mv).then_inc(stats_ready, 1)

                def front_norm(i):
                    dve.wait_ge(rs_ready, i + 1)
                    normalise(dve, xn, xin, mv, rs).then_inc(xn_ready, 1)

                def combination(i):
                    dve.wait_ge(*ring.data("gate", i))
                    dve.tensor_tensor(score[:, :, :], ring.bank("gate")[:, 0:SUBS * NE].rearrange("p (s e) -> p s e", s=SUBS),
                                      gb[:, :].unsqueeze(1).broadcast_to([P, SUBS, NE]), ALU.add)\
                       .then_inc(ring.free("gate"), 1)
                    dve.drain()
                    for s in range(SUBS):
                        dve.max(top[:, s, :], score[:, s, :])
                    dve.drain()
                    for s in range(SUBS):
                        dve.max_index(topi[:, s, :], top[:, s, :], score[:, s, :])
                    dve.drain()
                    dve.tensor_copy(topf[:, :, :], topi[:, :, :])
                    dve.drain()
                    for s in range(SUBS):
                        for t in range(2):
                            dve.tensor_scalar(pick[:, t, s, :], iota[:, :], topf[:, s, t:t + 1], top[:, s, t:t + 1],
                                              ALU.is_equal, ALU.mult)
                    dve.drain()
                    dve.tensor_tensor(comb[:, :, :], pick[:, 0, :, :], pick[:, 1, :, :], ALU.add).then_inc(comb_ready, 1)

                def norm_qk(i, s):
                    tag = f"qk{s}"
                    dve.wait_ge(rr_ready, nth(i, s))
                    dve.wait_ge(*ring.data(tag, i))
                    for t in range(2):
                        r = dve.scalar_tensor_tensor(
                            out=qk[:, t, :, 0:D16],
                            in0=ring.bank(tag)[:, t * C:(t + 1) * C].rearrange("p (h d) -> p h d", h=H16),
                            scalar=rr[:, t:t + 1], in1=lnw[:, :].rearrange("p (h d) -> p h d", h=H16),
                            op0=ALU.mult, op1=ALU.mult)
                    r.then_inc(ring.free(tag), 1)

                def copy(i, tag, dst, src):
                    dve.wait_ge(*ring.data(tag, i))
                    dve.tensor_copy(dst, src).then_inc(ring.free(tag), 1)

                def add_expert(i, e):
                    dve.drain()
                    if e == 0:
                        dve.wait_ge(res_loaded, 16 * (i + 1))
                        dve.wait_ge(stored, (i + 1) * 32)
                    for s in range(SUBS):
                        tag = f"eo{e}_{s // 2}"
                        if s % 2 == 0:
                            dve.wait_ge(*ring.data(tag, i))
                        r = dve.scalar_tensor_tensor(
                            out=acc[:, s, :], in0=ring.bank(tag)[:, (s % 2) * C:(s % 2 + 1) * C],
                            scalar=comb[:, s, e:e + 1], in1=(acc if e else xres)[:, s, :], op0=ALU.mult, op1=ALU.add)
                        if s % 2 == 1:
                            r.then_inc(ring.free(tag), 1)
                    if e == 0:
                        dve.drain().then_inc(res_used, 1)

                def maxima(i, s):
                    dve.wait_ge(scores_done, nth(i, s))
                    dve.tensor_reduce(mx[:, :], wide[:, :, :].rearrange("p j (g k) -> p (j g) k", g=4), AX, ALU.max)
                    dve.drain()
                    dve.tensor_scalar(nm[:, :], mx[:, :], -(D16 ** -0.5), None, ALU.mult).then_inc(max_ready, 1)

                def keep_turned(i, s):
                    dve.wait_ge(turned, nth(i, s))
                    dve.tensor_copy(pT[:, 0:2, :, :].rearrange("p a b c -> p (a b c)"),
                                    wide[:, 0:2, :].rearrange("p a b -> p (a b)")).then_inc(pT_dve, 1)
                    dve.reciprocal(rden[:, :], den[:, :])
                    dve.drain()

                def outputs(i, s):
                    tag = f"pv{s}"
                    dve.wait_ge(*ring.data(tag, i))
                    dve.tensor_tensor(
                        y[:, :].rearrange("p (g j e) -> p j g e", g=4, j=4),
                        ring.bank(tag)[:, 0:C].rearrange("p (g j e) -> p j g e", g=4, j=4),
                        rden[:, :].rearrange("p (j g) -> p j g", j=4).unsqueeze(3).broadcast_to([P, 4, 4, D16]),
                        ALU.mult).then_inc(ring.free(tag), 1)
                    dve.drain().then_inc(y_ready, 1)

                def body(i, more):
                    combination(i)
                    norm_qk(i, 0)
                    copy(i, "cT", combT[:, :], ring.bank("cT")[0:NE, :])
                    copy(i, "tk0", qkT[:, 1, :, :].rearrange("p a b -> p (a b)"), ring.bank("tk0")[:, :])
                    add_expert(i, 0)
                    for s in range(SUBS):
                        e = 2 * s + 1
                        maxima(i, s)
                        add_expert(i, e)
                        keep_turned(i, s)
                        if s + 1 < SUBS:
                            norm_qk(i, s + 1)
                        if more and s == 1:
                            front_stats(i + 1)
                        outputs(i, s)
                        if s + 1 < SUBS:
                            tag = f"tk{s + 1}"
                            copy(i, tag, qkT[:, 1, :, :].rearrange("p a b -> p (a b)"), ring.bank(tag)[:, :])
                            add_expert(i, e + 1)
                        if more and s == 2:
                            front_norm(i + 1)
                        tag = f"proj{s}"
                        dve.drain()
                        dve.wait_ge(*ring.data(tag, i))
                        dve.tensor_tensor(acc[:, s, :], ring.bank(tag)[:, 0:C], acc[:, s, :], ALU.add)\
                           .then_inc(ring.free(tag), 1)
                    dve.drain().then_inc(acc_ready, 1)
                    row_stats(dve, acc, st2, mv2).then_inc(stats2_ready, 1)
                    dve.wait_ge(rs2_ready, i + 1)
                    normalise(dve, xn1, acc, mv2, rs2).then_inc(xn1_ready, 1)

                dve.memset(qk[:, :, :, :], 0.0).then_inc(setup_done, 1)
                dve.wait_ge(w_loaded, 16 * len(weights))
                dve.tensor_copy(mask[:, :, :], maskf[:, :].unsqueeze(1).broadcast_to([P, 4, P])).then_inc(setup_done, 1)
                dve.drain()
                front_stats(0)
                front_norm(0)
                blocks_loop(dve, body)


def shifted_loads(sp, dst, src, i, loaded):
    sp.dma_start(dst[:, :, 0:P], token_rows(src, i, 1, 0, P)).then_inc(loaded, 16)
    sp.dma_start(dst[:, :, P:C], token_rows(src, i, 0, P, C)).then_inc(loaded, 16)


def local_attention(nc, buffers, sem, banks, wide, shared, t_in, scratch, w, src, dst, prefetch):
    ctx = ExitStack()
    with ctx:
        sb = buffers(ctx, "d_")
        ident, identb, neghalf = shared["ident"], shared["identb"], shared["neghalf"]
        maskf = sb("maskf", [P, 2, 2 * P])
        mask = sb("mask", [P, 2, 2, 2 * P], BF16)
        xin = sb("xin", [P, SUBS, C])
        xT = sb("xT", [P, NCH, BT])
        xres = sb("xres", [P, SUBS, C])
        xout = sb("xout", [P, SUBS, C])
        rotary = sb("rotary", [P, SUBS, 4, D64 // 2])
        turn = sb("turn", [P, SUBS, 4, D64])
        junk = sb("junk", [P, 2, INNER])
        ss = sb("ss", [P, 2, H8])
        rr = sb("rr", [P, 2, 2, H8])
        rot = sb("rot", [P, 2, 2, INNER])
        qk = sb("qk", [P, 2, INNER])
        qT = sb("qT", [P, H8 // 2, P])
        kT = sb("kT", [P, H8 // 2, SUBS + 1, P])
        v = sb("v", [P, SUBS + 1, INNER])
        mx = sb("mx", [P, H8])
        scale = sb("scale", [P, H8])
        nm = sb("nm", [P, H8])
        probs = sb("probs", [P, 4, 2, 2 * P])
        den = sb("den", [P, H8])
        rden = sb("rden", [P, H8])
        pT = sb("pT", [P, 4, 4, P])
        o = sb("o", [P, INNER])
        oT = sb("oT", [P, INNER // P, P])

        order = ["xT0", "xT1"]
        for s in range(SUBS):
            order += [f"{t}{s}" for t in ("q", "k", "v", "tq", "tk")]
        ring = Ring(banks[0:3], sem, order)
        order = []
        for s in range(SUBS):
            order += [f"pv{s}", f"oT{s}", f"wo{s}"]
        out_ring = Ring(banks[3:4], lambda name: sem("out_" + name), order)

        def ahead(i, s, n, last):
            return (i, s + n) if s + n < SUBS else None if last else (i + 1, s + n - SUBS)

        def staggered(eng, body):
            body(0, True, False)
            with eng.Fori(1, NB - 1) as i:
                body(i, False, False)
            body(NB - 1, False, True)

        def place(h):
            pair, odd = h // 2, h % 2
            return 2 * odd + pair // 2, pair % 2

        setup_loaded, setup_done = sem("setup_loaded"), sem("setup_done")
        x_loaded, x_used, res_loaded, rotary_loaded = (
            sem("x_loaded"), sem("x_used"), sem("res_loaded"), sem("rotary_loaded"))
        turn_ready, mask_ready, before_ready = sem("turn_ready"), sem("mask_ready"), sem("before_ready")
        squared, ss_ready, rr_ready = sem("squared"), sem("ss_ready"), sem("rr_ready")
        parts_ready, qk_ready = sem("parts_ready"), sem("qk_ready")
        scores_done, max_ready, probs_ready = sem("scores_done"), sem("max_ready"), sem("probs_ready")
        turned, pT_act, pT_dve = sem("turned"), sem("pT_act"), sem("pT_dve")
        o_ready, xout_ready, stored = sem("o_ready"), sem("xout_ready"), sem("stored")

        with nc.Block() as block:

            @block.sync
            def _(sp):
                def load(i):
                    shifted_loads(sp, xin, scratch[src], i, x_loaded)

                def load_rotary(i):
                    sp.dma_start(rotary[:, :, :, :],
                                 t_in["k_rotary"][bass.ds(i * BT, BT), :, :].rearrange("(s p) a d -> p s (a d)", p=P))\
                      .then_inc(rotary_loaded, 16)

                def load_res(i):
                    sp.dma_start(xres[:, :, :], token_rows(scratch[src], i, 1)).then_inc(res_loaded, 16)

                ring.open(sp)
                out_ring.open(sp)
                sp.sem_inc(stored, 16)
                load(0)
                load_rotary(0)
                load_res(0)
                sp.dma_start(maskf[:, :, :], t_in["k_mask_local"]).then_inc(setup_loaded, 16)
                for group in prefetch:
                    for d, a in group["loads"]:
                        sp.dma_start(whole(d), a).then_inc(group["loaded"], 16)

                def body(i, more):
                    if more:
                        sp.wait_ge(*ring.data("xT1", i))
                        load(i + 1)
                        sp.wait_ge(turn_ready, i + 1)
                        load_rotary(i + 1)
                    sp.wait_ge(xout_ready, i + 1)
                    if more:
                        load_res(i + 1)
                    sp.dma_start(token_rows(scratch[dst], i, 1), xout[:, :, :]).then_inc(stored, 16)

                blocks_loop(sp, body)
                sp.wait_ge(stored, 16 * (NB + 1))

            @block.gpsimd
            def _(pool):
                def tables(i):
                    for t, name in enumerate(("q_scale", "k_scale")):
                        for a, (table, scales) in enumerate(((2 * t, w[name]), (2 * t + 1, w[name + "_turned"]))):
                            r = pool.tensor_tensor(
                                turn[:, :, 2 * t + a, :].rearrange("p s (a d) -> p s a d", a=2),
                                rotary[:, :, table, :].unsqueeze(2).broadcast_to([P, SUBS, 2, D64 // 2]),
                                scales[:, :].rearrange("p (a d) -> p a d", a=2).unsqueeze(1)
                                            .broadcast_to([P, SUBS, 2, D64 // 2]), ALU.mult)
                    return r

                def roots(i, s):
                    pool.wait_ge(ss_ready, nth(i, s))
                    pool.tensor_tensor(rr[:, s % 2, :, :].rearrange("p a b -> p (a b)"), ss[:, :, :].rearrange("p a b -> p (a b)"),
                                       neghalf[:, :], ALU.pow).then_inc(rr_ready, 1)

                def rotate(i, s):
                    pool.wait_ge(parts_ready, nth(i, s))
                    pool.tensor_tensor(qk[:, :, :], rot[:, :, 0, :], rot[:, :, 1, :], ALU.add)
                    pool.drain()
                    pool.tensor_tensor(qk[:, 1, :].rearrange("p (h d) -> p h d", h=H8),
                                       qk[:, 1, :].rearrange("p (h d) -> p h d", h=H8),
                                       rr[:, s % 2, 1, :].unsqueeze(2).broadcast_to([P, H8, D64]), ALU.mult).then_inc(qk_ready, 1)

                def body(i, more):
                    for s in range(SUBS):
                        if s == 0:
                            pool.wait_ge(rotary_loaded, 16 * (i + 1))
                            tables(i).then_inc(turn_ready, 1)
                        roots(i, s)
                        rotate(i, s)

                pool.memset(kT[:, :, 0, :], 0.0)
                pool.memset(v[:, 0, :], 0.0).then_inc(before_ready, 1)
                pool.wait_ge(w["loaded"], 16 * len(w["loads"]))
                for name in ("q_scale_turned", "k_scale_turned"):
                    r = pool.tensor_scalar(w[name][:, 0:D64 // 2], w[name][:, 0:D64 // 2], -1.0, None, ALU.mult)
                pool.drain()
                blocks_loop(pool, body)

            @block.tensor
            def _(pe):
                def channels(i, s, n):
                    tag = f"{'qkv'[n]}{s}"
                    pe.wait_ge(*ring.space(tag, i))
                    for c in range(NCH):
                        mm = pe.matmul(ring.bank(tag)[:, :], xT[:, c, s * P:(s + 1) * P],
                                       w["wqkv"][:, c, n * INNER:(n + 1) * INNER], start=c == 0, stop=c == NCH - 1)
                    mm.then_inc(ring.full(tag), 1)

                def turn_x(i):
                    pe.wait_ge(x_loaded, 32 * (i + 1))
                    turn_block(pe, ring, ("xT0", "xT1"), i, xin, ident)

                def turn_qk(i, s):
                    pe.wait_ge(qk_ready, nth(i, s))
                    for t, tag in enumerate((f"tq{s}", f"tk{s}")):
                        pe.wait_ge(*ring.space(tag, i))
                        for g in range(INNER // P):
                            mm = pe.transpose(ring.bank(tag)[:, g * P:(g + 1) * P], qk[:, t, g * P:(g + 1) * P], ident[:, :])
                        mm.then_inc(ring.full(tag), 1)

                def scores(i, s):
                    pe.wait_ge(*ring.copied(f"tq{s}", i))
                    pe.wait_ge(*ring.copied(f"tk{s}", i))
                    if s == 0:
                        pe.wait_ge(mask_ready, i + 1)
                    for b in range(4):
                        pe.matmul(wide[:, b, :], identb[:, :], mask[:, int(s == 0), :, :].rearrange("p a b -> p (a b)"),
                                  start=True, stop=False)
                    for pair in (0, 2, 1, 3):
                        for odd in range(2):
                            h = 2 * pair + odd
                            b, half = place(h)
                            r = slice(D64 * odd, D64 * (odd + 1))
                            mm = pe.matmul(wide[:, b, half * 2 * P:(half + 1) * 2 * P], qT[r, pair, :],
                                           kT[r, pair, s:s + 2, :].rearrange("p a b -> p (a b)"),
                                           start=False, stop=half == 1)
                    mm.then_inc(scores_done, 1)

                def turn_probs(i, s):
                    pe.wait_ge(probs_ready, nth(i, s))
                    for b in range(4):
                        for g in range(4):
                            mm = pe.transpose(wide[:, b, g * P:(g + 1) * P],
                                              probs[:, b, g // 2, (g % 2) * P:(g % 2 + 1) * P], ident[:, :])
                    mm.then_inc(turned, 1)

                def values(i, s):
                    tag = f"pv{s}"
                    pe.wait_ge(pT_act, nth(i, s))
                    pe.wait_ge(pT_dve, nth(i, s))
                    pe.wait_ge(*ring.copied(f"v{s}", i))
                    pe.wait_ge(*out_ring.space(tag, i))
                    for h in range(H8):
                        b, half = place(h)
                        cols = slice(h * D64, (h + 1) * D64)
                        for k in range(2):
                            mm = pe.matmul(out_ring.bank(tag)[:, cols], pT[:, b, 2 * half + k, :], v[:, s + k, cols],
                                           start=k == 0, stop=k == 1)
                    mm.then_inc(out_ring.full(tag), 1)

                def turn_o(i, s):
                    tag = f"oT{s}"
                    pe.wait_ge(o_ready, nth(i, s))
                    pe.wait_ge(*out_ring.space(tag, i))
                    for g in range(INNER // P):
                        mm = pe.transpose(out_ring.bank(tag)[:, g * P:(g + 1) * P], o[:, g * P:(g + 1) * P], ident[:, :])
                    mm.then_inc(out_ring.full(tag), 1)

                def project(i, s):
                    tag = f"wo{s}"
                    pe.wait_ge(*out_ring.space(tag, i))
                    for g in range(INNER // P):
                        mm = pe.matmul(out_ring.bank(tag)[:, 0:C], oT[:, g, :], w["wo"][:, g, :],
                                       start=g == 0, stop=g == INNER // P - 1)
                    mm.then_inc(out_ring.full(tag), 1)

                def body(i, first, last):
                    for s in range(SUBS):
                        one, two = ahead(i, s, 1, last), ahead(i, s, 2, last)
                        before = (i, s - 1) if s else None if first else (i - 1, SUBS - 1)
                        scores(i, s)
                        if one:
                            turn_qk(*one)
                        if two and s == 2:
                            turn_x(i + 1)
                        if before:
                            turn_o(*before)
                        if two and s != 2:
                            channels(*two, 0)
                        if before:
                            project(*before)
                        if two and s == 2:
                            for tag in ("xT0", "xT1"):
                                pe.wait_ge(*ring.copied(tag, i + 1))
                            channels(*two, 0)
                        if two:
                            channels(*two, 1)
                        turn_probs(i, s)
                        if two:
                            channels(*two, 2)
                        values(i, s)

                pe.wait_ge(w["loaded"], 16 * len(w["loads"]))
                pe.wait_ge(before_ready, 1)
                turn_x(0)
                for tag in ("xT0", "xT1"):
                    pe.wait_ge(*ring.copied(tag, 0))
                for n in range(3):
                    channels(0, 0, n)
                turn_qk(0, 0)
                for n in range(3):
                    channels(0, 1, n)
                staggered(pe, body)
                turn_o(NB - 1, SUBS - 1)
                project(NB - 1, SUBS - 1)

            @block.scalar
            def _(act):
                def copy(i, tag, dst, src, ring=ring):
                    act.wait_ge(*ring.data(tag, i))
                    act.copy(dst, src).then_inc(ring.free(tag), 1)

                def copy_x(i):
                    for c in range(NCH):
                        copy(i, f"xT{c}", xT[:, c, :], ring.bank(f"xT{c}")[:, :])

                def copy_q(i, s):
                    copy(i, f"tq{s}", qT[:, :, :].rearrange("p a b -> p (a b)"), ring.bank(f"tq{s}")[:, :])

                def copy_v(i, s):
                    copy(i, f"v{s}", v[:, s + 1, :], ring.bank(f"v{s}")[:, :])

                def copy_o(i, s):
                    tag = f"oT{s}"
                    copy(i, tag, oT[:, :, :].rearrange("p a b -> p (a b)"), out_ring.bank(tag)[:, :], out_ring)

                def squares(i, s):
                    for t in range(2):
                        tag = f"{'qk'[t]}{s}"
                        act.wait_ge(*ring.data(tag, i))
                        r = act.activation(junk[:, t, :], ring.bank(tag)[:, :], ACT.Square)
                    r.then_inc(squared, 1)

                def exponentials(i, s):
                    act.wait_ge(max_ready, nth(i, s))
                    for h in range(H8):
                        b, half = place(h)
                        r = act.activation(probs[:, b, half, :], wide[:, b, half * 2 * P:(half + 1) * 2 * P], ACT.Exp,
                                           bias=nm[:, h:h + 1], scale=scale[:, h:h + 1], accum_out=den[:, h:h + 1])
                    r.then_inc(probs_ready, 1)

                def keep_turned(i, s):
                    act.wait_ge(turned, nth(i, s))
                    act.copy(pT[:, 2:4, :, :].rearrange("p a b c -> p (a b c)"),
                             wide[:, 2:4, :].rearrange("p a b -> p (a b)")).then_inc(pT_act, 1)

                def body(i, first, last):
                    for s in range(SUBS):
                        one, two = ahead(i, s, 1, last), ahead(i, s, 2, last)
                        before = (i, s - 1) if s else None if first else (i - 1, SUBS - 1)
                        if one:
                            copy_q(*one)
                        if two and s == 2:
                            copy_x(i + 1)
                        if before:
                            copy_o(*before)
                        exponentials(i, s)
                        keep_turned(i, s)
                        if two:
                            squares(*two)
                            copy_v(*two)
                        if s == SUBS - 1 and not last:
                            act.copy(v[:, 0, :], v[:, SUBS, :])

                act.wait_ge(before_ready, 1)
                copy_x(0)
                squares(0, 0)
                copy_v(0, 0)
                copy_q(0, 0)
                squares(0, 1)
                copy_v(0, 1)
                staggered(act, body)
                copy_o(NB - 1, SUBS - 1)

            @block.vector
            def _(dve):
                def copy(i, tag, dst, src):
                    dve.wait_ge(*ring.data(tag, i))
                    dve.tensor_copy(dst, src).then_inc(ring.free(tag), 1)

                def rotate(i, s):
                    dve.wait_ge(squared, nth(i, s))
                    dve.tensor_reduce(ss[:, :, :], junk[:, :, :].rearrange("p t (h d) -> p t h d", h=H8), AX, ALU.add)
                    dve.drain()
                    dve.tensor_scalar(ss[:, :, :], ss[:, :, :], NORM_FLOOR, None, ALU.max).then_inc(ss_ready, 1)
                    if s == 0:
                        dve.wait_ge(turn_ready, i + 1)
                    half = D64 // 2
                    for t in range(2):
                        tag = f"{'qk'[t]}{s}"
                        dve.wait_ge(*ring.data(tag, i))
                        x = ring.bank(tag)[:, :].rearrange("p (h d) -> p h d", h=H8)
                        cos = rot[:, t, 0, :].rearrange("p (h d) -> p h d", h=H8)
                        sin = rot[:, t, 1, :].rearrange("p (h d) -> p h d", h=H8)
                        dve.tensor_tensor(cos, x, turn[:, s, 2 * t, :].unsqueeze(1).broadcast_to([P, H8, D64]), ALU.mult)
                        for a in range(2):
                            here, there = slice(a * half, (a + 1) * half), slice((1 - a) * half, (2 - a) * half)
                            r = dve.tensor_tensor(
                                sin[:, :, here], x[:, :, there],
                                turn[:, s, 2 * t + 1, here].unsqueeze(1).broadcast_to([P, H8, half]), ALU.mult)
                        r.then_inc(ring.free(tag), 1)
                    dve.drain().then_inc(parts_ready, 1)

                def maxima(i, s):
                    dve.wait_ge(scores_done, nth(i, s))
                    dve.tensor_reduce(mx[:, :].rearrange("p (pair odd) -> p odd pair", odd=2),
                                      wide[:, :, :].rearrange("p (o b) (a k) -> p o (b a) k", o=2, a=2), AX, ALU.max)
                    dve.tensor_scalar(scale[:, :], rr[:, s % 2, 0, :], QK_SCALE, None, ALU.mult)
                    dve.drain()
                    dve.scalar_tensor_tensor(out=nm[:, :], in0=mx[:, :], scalar=-1.0, in1=scale[:, :],
                                             op0=ALU.mult, op1=ALU.mult).then_inc(max_ready, 1)

                def keep_turned(i, s):
                    dve.wait_ge(turned, nth(i, s))
                    dve.tensor_copy(pT[:, 0:2, :, :].rearrange("p a b c -> p (a b c)"),
                                    wide[:, 0:2, :].rearrange("p a b -> p (a b)")).then_inc(pT_dve, 1)
                    dve.reciprocal(rden[:, :], den[:, :])
                    dve.drain()

                def outputs(i, s):
                    tag = f"pv{s}"
                    dve.wait_ge(*out_ring.data(tag, i))
                    dve.tensor_tensor(o[:, :].rearrange("p (h d) -> p h d", h=H8),
                                      out_ring.bank(tag)[:, :].rearrange("p (h d) -> p h d", h=H8),
                                      rden[:, :].unsqueeze(2).broadcast_to([P, H8, D64]), ALU.mult)\
                       .then_inc(out_ring.free(tag), 1)
                    dve.drain().then_inc(o_ready, 1)

                def keys(i, s):
                    tag = f"tk{s}"
                    copy(i, tag, kT[:, :, s + 1, :], ring.bank(tag)[:, :].rearrange("p (a b) -> p a b", a=H8 // 2))

                def add(i, s):
                    if s == 0:
                        dve.wait_ge(res_loaded, 16 * (i + 1))
                        dve.wait_ge(stored, 16 * (i + 1))
                    tag = f"wo{s}"
                    dve.wait_ge(*out_ring.data(tag, i))
                    dve.tensor_tensor(xout[:, s, :], out_ring.bank(tag)[:, 0:C], xres[:, s, :], ALU.add)\
                       .then_inc(out_ring.free(tag), 1)
                    if s == SUBS - 1:
                        dve.drain().then_inc(xout_ready, 1)

                def body(i, first, last):
                    for s in range(SUBS):
                        one, two = ahead(i, s, 1, last), ahead(i, s, 2, last)
                        before = (i, s - 1) if s else None if first else (i - 1, SUBS - 1)
                        maxima(i, s)
                        if s == 0:
                            dve.tensor_copy(mask[:, 1, :, :], mask[:, 0, :, :]).then_inc(mask_ready, 1)
                        if s == SUBS - 1 and not last:
                            dve.tensor_copy(kT[:, :, 0, :], kT[:, :, SUBS, :])
                        if one:
                            keys(*one)
                        if before:
                            add(*before)
                        keep_turned(i, s)
                        if two:
                            rotate(*two)
                        outputs(i, s)

                dve.wait_ge(setup_loaded, 16)
                dve.wait_ge(before_ready, 1)
                for n in range(2):
                    r = dve.tensor_copy(mask[:, n, :, :], maskf[:, n, :].unsqueeze(1).broadcast_to([P, 2, 2 * P]))
                r.then_inc(mask_ready, 1)
                rotate(0, 0)
                keys(0, 0)
                rotate(0, 1)
                staggered(dve, body)
                add(NB - 1, SUBS - 1)


def local_ffn(nc, buffers, sem, banks, wide, shared, t_in, scratch, w, src, dst):
    ctx = ExitStack()
    with ctx:
        sb = buffers(ctx, "f_")
        ident, neghalf = shared["ident"], shared["neghalf"]
        xin = sb("xin", [P, SUBS, C])
        st = sb("st", [P, SUBS, 6])
        mv = sb("mv", [P, SUBS, 2])
        rs = sb("rs", [P, SUBS])
        xn = sb("xn", [P, SUBS, C])
        xT = sb("xT", [P, NCH, BT])
        xres = sb("xres", [P, SUBS, C])
        xb = sb("xb", [P, SUBS, C])
        xout = sb("xout", [P, SUBS, C])
        gate = sb("gate", [P, 2, BT])
        u = sb("u", [P, HCH, BT])

        order = ["xT0", "xT1"]
        for m in range(HCH):
            order += [f"g{m}", f"a{m}"]
        order += [f"y{s}" for s in range(SUBS)]
        ring = Ring(banks, sem, order)
        rows = [min(P, HID - m * P) for m in range(HCH)]

        x_loaded, res_loaded, stored = sem("x_loaded"), sem("res_loaded"), sem("stored")
        stats_ready, rs_ready, xn_ready = sem("stats_ready"), sem("rs_ready"), sem("xn_ready")
        xb_ready, gate_ready, xout_ready = sem("xb_ready"), sem("gate_ready"), sem("xout_ready")

        with nc.Block() as block:

            @block.sync
            def _(sp):
                def load(i):
                    shifted_loads(sp, xin, scratch[src], i, x_loaded)

                def load_res(i):
                    sp.dma_start(xres[:, :, :], token_rows(scratch[src], i, 1)).then_inc(res_loaded, 16)

                ring.open(sp)
                sp.sem_inc(stored, 16)
                load(0)
                load_res(0)

                def body(i, more):
                    if more:
                        sp.wait_ge(xn_ready, i + 1)
                        load(i + 1)
                        sp.wait_ge(xb_ready, i + 1)
                        load_res(i + 1)
                    sp.wait_ge(xout_ready, i + 1)
                    rows_out = token_rows(scratch[dst], i, int(dst in PADDED))
                    sp.dma_start(rows_out, xout[:, :, :]).then_inc(stored, 16)

                blocks_loop(sp, body)
                sp.wait_ge(stored, 16 * (NB + 1))

            @block.gpsimd
            def _(pool):
                def front(i):
                    pool.wait_ge(stats_ready, i + 1)
                    inverse_root(pool, rs[:, :], mv[:, :, 1], shared["eps_ln"][:, :], neghalf[:, 0:SUBS]).then_inc(rs_ready, 1)

                def body(i, more):
                    pool.wait_ge(res_loaded, 16 * (i + 1))
                    pool.tensor_tensor(xb[:, :, :], xres[:, :, :], w["b2"][:, :].unsqueeze(1).broadcast_to([P, SUBS, C]),
                                       ALU.add).then_inc(xb_ready, 1)
                    if more:
                        front(i + 1)
                        pool.wait_ge(xout_ready, i + 1)

                front(0)
                pool.wait_ge(w["loaded"], 16 * len(w["loads"]))
                blocks_loop(pool, body)

            @block.tensor
            def _(pe):
                def body(i, more):
                    pe.wait_ge(xn_ready, i + 1)
                    turn_block(pe, ring, ("xT0", "xT1"), i, xn, ident)
                    for tag in ("xT0", "xT1"):
                        pe.wait_ge(*ring.copied(tag, i))
                    for m, r in enumerate(rows):
                        for tag, first in ((f"g{m}", HID + m * P), (f"a{m}", m * P)):
                            pe.wait_ge(*ring.space(tag, i))
                            for c in range(NCH):
                                mm = pe.matmul(ring.bank(tag)[0:r, :], w["w1"][:, c, first:first + r], xT[:, c, :],
                                               start=c == 0, stop=c == NCH - 1)
                            mm.then_inc(ring.full(tag), 1)
                    for s in range(SUBS):
                        pe.wait_ge(*ring.space(f"y{s}", i))
                        for m, r in enumerate(rows):
                            if s == 0:
                                pe.wait_ge(*ring.copied(f"a{m}", i))
                            mm = pe.matmul(ring.bank(f"y{s}")[:, 0:C], u[0:r, m, s * P:(s + 1) * P], w["w2"][0:r, m, :],
                                           start=m == 0, stop=m == HCH - 1)
                        mm.then_inc(ring.full(f"y{s}"), 1)

                pe.wait_ge(w["loaded"], 16 * len(w["loads"]))
                blocks_loop(pe, body)

            @block.scalar
            def _(act):
                def body(i, more):
                    for c in range(NCH):
                        tag = f"xT{c}"
                        act.wait_ge(*ring.data(tag, i))
                        act.activation(xT[:, c, :], ring.bank(tag)[:, :], ACT.Identity, bias=w["lb"][:, c:c + 1],
                                       scale=w["lg"][:, c:c + 1]).then_inc(ring.free(tag), 1)
                    for m, r in enumerate(rows):
                        tag = f"g{m}"
                        if m >= 2:
                            act.wait_ge(*ring.copied(f"a{m - 2}", i))
                        act.wait_ge(*ring.data(tag, i))
                        act.activation(gate[0:r, m % 2, :], ring.bank(tag)[0:r, :], ACT.Gelu,
                                       bias=w["b1"][0:r, 1, m:m + 1]).then_inc(ring.free(tag), 1)

                act.wait_ge(w["loaded"], 16 * len(w["loads"]))
                blocks_loop(act, body)

            @block.vector
            def _(dve):
                def front_stats(i):
                    dve.wait_ge(x_loaded, 32 * (i + 1))
                    row_stats(dve, xin, st, mv).then_inc(stats_ready, 1)

                def front_norm(i):
                    dve.wait_ge(rs_ready, i + 1)
                    normalise(dve, xn, xin, mv, rs).then_inc(xn_ready, 1)

                def body(i, more):
                    for m, r in enumerate(rows):
                        dve.wait_ge(*ring.copied(f"g{m}", i))
                        dve.wait_ge(*ring.data(f"a{m}", i))
                        dve.scalar_tensor_tensor(out=u[0:r, m, :], in0=ring.bank(f"a{m}")[0:r, :],
                                                 scalar=w["b1"][0:r, 0, m:m + 1], in1=gate[0:r, m % 2, :],
                                                 op0=ALU.add, op1=ALU.mult).then_inc(ring.free(f"a{m}"), 1)
                        if more and m == 1:
                            front_stats(i + 1)
                        if more and m == 3:
                            front_norm(i + 1)
                    dve.wait_ge(xb_ready, i + 1)
                    dve.wait_ge(stored, 16 * (i + 1))
                    for s in range(SUBS):
                        dve.wait_ge(*ring.data(f"y{s}", i))
                        dve.tensor_tensor(xout[:, s, :], ring.bank(f"y{s}")[:, 0:C], xb[:, s, :], ALU.add)\
                           .then_inc(ring.free(f"y{s}"), 1)
                    dve.drain().then_inc(xout_ready, 1)

                dve.wait_ge(w["loaded"], 16 * len(w["loads"]))
                front_stats(0)
                front_norm(0)
                blocks_loop(dve, body)


POOL_D = 6


def linear_stage(nc, buffers, sem, banks, wide, shared, t_in, scratch, w, spare, out):
    ctx = ExitStack()
    with ctx:
        sb = buffers(ctx, "l_")
        ident, neghalf, eps = shared["ident"], shared["neghalf"], shared["eps_ln"]
        xin = sb("xin", [P, SUBS, C])
        st = sb("st", [P, SUBS, 6])
        mv = sb("mv", [P, SUBS, 2])
        rs = sb("rs", [P, SUBS])
        xn = sb("xn", [P, SUBS, C])
        xT = sb("xT", [P, NCH, BT])
        xb = sb("xb", [P, SUBS, C])
        x1, xl = spare
        base = sb("base", [P, C])
        z = sb("z", [P, 2 * C])
        neg = sb("neg", [P, 2 * C])
        ez = sb("ez", [P, 2 * C])
        f = sb("f", [P, 2, 2, C])
        v = sb("v", [P, 2, C])
        prod = sb("prod", [P, 2, D16, D16, H16])
        prod2 = sb("prod2", [P, D16, H16, D16])
        kv = sb("kv", [P, D16, D16])
        ksum = sb("ksum", [P, D16])
        dprod = sb("dprod", [P, H16, D16])
        den = sb("den", [P, 2, H16])
        y = sb("y", [P, C])
        yT = sb("yT", [P, NCH, P])
        x2 = sb("x2", [P, SUBS, C])
        st2 = sb("st2", [P, 6])
        mv2 = sb("mv2", [P, 2])
        rs2 = sb("rs2", [P, 1])
        xn2 = sb("xn2", [P, C])
        x2T = sb("x2T", [P, NCH, BT])
        hT = sb("hT", [P, MLP // P, 2 * P])
        rest = sb("rest", [P, SUBS, C])
        total = sb("total", [P, SUBS, C])

        order = []
        for s in range(SUBS):
            old, later = (s - 1) % SUBS, (s + 2) % SUBS
            order += [f"yT{old}"] + (["xT0", "xT1"] if s == 2 else [])
            order += [f"qk{later}", f"v{later}", f"wo{old}", f"num{s}", f"x2T{old}"]
        ring = Ring(banks, sem, order)
        mlp_order = []
        for pair in range(2):
            mlp_order += [f"h{pair}_{m}" for m in range(MLP // P)] + [f"p{2 * pair + k}" for k in range(2)]
        mlp_ring = Ring([wide[:, b, :] for b in range(4)], lambda name: sem("mlp_" + name), mlp_order)

        x_loaded, rest_loaded, stored = sem("x_loaded"), sem("rest_loaded"), sem("stored")
        stats_ready, rs_ready, xn_ready = sem("stats_ready"), sem("rs_ready"), sem("xn_ready")
        xb_ready, rest_ready, total_ready = sem("xb_ready"), sem("rest_ready"), sem("total_ready")
        z_ready, elu_ready, f_ready = sem("z_ready"), sem("elu_ready"), sem("f_ready")
        prod_pool, kv_ready = sem("prod_pool"), sem("kv_ready")
        prod2_pool, prod2_vector, y_ready = sem("prod2_pool"), sem("prod2_vector"), sem("y_ready")
        stats2_ready, rs2_ready, xn2_ready = sem("stats2_ready"), sem("rs2_ready"), sem("xn2_ready")

        def pipeline(eng, slot):
            def run(r, before, here, after):
                for s in range(SUBS):
                    def at(k, s=s):
                        turn, sub = divmod(s + k, SUBS)
                        return (r + turn, sub) if (before, here, after)[turn + 1] else None
                    slot(r, s, before, here, after, at)
            run(-1, False, False, True)
            run(0, False, True, True)
            with eng.Fori(1, NB - 1) as r:
                run(r, True, True, True)
            run(NB - 1, True, True, False)
            run(NB, True, False, False)

        def mlp_part(r, s, before, here):
            if s == SUBS - 1:
                return (r, 0, "in") if here else None
            return (r - 1, (0, 1, 1)[s], ("out", "in", "out")[s]) if before else None

        shape = [P, D16, D16, D16]

        def fkv(eng, s, lo, hi):
            fk = f[:, s % 2, 1, :].rearrange("p (h d) -> p d h", h=H16).unsqueeze(2).broadcast_to(shape)
            vt = v[:, s % 2, :].rearrange("p (h e) -> p e h", h=H16).unsqueeze(1).broadcast_to(shape)
            return eng.tensor_tensor(prod[:, s % 2, lo:hi], fk[:, lo:hi], vt[:, lo:hi], ALU.mult)

        def fqkv(eng, s, lo, hi):
            fq = f[:, s % 2, 0, :].rearrange("p (h d) -> p d h", h=H16).unsqueeze(3).broadcast_to(shape)
            kvs = kv[:, :, :].unsqueeze(2).broadcast_to(shape)
            return eng.tensor_tensor(prod2[:, lo:hi], fq[:, lo:hi], kvs[:, lo:hi], ALU.mult)

        with nc.Block() as block:

            @block.sync
            def _(sp):
                def load_x(b):
                    sp.dma_start(xin[:, :, :], token_rows(scratch["xn1"], b, 1)).then_inc(x_loaded, 16)

                def load_rest(b):
                    sp.dma_start(x1[:, :, :], token_rows(scratch["x1"], b)).then_inc(rest_loaded, 16)
                    sp.dma_start(xl[:, :, :], token_rows(scratch["xl2"], b)).then_inc(rest_loaded, 16)

                ring.open(sp)
                mlp_ring.open(sp)
                sp.sem_inc(stored, 16)
                load_x(0)
                load_rest(0)

                def slot(r, s, before, here, after, at):
                    if s == 0 and here and after:
                        sp.wait_ge(xn_ready, r + 1)
                        sp.wait_ge(xb_ready, r + 1)
                        load_x(r + 1)
                    if s == 1 and before and here:
                        sp.wait_ge(rest_ready, nth(r - 1, SUBS - 1))
                        load_rest(r)
                    if s == 3 and before:
                        sp.wait_ge(total_ready, r)
                        sp.dma_start(token_rows(out, r - 1), total[:, :, :]).then_inc(stored, 16)

                pipeline(sp, slot)
                sp.wait_ge(stored, 16 * (NB + 1))

            @block.gpsimd
            def _(pool):
                def slot(r, s, before, here, after, at):
                    old, cur, nxt = at(-1), at(0), at(1)
                    if nxt:
                        pool.wait_ge(f_ready, nth(*nxt))
                        fkv(pool, nxt[1], D16 - POOL_D, D16).then_inc(prod_pool, 1)
                    if cur:
                        pool.wait_ge(kv_ready, nth(*cur))
                        fqkv(pool, s, D16 - POOL_D, D16).then_inc(prod2_pool, 1)
                    if old:
                        pool.wait_ge(stats2_ready, nth(*old))
                        inverse_root(pool, rs2[:, :], mv2[:, 1:2], eps[:, 0:1], neghalf[:, 0:1]).then_inc(rs2_ready, 1)
                    if s == 0 and here:
                        bias = w["bo"][:, :].unsqueeze(1).broadcast_to([P, SUBS, C])
                        pool.tensor_tensor(xb[:, :, :], xin[:, :, :], bias, ALU.add).then_inc(xb_ready, 1)
                    if s == 1 and after:
                        pool.wait_ge(stats_ready, r + 2)
                        inverse_root(pool, rs[:, :], mv[:, :, 1], eps[:, :], neghalf[:, 0:SUBS]).then_inc(rs_ready, 1)
                    if old:
                        b, o = old
                        if o == 0:
                            pool.wait_ge(rest_loaded, 32 * (b + 1))
                        pool.tensor_tensor(base[:, :], x1[:, o, :], xl[:, o, :], ALU.add)
                        pool.drain()
                        pool.tensor_tensor(base[:, :], base[:, :], w["projb"][:, :], ALU.add)
                        pool.drain()
                        pool.tensor_tensor(rest[:, o, :], base[:, :], x2[:, o, :], ALU.add).then_inc(rest_ready, 1)
                        pool.drain()

                pool.wait_ge(w["loaded"], 16 * len(w["loads"]))
                pipeline(pool, slot)

            @block.tensor
            def _(pe):
                def turn(use, tag, x):
                    pe.wait_ge(*ring.space(tag, use))
                    for c in range(NCH):
                        mm = pe.transpose(ring.bank(tag)[:, c * P:(c + 1) * P], x[:, c * P:(c + 1) * P], ident[:, :])
                    mm.then_inc(ring.full(tag), 1)

                def skip(use, *tags):
                    for tag in tags:
                        pe.wait_ge(*ring.space(tag, use))
                        pe.sem_inc(ring.full(tag), 1)
                        pe.sem_inc(ring.free(tag), 1)

                def mlp(part, use, half):
                    i, pair, layer = part
                    if layer == "in":
                        if half == 0:
                            pe.wait_ge(*ring.copied(f"x2T{2 * pair + 1}", use))
                        for m in range(half * MLP // P // 2, (half + 1) * MLP // P // 2):
                            tag = f"h{pair}_{m}"
                            pe.wait_ge(*mlp_ring.space(tag, i))
                            for c in range(NCH):
                                mm = pe.matmul(mlp_ring.bank(tag)[:, 0:2 * P], w["fc"][:, c, m * P:(m + 1) * P],
                                               x2T[:, c, pair * 2 * P:(pair + 1) * 2 * P],
                                               start=c == 0, stop=c == NCH - 1)
                            mm.then_inc(mlp_ring.full(tag), 1)
                    else:
                        tag = f"p{2 * pair + half}"
                        pe.wait_ge(*mlp_ring.space(tag, i))
                        for m in range(MLP // P):
                            if half == 0:
                                pe.wait_ge(*mlp_ring.copied(f"h{pair}_{m}", i))
                            mm = pe.matmul(mlp_ring.bank(tag)[:, 0:C], hT[:, m, half * P:(half + 1) * P],
                                           w["proj"][:, m, :], start=m == 0, stop=m == MLP // P - 1)
                        mm.then_inc(mlp_ring.full(tag), 1)

                def slot(r, s, before, here, after, at):
                    old, cur, later, use = at(-1), at(0), at(2), r + 1
                    part = mlp_part(r, s, before, here)
                    o, n = (s - 1) % SUBS, (s + 2) % SUBS
                    if old:
                        pe.wait_ge(y_ready, nth(*old))
                        turn(use, f"yT{o}", y)
                    else:
                        skip(use, f"yT{o}")
                    if s == 2 and after:
                        pe.wait_ge(xn_ready, r + 2)
                        turn_block(pe, ring, ("xT0", "xT1"), use, xn, ident)
                        for tag in ("xT0", "xT1"):
                            pe.wait_ge(*ring.copied(tag, use))
                    elif s == 2:
                        skip(use, "xT0", "xT1")
                    if later:
                        for tag, lo, hi in ((f"qk{n}", 0, 2 * C), (f"v{n}", 2 * C, 3 * C)):
                            pe.wait_ge(*ring.space(tag, use))
                            for c in range(NCH):
                                mm = pe.matmul(ring.bank(tag)[:, 0:hi - lo], xT[:, c, n * P:(n + 1) * P],
                                               w["wqkv"][:, c, lo:hi], start=c == 0, stop=c == NCH - 1)
                            mm.then_inc(ring.full(tag), 1)
                    else:
                        skip(use, f"qk{n}", f"v{n}")
                    if old:
                        pe.wait_ge(*ring.space(f"wo{o}", use))
                        pe.wait_ge(*ring.copied(f"yT{o}", use))
                        for c in range(NCH):
                            mm = pe.matmul(ring.bank(f"wo{o}")[:, 0:C], yT[:, c, :], w["wo"][:, c, :],
                                           start=c == 0, stop=c == NCH - 1)
                        mm.then_inc(ring.full(f"wo{o}"), 1)
                    else:
                        skip(use, f"wo{o}")
                    if part:
                        mlp(part, use, 0)
                    if cur:
                        tag = f"num{s}"
                        pe.wait_ge(*ring.space(tag, use))
                        pe.wait_ge(prod2_vector, nth(*cur))
                        for d in range(D16):
                            if d == D16 - POOL_D:
                                pe.wait_ge(prod2_pool, nth(*cur))
                            mm = pe.matmul(ring.bank(tag)[:, 0:C], ident[:, :],
                                           prod2[:, d, :, :].rearrange("p h e -> p (h e)"), start=d == 0, stop=d == D16 - 1)
                        mm.then_inc(ring.full(tag), 1)
                    else:
                        skip(use, f"num{s}")
                    if part:
                        mlp(part, use, 1)
                    if old:
                        pe.wait_ge(xn2_ready, nth(*old))
                        turn(use, f"x2T{o}", xn2)
                    else:
                        skip(use, f"x2T{o}")

                pe.wait_ge(w["loaded"], 16 * len(w["loads"]))
                pipeline(pe, slot)

            @block.scalar
            def _(act):
                def gelu(part, half):
                    i, pair, layer = part
                    if layer == "in":
                        for m in range(half * MLP // P // 2, (half + 1) * MLP // P // 2):
                            tag = f"h{pair}_{m}"
                            act.wait_ge(*mlp_ring.data(tag, i))
                            act.activation(hT[:, m, :], mlp_ring.bank(tag)[:, 0:2 * P], ACT.Gelu,
                                           bias=w["fcb"][:, m:m + 1]).then_inc(mlp_ring.free(tag), 1)

                def slot(r, s, before, here, after, at):
                    old, later, use = at(-1), at(2), r + 1
                    part = mlp_part(r, s, before, here)
                    o = (s - 1) % SUBS
                    if old:
                        tag = f"yT{o}"
                        act.wait_ge(*ring.data(tag, use))
                        act.copy(yT[:, :, :].rearrange("p a b -> p (a b)"), ring.bank(tag)[:, 0:C])\
                           .then_inc(ring.free(tag), 1)
                    if s == 2 and after:
                        for c in range(NCH):
                            tag = f"xT{c}"
                            act.wait_ge(*ring.data(tag, use))
                            act.activation(xT[:, c, :], ring.bank(tag)[:, :], ACT.Identity, bias=w["o1"][:, c:c + 1],
                                           scale=w["g1"][:, c:c + 1]).then_inc(ring.free(tag), 1)
                    if part:
                        gelu(part, 0)
                    if later:
                        act.wait_ge(z_ready, nth(*later))
                        act.activation(neg[:, :], z[:, :], ACT.Relu, scale=-1.0)
                        act.drain()
                        act.activation(ez[:, :], neg[:, :], ACT.Exp, scale=-1.0).then_inc(elu_ready, 1)
                    if part:
                        gelu(part, 1)
                    if old:
                        tag = f"x2T{o}"
                        act.wait_ge(*ring.data(tag, use))
                        for c in range(NCH):
                            a = act.activation(x2T[:, c, o * P:(o + 1) * P], ring.bank(tag)[:, c * P:(c + 1) * P],
                                               ACT.Identity, bias=w["o2"][:, c:c + 1], scale=w["g2"][:, c:c + 1])
                        a.then_inc(ring.free(tag), 1)

                act.wait_ge(w["loaded"], 16 * len(w["loads"]))
                pipeline(act, slot)

            @block.vector
            def _(dve):
                def weigh(b, s):
                    tag = f"num{s}"
                    dve.wait_ge(*ring.data(tag, b + 1))
                    dve.tensor_tensor(y[:, :].rearrange("p (h e) -> p h e", h=H16),
                                      ring.bank(tag)[:, 0:C].rearrange("p (h e) -> p h e", h=H16),
                                      den[:, s % 2, :].unsqueeze(2).broadcast_to([P, H16, D16]), ALU.mult)\
                       .then_inc(ring.free(tag), 1)
                    dve.drain().then_inc(y_ready, 1)

                def features(b, s):
                    fs, d = f[:, s % 2, :, :], den[:, s % 2, :]
                    dve.wait_ge(elu_ready, nth(b, s))
                    dve.scalar_tensor_tensor(fs.rearrange("p a b -> p (a b)"), z[:, :], 0.0, ez[:, :], ALU.max, ALU.add)
                    dve.drain().then_inc(f_ready, 1)
                    dve.tensor_reduce(ksum[:, :], fs[:, 1, :].rearrange("p (h d) -> p d h", h=H16), AX, ALU.add)
                    dve.drain()
                    dve.tensor_tensor(dprod[:, :, :], fs[:, 0, :].rearrange("p (h d) -> p h d", h=H16),
                                      ksum[:, :].unsqueeze(1).broadcast_to([P, H16, D16]), ALU.mult)
                    dve.drain()
                    dve.tensor_reduce(d, dprod[:, :, :], AX, ALU.add)
                    dve.drain()
                    dve.tensor_scalar(d, d, 1e-6, None, ALU.add)
                    dve.drain()
                    dve.reciprocal(d, d)

                def project_in(use, b, s):
                    dve.wait_ge(*ring.data(f"qk{s}", use))
                    dve.tensor_tensor(z[:, :], ring.bank(f"qk{s}")[:, :], w["bqkv"][:, 0:2 * C], ALU.add)\
                       .then_inc(ring.free(f"qk{s}"), 1)
                    dve.wait_ge(*ring.data(f"v{s}", use))
                    dve.tensor_tensor(v[:, s % 2, :], ring.bank(f"v{s}")[:, 0:C], w["bqkv"][:, 2 * C:3 * C], ALU.add)\
                       .then_inc(ring.free(f"v{s}"), 1)
                    dve.drain().then_inc(z_ready, 1)

                def add(i, s):
                    if s == 0:
                        dve.wait_ge(stored, 16 * (i + 1))
                    dve.wait_ge(rest_ready, nth(i, s))
                    dve.wait_ge(*mlp_ring.data(f"p{s}", i))
                    dve.tensor_tensor(total[:, s, :], mlp_ring.bank(f"p{s}")[:, 0:C], rest[:, s, :], ALU.add)\
                       .then_inc(mlp_ring.free(f"p{s}"), 1)

                def slot(r, s, before, here, after, at):
                    old, cur, nxt, later, use = at(-1), at(0), at(1), at(2), r + 1
                    if old:
                        weigh(*old)
                    if nxt:
                        features(*nxt)
                    if s == 1 and before:
                        add(r - 1, 0)
                        add(r - 1, 1)
                    if s == 3 and before:
                        add(r - 1, 2)
                        add(r - 1, 3)
                        dve.drain().then_inc(total_ready, 1)
                    if cur:
                        dve.wait_ge(prod_pool, nth(*cur))
                        dve.tensor_reduce(kv[:, :, :].rearrange("p a b -> p (a b)"),
                                          prod[:, s % 2].rearrange("p d e h -> p (d e) h"), AX, ALU.add)
                        dve.drain().then_inc(kv_ready, 1)
                        fqkv(dve, s, 0, D16 - POOL_D).then_inc(prod2_vector, 1)
                    if later:
                        project_in(use, *later)
                    if s == 1 and after:
                        dve.wait_ge(x_loaded, 16 * (r + 2))
                        row_stats(dve, xin, st, mv).then_inc(stats_ready, 1)
                    if old:
                        o = old[1]
                        if o == 0:
                            dve.wait_ge(xb_ready, old[0] + 1)
                        dve.wait_ge(*ring.data(f"wo{o}", use))
                        dve.tensor_tensor(x2[:, o, :], ring.bank(f"wo{o}")[:, 0:C], xb[:, o, :], ALU.add)\
                           .then_inc(ring.free(f"wo{o}"), 1)
                        dve.drain()
                        dve.bn_stats(st2[:, :], x2[:, o, :])
                        dve.drain()
                        dve.bn_aggr(mv2[:, :], st2[:, :]).then_inc(stats2_ready, 1)
                    if nxt:
                        fkv(dve, nxt[1], 0, D16 - POOL_D)
                    if old:
                        dve.wait_ge(rs2_ready, nth(*old))
                        dve.tensor_scalar(xn2[:, :], x2[:, old[1], :], mv2[:, 0:1], rs2[:, 0:1], ALU.subtract, ALU.mult)\
                           .then_inc(xn2_ready, 1)
                    if s == 1 and after:
                        dve.wait_ge(rs_ready, r + 2)
                        normalise(dve, xn, xin, mv, rs).then_inc(xn_ready, 1)
                    dve.drain()

                dve.wait_ge(w["loaded"], 16 * len(w["loads"]))
                pipeline(dve, slot)


_INS = ['L0_attn_x', 'L0_attn_w_qkv', 'L0_attn_ln_w', 'L0_attn_w_proj', 'L0_ffn_gate_w', 'L0_ffn_gate_b', 'L0_ffn_w1',
        'L0_ffn_b1', 'L0_ffn_w2', 'L0_ffn_b2', 'L1_attn_ln1_w', 'L1_attn_ln1_b', 'L1_attn_wq', 'L1_attn_bq',
        'L1_attn_wk', 'L1_attn_bk', 'L1_attn_wv', 'L1_attn_bv', 'L1_attn_wo', 'L1_attn_bo', 'L1_attn_ln2_w',
        'L1_attn_ln2_b', 'L1_attn_fc_w', 'L1_attn_fc_b', 'L1_attn_proj_w', 'L1_attn_proj_b', 'L1_ffn_wqkv',
        'L1_ffn_q_scale', 'L1_ffn_k_scale', 'L1_ffn_wo', 'L1_ffn_ln_g', 'L1_ffn_ln_b', 'L1_ffn_w1', 'L1_ffn_b1',
        'L1_ffn_w2', 'L1_ffn_b2']


def shape_constants():
    import numpy as np

    masked = np.float32(-1e30)
    q, k = np.arange(P)[:, None], np.arange(P)[None, :]
    group = 64
    local = np.concatenate([q <= k, k <= q], axis=1)
    first = np.concatenate([np.zeros((P, P), bool), k <= q], axis=1)
    half = np.arange(0, D64, 2, dtype=np.float32)
    freq = (np.float32(1.0) / np.float32(10000.0) ** (half / np.float32(D64))).astype(np.float32)
    t = np.arange(NT, dtype=np.float32)
    angle = (t[:, None] * freq[None, :]).astype(np.float32)
    base = ((half + np.float32(0.4 * D64)) / np.float32(1.4 * D64)).astype(np.float32)
    power = ((t - NT // 2) / np.float32(P // 2)).astype(np.float32)
    scale = (base[None, :] ** power[:, None]).astype(np.float32)
    cos, sin = np.cos(angle), np.sin(angle)
    return {
        "k_ident": np.eye(P, dtype=np.float32),
        "k_iota": np.arange(NE, dtype=np.float32),
        "k_mask_group": np.where((k <= q) & (k // group == q // group), np.float32(0), masked),
        "k_mask_local": np.stack([np.where(m, np.float32(0), masked) for m in (local, first)], axis=1),
        "k_rotary": np.stack([cos * scale, sin * scale, cos / scale, sin / scale], axis=1).astype(np.float32),
    }


def kernel(**inputs):
    import numpy as _np
    import concourse.bacc as _bacc
    from concourse.bass_utils import run_bass_kernel_spmd as _run

    nc = _bacc.Bacc("TRN2", target_bir_lowering=False, num_devices=1)
    arrays, t_in = {}, {}
    for name in _INS:
        a = _np.ascontiguousarray(inputs[name])
        if name == 'L0_attn_x':
            name, a = 'x', a.reshape(NT, C)
        arrays[f"in_{name}"] = a
        t_in[name] = nc.dram_tensor(f"in_{name}", a.shape, mybir.dt.from_np(a.dtype), kind="ExternalInput").ap()
    for name, a in shape_constants().items():
        arrays[name] = a
        t_in[name] = nc.dram_tensor(name, a.shape, F32, kind="ExternalInput").ap()
    out = nc.dram_tensor("out_0_dram", (1, NT, C), F32, kind="ExternalOutput").ap()
    scratch = {name: nc.dram_tensor(f"s_{name}", (NT + (name in PADDED), C), F32).ap()
               for name in ("x1", "xl2") + PADDED}
    build(nc, t_in, out[0], scratch)
    r = _run(nc, [arrays], core_ids=[0])
    return r.results[0]["out_0_dram"]
```

```python
from contextlib import ExitStack

import concourse.bass as bass
from concourse import mybir

F32 = mybir.dt.float32
BF16 = mybir.dt.bfloat16
F32R = mybir.dt.float32r
U32 = mybir.dt.uint32
ALU = mybir.AluOpType
ACT = mybir.ActivationFunctionType
AX = mybir.AxisListType.X

P = 128
C = 256
NCH = C // P
NT = 4096
SUBS = 4
BT = SUBS * P
NB = NT // BT
H16, D16 = 16, 16
NE, ED = 8, 256
MLP = 1024
H8, D64 = 8, 64
INNER = D64 * H8
HID = 682
HCH = (HID + P - 1) // P
EPS_LN, EPS_RMS = 1e-5, 1e-6
NORM_FLOOR = 1e-24
QK_SCALE = 8.0
PADDED = ("xn1", "xm0", "xl1", "xm1")


class Ring:

    def __init__(self, banks, sem, order, early=()):
        n = len(banks)
        self.banks = banks
        self.full_sems = [sem(f"bank{b}_full") for b in range(n)]
        self.free_sems = [sem(f"bank{b}_free") for b in range(n)]
        self.at = {tag: (u % n, u // n) for u, tag in enumerate(order)}
        self.late = {tag: int(bool(early) and tag not in early) for tag in order}
        self.per = [len(range(b, len(order), n)) for b in range(n)]

    def bank(self, tag):
        return self.banks[self.at[tag][0]]

    def full(self, tag):
        return self.full_sems[self.at[tag][0]]

    def free(self, tag):
        return self.free_sems[self.at[tag][0]]

    def space(self, tag, i):
        b, k = self.at[tag]
        return self.free_sems[b], (i + self.late[tag]) * self.per[b] + (k + 1)

    def data(self, tag, i):
        b, k = self.at[tag]
        return self.full_sems[b], (i + self.late[tag]) * self.per[b] + (k + 1)

    def copied(self, tag, i):
        b, k = self.at[tag]
        return self.free_sems[b], (i + self.late[tag]) * self.per[b] + (k + 2)

    def skip(self, pe, i, *tags):
        for tag in tags:
            pe.wait_ge(*self.space(tag, i))
            pe.sem_inc(self.full(tag), 1)
            pe.sem_inc(self.free(tag), 1)

    def open(self, eng):
        for s in self.free_sems:
            eng.sem_inc(s, 1)


def blocks_loop(eng, body):
    with eng.Fori(0, NB - 1) as i:
        body(i, True)
    body(NB - 1, False)


def peeled_loop(eng, body):
    body(0, True, True)
    with eng.Fori(1, NB - 1) as i:
        body(i, False, True)
    body(NB - 1, False, False)


def token_rows(ap, i, first=0, c0=0, c1=C):
    return ap[bass.ds(i * BT + first, BT), c0:c1].rearrange("(s p) c -> p s c", p=P)


def nth(i, s):
    return i * SUBS + (s + 1)


def split_product(pe, out, a, b, start, stop):
    pe.matmul(out, a[0], b[0], start=start, stop=False)
    pe.matmul(out, a[0], b[1], start=False, stop=False)
    return pe.matmul(out, a[1], b[0], start=False, stop=stop)


def row_stats(dve, x, st, mv):
    for s in range(SUBS):
        dve.bn_stats(st[:, s, :], x[:, s, :])
    dve.drain()
    for s in range(SUBS):
        r = dve.bn_aggr(mv[:, s, :], st[:, s, :])
    return r


def inverse_root(pool, out, x, eps, neghalf):
    pool.tensor_tensor(out, x, eps, ALU.add)
    pool.drain()
    return pool.tensor_tensor(out, out, neghalf, ALU.pow)


def normalise(dve, xn, x, mv, rs):
    for s in range(SUBS):
        r = dve.tensor_scalar(xn[:, s, :], x[:, s, :], mv[:, s, 0:1], rs[:, s:s + 1], ALU.subtract, ALU.mult)
    return r


def turn_block(pe, ring, tags, i, x, ident):
    for c, tag in enumerate(tags):
        pe.wait_ge(*ring.space(tag, i))
        for s in range(SUBS):
            mm = pe.transpose(ring.bank(tag)[:, s * P:(s + 1) * P], x[:, s, c * P:(c + 1) * P], ident[:, :])
        mm.then_inc(ring.full(tag), 1)


def chunks(ap):
    return ap.rearrange("(c p) n -> p c n", p=P)


def column(ap):
    return ap.rearrange("(c p) -> p c", p=P)


def build(nc, t_in, out, scratch):
    stack = ExitStack()
    with stack:
        def sb(name, shape, dt=F32):
            return stack.enter_context(nc.sbuf_tensor(name, shape, dt))

        semaphores = {}

        def sems(prefix):
            def sem(name):
                if prefix + name not in semaphores:
                    semaphores[prefix + name] = stack.enter_context(nc.semaphore(prefix + name))
                return semaphores[prefix + name]
            return sem

        def clear(prefixes):
            with nc.Block() as block:

                @block.gpsimd
                def _(pool):
                    for name, s in semaphores.items():
                        if name.startswith(prefixes):
                            pool.sem_clear(s)

        used = []

        def buffers(ctx, prefix):
            used.append(prefix)
            turn = f"{prefix}{used.count(prefix)}_"
            return lambda name, shape, dt=F32: ctx.enter_context(nc.sbuf_tensor(turn + name, shape, dt))

        stack.enter_context(nc.allow_non_contiguous_dma(reason="biases, a column per partition: a few KB"))
        banks = [stack.enter_context(nc.psum_tensor(f"bank{b}", [P, 512], F32)) for b in range(4)]
        wide = stack.enter_context(nc.psum_tensor("wide", [P, 4, 512], F32))
        shared = {
            "ident": sb("ident", [P, P]),
            "identb": sb("identb", [P, P], BF16),
            "neghalf": sb("neghalf", [P, 2 * H8]),
            "eps_ln": sb("eps_ln", [P, SUBS]),
            "eps_rms": sb("eps_rms", [P, 2]),
        }
        attention = [attention_weights(sb, sems("w0_"), t_in, 0)]
        load_constants(nc, sb, sems("c_"), shared, t_in, scratch)
        first_stage(nc, buffers, sems("a_"), banks, wide, shared, t_in, scratch, attention)
        attention.append(attention_weights(sb, sems("w1_"), t_in, 1))
        ffn = [ffn_weights(sb, sems(f"w{n}_"), t_in, n) for n in range(2)]
        linear = linear_weights(sb, sems("wl_"), t_in)
        for n, (src, mid, dst) in enumerate((("xn1", "xm0", "xl1"), ("xl1", "xm1", "xl2"))):
            local_attention(nc, buffers, sems("d_"), banks, wide, shared, t_in, scratch, attention[n], src, mid,
                            [ffn[0], attention[1], ffn[1], linear] if n == 0 else [])
            local_ffn(nc, buffers, sems("f_"), banks, wide, shared, t_in, scratch, ffn[n], mid, dst)
            if n == 0:
                clear(("d_", "f_"))
        linear_stage(nc, buffers, sems("l_"), banks, wide, shared, t_in, scratch, linear,
                     [layer["wo"] for layer in attention], out)


def attention_weights(sb, sem, t_in, n):
    w = {"loaded": sem("attn_loaded"), "loads": []}

    def add(name, shape, src):
        w[name] = sb(f"{name}_{n}", shape)
        if src is not None:
            w["loads"].append((w[name], src))

    add("wqkv", [P, NCH, 3 * INNER], chunks(t_in["L1_ffn_wqkv"][n]))
    add("wo", [P, INNER // P, C], chunks(t_in["L1_ffn_wo"][n]))
    for name in ("q_scale", "k_scale"):
        add(name, [P, D64], t_in[f"L1_ffn_{name}"][n].partition_broadcast(P))
        add(name + "_turned", [P, D64], None)
        for a in range(2):
            other = slice((1 - a) * D64 // 2, (2 - a) * D64 // 2)
            w["loads"].append((w[name + "_turned"][:, a * D64 // 2:(a + 1) * D64 // 2],
                               t_in[f"L1_ffn_{name}"][n, other].partition_broadcast(P)))
    return w


def ffn_weights(sb, sem, t_in, n):
    w = {"loaded": sem("ffn_loaded"), "loads": []}

    def add(name, shape, src):
        w[name] = sb(f"{name}_{n}", shape)
        if src is not None:
            w["loads"].append((w[name], src))

    full = HID // P * P
    add("w1", [P, NCH, 2 * HID], chunks(t_in["L1_ffn_w1"][n]))
    add("w2", [P, HCH, C], None)
    w["loads"].append((w["w2"][:, 0:HID // P, :], chunks(t_in["L1_ffn_w2"][n, 0:full])))
    w["loads"].append((w["w2"][0:HID - full, HID // P, :], t_in["L1_ffn_w2"][n, full:HID]))
    add("b1", [P, 2, HCH], None)
    for t in range(2):
        a = t * HID
        w["loads"].append((w["b1"][:, t, 0:HID // P], column(t_in["L1_ffn_b1"][n, a:a + full])))
        w["loads"].append((w["b1"][0:HID - full, t, HID // P:HCH],
                           t_in["L1_ffn_b1"][n, a + full:a + HID].rearrange("(p a) -> p a", a=1)))
    add("b2", [P, C], t_in["L1_ffn_b2"][n].partition_broadcast(P))
    add("lg", [P, NCH], column(t_in["L1_ffn_ln_g"][n]))
    add("lb", [P, NCH], column(t_in["L1_ffn_ln_b"][n]))
    return w


def linear_weights(sb, sem, t_in):
    w = {"loaded": sem("loaded"), "loads": []}
    w["wqkv"] = sb("l_wqkv", [P, NCH, 3 * C])
    w["bqkv"] = sb("l_bqkv", [P, 3 * C])
    for k, name in enumerate("qkv"):
        w["loads"].append((w["wqkv"][:, :, k * C:(k + 1) * C], chunks(t_in[f"L1_attn_w{name}"])))
        w["loads"].append((w["bqkv"][:, k * C:(k + 1) * C], t_in[f"L1_attn_b{name}"].partition_broadcast(P)))
    for name, shape, src in (
        ("wo", [P, NCH, C], chunks(t_in["L1_attn_wo"])),
        ("fc", [P, NCH, MLP], chunks(t_in["L1_attn_fc_w"])),
        ("proj", [P, MLP // P, C], chunks(t_in["L1_attn_proj_w"])),
        ("fcb", [P, MLP // P], column(t_in["L1_attn_fc_b"])),
        ("bo", [P, C], t_in["L1_attn_bo"].partition_broadcast(P)),
        ("projb", [P, C], t_in["L1_attn_proj_b"].partition_broadcast(P)),
        ("g1", [P, NCH], column(t_in["L1_attn_ln1_w"])),
        ("o1", [P, NCH], column(t_in["L1_attn_ln1_b"])),
        ("g2", [P, NCH], column(t_in["L1_attn_ln2_w"])),
        ("o2", [P, NCH], column(t_in["L1_attn_ln2_b"])),
    ):
        w[name] = sb("l_" + name, shape)
        w["loads"].append((w[name], src))
    return w


def whole(t):
    return t if isinstance(t, bass.AP) else t[tuple(slice(None) for _ in t.shape)]


def load_constants(nc, sb, sem, shared, t_in, scratch):
    zrow = sb("zrow", [1, C])
    loaded, zeroed, stored = sem("loaded"), sem("zeroed"), sem("stored")
    with nc.Block() as block:

        @block.sync
        def _(sp):
            sp.dma_start(shared["ident"][:, :], t_in["k_ident"]).then_inc(loaded, 16)
            sp.wait_ge(zeroed, 1)
            for name in PADDED:
                sp.dma_start(scratch[name][0:1, :], zrow[:, :]).then_inc(stored, 16)
            sp.wait_ge(stored, 16 * len(PADDED))

        @block.vector
        def _(dve):
            dve.memset(zrow[:, :], 0.0).then_inc(zeroed, 1)
            for name, value in (("neghalf", -0.5), ("eps_ln", EPS_LN), ("eps_rms", EPS_RMS)):
                dve.memset(shared[name][:, :], value)
            dve.wait_ge(loaded, 16)
            dve.tensor_copy(shared["identb"][:, :], shared["ident"][:, :])
            dve.drain()


def first_stage(nc, buffers, sem, banks, wide, shared, t_in, scratch, later):
    ctx = ExitStack()
    with ctx:
        sb = buffers(ctx, "a_")
        ident, identb, neghalf = shared["ident"], shared["identb"], shared["neghalf"]
        wqkv = sb("wqkv", [P, NCH, 3 * C])
        wproj = sb("wproj", [P, NCH, C])
        w1_high = sb("w1_high", [P, NE, NCH, ED], F32R)
        w2_high = sb("w2_high", [P, NE, ED // P, C], F32R)
        w1_low = sb("w1_low", [P, NE, NCH, ED], F32R)
        w2_low = sb("w2_low", [P, NE, ED // P, C], F32R)
        gw = sb("gw", [P, NCH, NE])
        gb = sb("gb", [P, NE])
        b1 = sb("b1", [P, NE, ED // P])
        b2 = sb("b2", [NE, C])
        lnw = sb("lnw", [P, C])
        iota = sb("iota", [P, NE])
        maskf = sb("maskf", [P, P])
        mask = sb("mask", [P, 4, P], BF16)
        xin = sb("xin", [P, SUBS, C])
        st = sb("st", [P, SUBS, 6])
        mv = sb("mv", [P, SUBS, 2])
        rs = sb("rs", [P, SUBS])
        xn = sb("xn", [P, SUBS, C])
        xT = sb("xT", [P, NCH, BT])
        xT_high = sb("xT_high", [P, NCH, BT], F32R)
        xT_low = sb("xT_low", [P, NCH, BT], F32R)
        xres = sb("xres", [P, SUBS, C])
        acc = sb("acc", [P, SUBS, C])
        st2 = sb("st2", [P, SUBS, 6])
        mv2 = sb("mv2", [P, SUBS, 2])
        rs2 = sb("rs2", [P, SUBS])
        xn1 = sb("xn1", [P, SUBS, C])
        score = sb("score", [P, SUBS, NE])
        top = sb("top", [P, SUBS, 8])
        topi = sb("topi", [P, SUBS, 8], U32)
        topf = sb("topf", [P, SUBS, 8])
        pick = sb("pick", [P, 2, SUBS, NE])
        comb = sb("comb", [P, SUBS, NE])
        combT = sb("combT", [NE, BT])
        sq = sb("sq", [P, 2, C])
        ss = sb("ss", [P, 2])
        rr = sb("rr", [P, 2])
        qk = sb("qk", [P, 2, H16, 32])
        v = sb("v", [P, 2, C])
        qkT = sb("qkT", [P, 2, 4, P])
        mx = sb("mx", [P, H16])
        nm = sb("nm", [P, H16])
        probs = sb("probs", [P, 4, 4, P])
        den = sb("den", [P, H16])
        rden = sb("rden", [P, H16])
        pT = sb("pT", [P, 4, 4, P])
        y = sb("y", [P, C])
        yT = sb("yT", [P, NCH, P])
        hT = sb("hT", [P, BT])
        hT_high = sb("hT_high", [P, 2, ED // P, BT], F32R)
        hT_low = sb("hT_low", [P, 2, ED // P, BT], F32R)

        order = ["h0_0", "h0_1", "cT", "tq0", "tk0"]
        for s in range(SUBS):
            e, last = 2 * s + 1, s == SUBS - 1
            order += [f"h{e}_0", f"h{e}_1", f"eo{e - 1}_0", f"eo{e - 1}_1"]
            order += ["xT0", "xT1", "gate"] if last else [f"qk{s + 1}", f"v{s + 1}", f"h{e + 1}_0", f"h{e + 1}_1"]
            order += [f"pv{s}", f"eo{e}_0", f"eo{e}_1"]
            order += ["qk0", "v0"] if last else [f"tq{s + 1}", f"tk{s + 1}"]
            order += [f"yT{s}", f"proj{s}"]
        assert order.index("v0") % 4 == order.index("pv0") % 4
        early = ("xT0", "xT1", "gate", "qk0", "v0")
        ring = Ring(banks, sem, order, early)

        def probs_count(i, s, j):
            return i * (4 * SUBS) + (4 * s + j + 1)

        def lows(i, e, m):
            return i * (NE * ED // P) + (e * (ED // P) + m + 2)

        w_loaded, setup_done = sem("w_loaded"), sem("setup_done")
        staged = [sem(f"staged{a}") for a in range(2)]
        w_rounded, w_split = sem("w_rounded"), sem("w_split")
        x_low_ready, h_low_ready = sem("x_low_ready"), sem("h_low_ready")
        x_loaded, res_loaded, res_used = sem("x_loaded"), sem("res_loaded"), sem("res_used")
        stats_ready, rs_ready, xn_ready = sem("stats_ready"), sem("rs_ready"), sem("xn_ready")
        comb_ready = sem("comb_ready")
        ss_ready, rr_ready = sem("ss_ready"), sem("rr_ready")
        scores_done, max_ready, probs_ready = sem("scores_done"), sem("max_ready"), sem("probs_ready")
        turned, pT_act, pT_dve = sem("turned"), sem("pT_act"), sem("pT_dve")
        y_ready = sem("y_ready")
        acc_ready, stats2_ready, rs2_ready, xn1_ready = (
            sem("acc_ready"), sem("stats2_ready"), sem("rs2_ready"), sem("xn1_ready"))
        stored = sem("stored")

        weights = (
            (gw[:, :, :], chunks(t_in["L0_ffn_gate_w"])),
            (wqkv[:, :, :], chunks(t_in["L0_attn_w_qkv"])),
            (gb[:, :], t_in["L0_ffn_gate_b"].partition_broadcast(P)),
            (lnw[:, :], t_in["L0_attn_ln_w"].partition_broadcast(P)),
            (b1[:, :, :], t_in["L0_ffn_b1"].rearrange("e (m p) -> p e m", p=P)),
            (b2[:, :], t_in["L0_ffn_b2"]),
            (iota[:, :], t_in["k_iota"].partition_broadcast(P)),
            (maskf[:, :], t_in["k_mask_group"]),
            (wproj[:, :, :], chunks(t_in["L0_attn_w_proj"])),
        )
        half = NE // 2
        expert_weights = [
            (high[:, a:a + half], low[:, a:a + half], src[a:a + half].rearrange("e (c p) n -> p e c n", p=P))
            for a in (0, half)
            for high, low, src in ((w1_high, w1_low, t_in["L0_ffn_w1"]), (w2_high, w2_low, t_in["L0_ffn_w2"]))
        ]
        stage = [t[:, :, :, :].rearrange("p a b c -> p (a b c)").rearrange("p (e c n) -> p e c n", e=half, c=NCH)
                 for t in (probs, pT)]

        with nc.Block() as block:

            @block.sync
            def _(sp):
                def load_x(i):
                    sp.dma_start(xin[:, :, :], token_rows(t_in["x"], i)).then_inc(x_loaded, 16)

                def load_res(i):
                    sp.dma_start(xres[:, :, :], token_rows(t_in["x"], i)).then_inc(res_loaded, 16)

                ring.open(sp)
                sp.sem_inc(stored, 32)
                sp.sem_inc(h_low_ready, 1)
                load_x(0)
                load_res(0)
                for dst, src in weights:
                    sp.dma_start(dst, src).then_inc(w_loaded, 16)
                for n, (high, low, src) in enumerate(expert_weights):
                    if n >= 2:
                        sp.wait_ge(w_split, n - 1)
                    sp.dma_start(stage[n % 2], src).then_inc(staged[n % 2], 16)
                for group in later:
                    for dst, src in group["loads"]:
                        sp.dma_start(whole(dst), src).then_inc(group["loaded"], 16)

                def body(i, more):
                    if more:
                        sp.wait_ge(xn_ready, i + 1)
                        load_x(i + 1)
                        sp.wait_ge(res_used, i + 1)
                        load_res(i + 1)
                    sp.wait_ge(acc_ready, i + 1)
                    sp.dma_start(token_rows(scratch["x1"], i), acc[:, :, :]).then_inc(stored, 16)
                    sp.wait_ge(xn1_ready, i + 1)
                    sp.dma_start(token_rows(scratch["xn1"], i, 1), xn1[:, :, :]).then_inc(stored, 16)

                blocks_loop(sp, body)
                sp.wait_ge(stored, 32 * (NB + 1))

            @block.gpsimd
            def _(pool):
                def front(i):
                    pool.wait_ge(stats_ready, i + 1)
                    inverse_root(pool, rs[:, :], mv[:, :, 1], shared["eps_ln"][:, :], neghalf[:, 0:SUBS]).then_inc(rs_ready, 1)

                def rms(i, s):
                    pool.wait_ge(ss_ready, nth(i, s))
                    inverse_root(pool, rr[:, :], ss[:, :], shared["eps_rms"][:, :], neghalf[:, 0:2]).then_inc(rr_ready, 1)

                def keep_low(i, e):
                    for m in range(ED // P):
                        pool.wait_ge(*ring.copied(f"h{e}_{m}", i))
                        pool.tensor_tensor(hT_low[:, e % 2, m, :], hT[:, :], hT_high[:, e % 2, m, :].bitcast(F32),
                                           ALU.subtract).then_inc(h_low_ready, 1)

                def root_of_sum(i):
                    pool.wait_ge(stats2_ready, i + 1)
                    inverse_root(pool, rs2[:, :], mv2[:, :, 1], shared["eps_ln"][:, :], neghalf[:, 0:SUBS])\
                        .then_inc(rs2_ready, 1)

                def body(i, first, more):
                    keep_low(i, 0)
                    if not first:
                        root_of_sum(i - 1)
                    for s in range(SUBS):
                        keep_low(i, 2 * s + 1)
                        if s + 1 < SUBS:
                            rms(i, s + 1)
                            keep_low(i, 2 * s + 2)
                        if more and s == 1:
                            front(i + 1)
                    if more:
                        rms(i + 1, 0)

                front(0)
                rms(0, 0)
                peeled_loop(pool, body)
                root_of_sum(NB - 1)

            @block.tensor
            def _(pe):
                def gate(i):
                    for tag in ("xT0", "xT1"):
                        pe.wait_ge(*ring.copied(tag, i))
                    pe.wait_ge(*ring.space("gate", i))
                    o = ring.bank("gate")
                    for s in range(SUBS):
                        for c in range(NCH):
                            mm = pe.matmul(o[:, s * NE:(s + 1) * NE], xT[:, c, s * P:(s + 1) * P], gw[:, c, :],
                                           start=c == 0, stop=c == NCH - 1)
                    mm.then_inc(ring.full("gate"), 1)

                def qkv(i, s):
                    for tag, a, b in ((f"qk{s}", 0, 2 * C), (f"v{s}", 2 * C, 3 * C)):
                        pe.wait_ge(*ring.space(tag, i))
                        for c in range(NCH):
                            mm = pe.matmul(ring.bank(tag)[:, 0:b - a], xT[:, c, s * P:(s + 1) * P], wqkv[:, c, a:b],
                                           start=c == 0, stop=c == NCH - 1)
                        mm.then_inc(ring.full(tag), 1)

                def turn_qk(i, s):
                    pe.wait_ge(*ring.copied(f"qk{s}", i))
                    for t, tag in enumerate((f"tq{s}", f"tk{s}")):
                        pe.wait_ge(*ring.space(tag, i))
                        for g in range(4):
                            mm = pe.transpose(ring.bank(tag)[:, g * P:(g + 1) * P],
                                              qk[:, t, 4 * g:4 * g + 4, :].rearrange("p a b -> p (a b)"), ident[:, :])
                        mm.then_inc(ring.full(tag), 1)

                def expert_in(i, e):
                    pe.wait_ge(w_split, 2 * (e // half) + 1)
                    for m in range(ED // P):
                        tag = f"h{e}_{m}"
                        pe.wait_ge(*ring.space(tag, i))
                        for c in range(NCH):
                            cols = slice(m * P, (m + 1) * P)
                            mm = split_product(pe, ring.bank(tag)[:, :],
                                               (w1_high[:, e, c, cols], w1_low[:, e, c, cols]),
                                               (xT_high[:, c, :], xT_low[:, c, :]), c == 0, c == NCH - 1)
                        mm.then_inc(ring.full(tag), 1)

                def expert_out(i, e, between=lambda n: None):
                    pe.wait_ge(w_split, 2 * (e // half) + 2)
                    pe.wait_ge(h_low_ready, lows(i, e, ED // P - 1))
                    for n in range(2):
                        tag = f"eo{e}_{n}"
                        pe.wait_ge(*ring.space(tag, i))
                        for k, s in enumerate((2 * n, 2 * n + 1)):
                            for m in range(ED // P):
                                cols = slice(s * P, (s + 1) * P)
                                mm = split_product(pe, ring.bank(tag)[:, (s % 2) * C:(s % 2 + 1) * C],
                                                   (hT_high[:, e % 2, m, cols], hT_low[:, e % 2, m, cols]),
                                                   (w2_high[:, e, m, :], w2_low[:, e, m, :]),
                                                   m == 0, m == ED // P - 1)
                                if (k, m) == (1, ED // P - 1):
                                    mm.then_inc(ring.full(tag), 1)
                                between(4 * n + 2 * k + m)

                def turn_comb(i):
                    pe.wait_ge(comb_ready, i + 1)
                    pe.wait_ge(*ring.space("cT", i))
                    for s in range(SUBS):
                        mm = pe.transpose(ring.bank("cT")[0:NE, s * P:(s + 1) * P], comb[:, s, :], ident[:, :])
                    mm.then_inc(ring.full("cT"), 1)

                def scores(i, s):
                    pe.wait_ge(*ring.copied(f"tq{s}", i))
                    pe.wait_ge(*ring.copied(f"tk{s}", i))
                    for j in range(4):
                        pe.matmul(wide[:, j, :], identb[:, :], mask[:, :, :].rearrange("p a b -> p (a b)"),
                                  start=True, stop=False)
                    for g in range(4):
                        for j in range(4):
                            r = slice(32 * j, 32 * j + D16)
                            mm = pe.matmul(wide[:, j, g * P:(g + 1) * P], qkT[r, 0, g, :], qkT[r, 1, g, :],
                                           start=False, stop=g == 3)
                    mm.then_inc(scores_done, 1)

                def turn_probs(i, s):
                    for j in range(4):
                        pe.wait_ge(probs_ready, probs_count(i, s, j))
                        for g in range(4):
                            mm = pe.transpose(wide[:, j, g * P:(g + 1) * P], probs[:, j, g, :], ident[:, :])
                    mm.then_inc(turned, 1)

                def values_and_expert(i, s, e):
                    tag = f"pv{s}"

                    def heads(n):
                        for head in range(2 * n, 2 * n + 2):
                            j, g = divmod(head, 4)
                            h = slice((4 * g + j) * D16, (4 * g + j + 1) * D16)
                            mm = pe.matmul(ring.bank(tag)[:, h], pT[:, j, g, :], v[:, s % 2, h], start=True, stop=True)
                        if n == H16 // 2 - 1:
                            mm.then_inc(ring.full(tag), 1)

                    pe.wait_ge(pT_act, nth(i, s))
                    pe.wait_ge(pT_dve, nth(i, s))
                    if s > 0:
                        pe.wait_ge(*ring.copied(f"v{s}", i))
                    pe.wait_ge(*ring.space(tag, i))
                    expert_out(i, e, heads)

                def turn_y(i, s):
                    pe.wait_ge(y_ready, nth(i, s))
                    pe.wait_ge(*ring.space(f"yT{s}", i))
                    for c in range(NCH):
                        mm = pe.transpose(ring.bank(f"yT{s}")[:, c * P:(c + 1) * P], y[:, c * P:(c + 1) * P], ident[:, :])
                    mm.then_inc(ring.full(f"yT{s}"), 1)

                def project(i, s):
                    o = ring.bank(f"proj{s}")
                    pe.wait_ge(*ring.space(f"proj{s}", i))
                    if s == 0:
                        pe.wait_ge(*ring.copied("cT", i))
                    pe.matmul(o[:, 0:C], combT[:, s * P:(s + 1) * P], b2[:, :], start=True, stop=False)
                    pe.wait_ge(*ring.copied(f"yT{s}", i))
                    for c in range(NCH):
                        mm = pe.matmul(o[:, 0:C], yT[:, c, :], wproj[:, c, :], start=False, stop=c == NCH - 1)
                    mm.then_inc(ring.full(f"proj{s}"), 1)

                def turn_x(i):
                    pe.wait_ge(xn_ready, i + 1)
                    turn_block(pe, ring, ("xT0", "xT1"), i, xn, ident)

                def body(i, more):
                    pe.wait_ge(x_low_ready, i + 1)
                    expert_in(i, 0)
                    turn_comb(i)
                    turn_qk(i, 0)
                    for s in range(SUBS):
                        e, last = 2 * s + 1, s == SUBS - 1
                        scores(i, s)
                        expert_in(i, e)
                        expert_out(i, e - 1)
                        if not last:
                            qkv(i, s + 1)
                        elif more:
                            turn_x(i + 1)
                        else:
                            ring.skip(pe, NB, "xT0", "xT1")
                        turn_probs(i, s)
                        if not last:
                            expert_in(i, e + 1)
                        elif more:
                            gate(i + 1)
                        else:
                            ring.skip(pe, NB, "gate")
                        values_and_expert(i, s, e)
                        if not last:
                            turn_qk(i, s + 1)
                        elif more:
                            qkv(i + 1, 0)
                        else:
                            ring.skip(pe, NB, "qk0", "v0")
                        turn_y(i, s)
                        project(i, s)

                pe.wait_ge(w_loaded, 16 * len(weights))
                pe.wait_ge(setup_done, 2)
                ring.skip(pe, -1, *order[:order.index("xT0")])
                turn_x(0)
                gate(0)
                ring.skip(pe, -1, *order[order.index("gate") + 1:order.index("qk0")])
                qkv(0, 0)
                ring.skip(pe, -1, *order[order.index("v0") + 1:])
                blocks_loop(pe, body)

            @block.scalar
            def _(act):
                def squares(i, s):
                    act.wait_ge(*ring.data(f"qk{s}", i))
                    for t in range(2):
                        r = act.activation(sq[:, t, :], ring.bank(f"qk{s}")[:, t * C:(t + 1) * C], ACT.Square,
                                           scale=C ** -0.5, accum_out=ss[:, t:t + 1])
                    r.then_inc(ss_ready, 1)

                def copy(i, tag, dst, src):
                    act.wait_ge(*ring.data(tag, i))
                    act.copy(dst, src).then_inc(ring.free(tag), 1)

                def hidden(i, e, ms=range(ED // P)):
                    if e >= 2 and 0 in ms:
                        act.wait_ge(*ring.data(f"eo{e - 2}_1", i))
                    for m in ms:
                        tag = f"h{e}_{m}"
                        act.wait_ge(*ring.data(tag, i))
                        act.activation(hT_high[:, e % 2, m, :], ring.bank(tag)[:, :], ACT.Relu, bias=b1[:, e, m:m + 1])
                        act.wait_ge(h_low_ready, lows(i, e, m) - 1)
                        act.activation(hT[:, :], ring.bank(tag)[:, :], ACT.Relu, bias=b1[:, e, m:m + 1])\
                           .then_inc(ring.free(tag), 1)

                def exponentials(i, s, js):
                    if 0 in js:
                        act.wait_ge(max_ready, nth(i, s))
                    for j in js:
                        for g in range(4):
                            n = 4 * j + g
                            r = act.activation(probs[:, j, g, :], wide[:, j, g * P:(g + 1) * P], ACT.Exp,
                                               bias=nm[:, n:n + 1], scale=D16 ** -0.5, accum_out=den[:, n:n + 1])
                        r.then_inc(probs_ready, 1)

                def keep_turned(i, s):
                    act.wait_ge(turned, nth(i, s))
                    act.copy(pT[:, 2:4, :, :].rearrange("p a b c -> p (a b c)"),
                             wide[:, 2:4, :].rearrange("p a b -> p (a b)")).then_inc(pT_act, 1)

                def copy_x(i):
                    for c in range(NCH):
                        act.wait_ge(*ring.data(f"xT{c}", i))
                        act.copy(xT[:, c, :], ring.bank(f"xT{c}")[:, :])
                        act.copy(xT_high[:, c, :], ring.bank(f"xT{c}")[:, :]).then_inc(ring.free(f"xT{c}"), 1)

                def qkv(i, s):
                    squares(i, s)
                    copy(i, f"v{s}", v[:, s % 2, :], ring.bank(f"v{s}")[:, 0:C])

                def copy_q(i, s):
                    copy(i, f"tq{s}", qkT[:, 0, :, :].rearrange("p a b -> p (a b)"), ring.bank(f"tq{s}")[:, :])

                def body(i, more):
                    hidden(i, 0)
                    copy_q(i, 0)
                    for s in range(SUBS):
                        e, last = 2 * s + 1, s == SUBS - 1
                        hidden(i, e, [0])
                        exponentials(i, s, [0])
                        hidden(i, e, [1])
                        exponentials(i, s, [1, 2, 3])
                        if not last:
                            qkv(i, s + 1)
                        elif more:
                            copy_x(i + 1)
                        keep_turned(i, s)
                        if not last:
                            hidden(i, e + 1)
                        if not last:
                            copy_q(i, s + 1)
                        elif more:
                            qkv(i + 1, 0)
                        tag = f"yT{s}"
                        copy(i, tag, yT[:, :, :].rearrange("p a b -> p (a b)"), ring.bank(tag)[:, 0:C])

                for n, (high, low, src) in enumerate(expert_weights):
                    act.wait_ge(staged[n % 2], 16 * (n // 2 + 1))
                    act.copy(high, stage[n % 2]).then_inc(w_rounded, 1)
                act.wait_ge(w_loaded, 16 * len(weights))
                copy_x(0)
                qkv(0, 0)
                blocks_loop(act, body)

            @block.vector
            def _(dve):
                def front_stats(i):
                    dve.wait_ge(x_loaded, 16 * (i + 1))
                    row_stats(dve, xin, st, mv).then_inc(stats_ready, 1)

                def front_norm(i):
                    dve.wait_ge(rs_ready, i + 1)
                    normalise(dve, xn, xin, mv, rs).then_inc(xn_ready, 1)

                def gate_scores(i):
                    dve.wait_ge(*ring.data("gate", i))
                    dve.tensor_tensor(score[:, :, :], ring.bank("gate")[:, 0:SUBS * NE].rearrange("p (s e) -> p s e", s=SUBS),
                                      gb[:, :].unsqueeze(1).broadcast_to([P, SUBS, NE]), ALU.add)\
                       .then_inc(ring.free("gate"), 1)
                    dve.drain()

                def combination(i):
                    for s in range(SUBS):
                        dve.max(top[:, s, :], score[:, s, :])
                    dve.drain()
                    for s in range(SUBS):
                        dve.max_index(topi[:, s, :], top[:, s, :], score[:, s, :])
                    dve.drain()
                    dve.tensor_copy(topf[:, :, :], topi[:, :, :])
                    dve.drain()
                    for s in range(SUBS):
                        for t in range(2):
                            dve.tensor_scalar(pick[:, t, s, :], iota[:, :], topf[:, s, t:t + 1], top[:, s, t:t + 1],
                                              ALU.is_equal, ALU.mult)
                    dve.drain()
                    dve.tensor_tensor(comb[:, :, :], pick[:, 0, :, :], pick[:, 1, :, :], ALU.add).then_inc(comb_ready, 1)

                def norm_qk(i, s):
                    tag = f"qk{s}"
                    dve.wait_ge(rr_ready, nth(i, s))
                    dve.wait_ge(*ring.data(tag, i))
                    for t in range(2):
                        r = dve.scalar_tensor_tensor(
                            out=qk[:, t, :, 0:D16],
                            in0=ring.bank(tag)[:, t * C:(t + 1) * C].rearrange("p (h d) -> p h d", h=H16),
                            scalar=rr[:, t:t + 1], in1=lnw[:, :].rearrange("p (h d) -> p h d", h=H16),
                            op0=ALU.mult, op1=ALU.mult)
                    r.then_inc(ring.free(tag), 1)

                def copy(i, tag, dst, src):
                    dve.wait_ge(*ring.data(tag, i))
                    dve.tensor_copy(dst, src).then_inc(ring.free(tag), 1)

                def add_expert(i, e):
                    dve.drain()
                    if e == 0:
                        dve.wait_ge(res_loaded, 16 * (i + 1))
                        dve.wait_ge(stored, (i + 1) * 32)
                    for s in range(SUBS):
                        tag = f"eo{e}_{s // 2}"
                        if s % 2 == 0:
                            dve.wait_ge(*ring.data(tag, i))
                        r = dve.scalar_tensor_tensor(
                            out=acc[:, s, :], in0=ring.bank(tag)[:, (s % 2) * C:(s % 2 + 1) * C],
                            scalar=comb[:, s, e:e + 1], in1=(acc if e else xres)[:, s, :], op0=ALU.mult, op1=ALU.add)
                        if s % 2 == 1:
                            r.then_inc(ring.free(tag), 1)
                    if e == 0:
                        dve.drain().then_inc(res_used, 1)

                def maxima(i, s):
                    dve.wait_ge(scores_done, nth(i, s))
                    dve.tensor_reduce(mx[:, :], wide[:, :, :].rearrange("p j (g k) -> p (j g) k", g=4), AX, ALU.max)
                    dve.drain()
                    dve.tensor_scalar(nm[:, :], mx[:, :], -(D16 ** -0.5), None, ALU.mult).then_inc(max_ready, 1)

                def keep_turned(i, s):
                    dve.wait_ge(turned, nth(i, s))
                    dve.tensor_copy(pT[:, 0:2, :, :].rearrange("p a b c -> p (a b c)"),
                                    wide[:, 0:2, :].rearrange("p a b -> p (a b)")).then_inc(pT_dve, 1)
                    dve.reciprocal(rden[:, :], den[:, :])
                    dve.drain()

                def outputs(i, s):
                    tag = f"pv{s}"
                    dve.wait_ge(*ring.data(tag, i))
                    dve.tensor_tensor(
                        y[:, :].rearrange("p (g j e) -> p j g e", g=4, j=4),
                        ring.bank(tag)[:, 0:C].rearrange("p (g j e) -> p j g e", g=4, j=4),
                        rden[:, :].rearrange("p (j g) -> p j g", j=4).unsqueeze(3).broadcast_to([P, 4, 4, D16]),
                        ALU.mult).then_inc(ring.free(tag), 1)
                    dve.drain().then_inc(y_ready, 1)

                def split_weights():
                    for n, (high, low, src) in enumerate(expert_weights):
                        dve.wait_ge(w_rounded, n + 1)
                        dve.tensor_tensor(low, stage[n % 2], high.bitcast(F32), ALU.subtract).then_inc(w_split, 1)

                def keep_low(i):
                    for c in range(NCH):
                        dve.wait_ge(*ring.copied(f"xT{c}", i))
                        r = dve.tensor_tensor(xT_low[:, c, :], xT[:, c, :], xT_high[:, c, :].bitcast(F32), ALU.subtract)
                    r.then_inc(x_low_ready, 1)

                def copy_k(i, s):
                    copy(i, f"tk{s}", qkT[:, 1, :, :].rearrange("p a b -> p (a b)"), ring.bank(f"tk{s}")[:, :])

                def norm_of_sum(i):
                    dve.wait_ge(rs2_ready, i + 1)
                    normalise(dve, xn1, acc, mv2, rs2).then_inc(xn1_ready, 1)

                def body(i, first, more):
                    copy(i, "cT", combT[:, :], ring.bank("cT")[0:NE, :])
                    copy_k(i, 0)
                    if not first:
                        norm_of_sum(i - 1)
                    for s in range(SUBS):
                        e, last = 2 * s + 1, s == SUBS - 1
                        maxima(i, s)
                        add_expert(i, e - 1)
                        if last and more:
                            keep_low(i + 1)
                        keep_turned(i, s)
                        if not last:
                            norm_qk(i, s + 1)
                        elif more:
                            gate_scores(i + 1)
                        if more and s == 1:
                            front_stats(i + 1)
                        outputs(i, s)
                        add_expert(i, e)
                        if not last:
                            copy_k(i, s + 1)
                        elif more:
                            combination(i + 1)
                            norm_qk(i + 1, 0)
                        if more and s == 2:
                            front_norm(i + 1)
                        tag = f"proj{s}"
                        dve.drain()
                        dve.wait_ge(*ring.data(tag, i))
                        dve.tensor_tensor(acc[:, s, :], ring.bank(tag)[:, 0:C], acc[:, s, :], ALU.add)\
                           .then_inc(ring.free(tag), 1)
                    dve.drain().then_inc(acc_ready, 1)
                    row_stats(dve, acc, st2, mv2).then_inc(stats2_ready, 1)

                dve.memset(qk[:, :, :, :], 0.0).then_inc(setup_done, 1)
                dve.wait_ge(w_loaded, 16 * len(weights))
                dve.tensor_copy(mask[:, :, :], maskf[:, :].unsqueeze(1).broadcast_to([P, 4, P])).then_inc(setup_done, 1)
                dve.drain()
                front_stats(0)
                front_norm(0)
                split_weights()
                keep_low(0)
                gate_scores(0)
                combination(0)
                norm_qk(0, 0)
                peeled_loop(dve, body)
                norm_of_sum(NB - 1)


def shifted_loads(sp, dst, src, i, loaded):
    sp.dma_start(dst[:, :, 0:P], token_rows(src, i, 1, 0, P)).then_inc(loaded, 16)
    sp.dma_start(dst[:, :, P:C], token_rows(src, i, 0, P, C)).then_inc(loaded, 16)


def local_attention(nc, buffers, sem, banks, wide, shared, t_in, scratch, w, src, dst, prefetch):
    ctx = ExitStack()
    with ctx:
        sb = buffers(ctx, "d_")
        ident, identb, neghalf = shared["ident"], shared["identb"], shared["neghalf"]
        maskf = sb("maskf", [P, 2, 2 * P])
        mask = sb("mask", [P, 2, 2, 2 * P], BF16)
        xin = sb("xin", [P, SUBS, C])
        xT = sb("xT", [P, NCH, BT])
        xT_high, xT_low = (sb("xT_" + n, [P, NCH, BT], F32R) for n in ("high", "low"))
        wqkv_high, wqkv_low = (sb("wqkv_" + n, [P, NCH, 3 * INNER], F32R) for n in ("high", "low"))
        xres = sb("xres", [P, SUBS, C])
        spare = w["wqkv"][:, :, :].rearrange("p c n -> p (c n)")
        turned_cols = 4 * 4 * P
        pT = spare[:, 0:turned_cols].rearrange("p (a b c) -> p a b c", a=4, b=4)
        xout = spare[:, turned_cols:turned_cols + SUBS * C].rearrange("p (s c) -> p s c", s=SUBS)
        rotary = sb("rotary", [P, SUBS, 4, D64 // 2])
        turn = sb("turn", [P, SUBS, 4, D64])
        junk = sb("junk", [P, 2, INNER])
        ss = sb("ss", [P, 2, H8])
        rr = sb("rr", [P, 2, 2, H8])
        rot = sb("rot", [P, 2, 2, INNER])
        qk = sb("qk", [P, 2, INNER])
        qT = sb("qT", [P, H8 // 2, P])
        kT = sb("kT", [P, H8 // 2, SUBS + 1, P])
        v = sb("v", [P, SUBS + 1, INNER])
        mx = sb("mx", [P, H8])
        scale = sb("scale", [P, H8])
        nm = sb("nm", [P, H8])
        probs = sb("probs", [P, 4, 2, 2 * P])
        den = sb("den", [P, H8])
        rden = sb("rden", [P, H8])
        o = sb("o", [P, INNER])
        oT = sb("oT", [P, INNER // P, P])

        order = []
        for s in range(SUBS):
            order += [f"{t}{s}" for t in ("q", "k", "v")]
            order += ["xT0", "xT1"] if s == SUBS - 1 else []
            order += [f"tq{s}", f"tk{s}"]
        ring = Ring(banks[0:3], sem, order, ("xT0", "xT1"))
        out_order = []
        for s in range(SUBS):
            out_order += [f"pv{s}", f"oT{s}", f"wo{s}"]
        out_ring = Ring(banks[3:4], lambda name: sem("out_" + name), out_order)

        def ahead(i, s, n, last):
            return (i, s + n) if s + n < SUBS else None if last else (i + 1, s + n - SUBS)

        def staggered(eng, body):
            body(0, True, False)
            with eng.Fori(1, NB - 1) as i:
                body(i, False, False)
            body(NB - 1, False, True)

        def place(h):
            pair, odd = h // 2, h % 2
            return 2 * odd + pair // 2, pair % 2

        setup_loaded, setup_done = sem("setup_loaded"), sem("setup_done")
        x_loaded, x_used, res_loaded, rotary_loaded = (
            sem("x_loaded"), sem("x_used"), sem("res_loaded"), sem("rotary_loaded"))
        w_rounded, w_split, x_low_ready = sem("w_rounded"), sem("w_split"), sem("x_low_ready")
        turn_ready, mask_ready, before_ready = sem("turn_ready"), sem("mask_ready"), sem("before_ready")
        squared, ss_ready, rr_ready = sem("squared"), sem("ss_ready"), sem("rr_ready")
        parts_ready, qk_ready = sem("parts_ready"), sem("qk_ready")
        scores_done, max_ready, probs_ready = sem("scores_done"), sem("max_ready"), sem("probs_ready")
        turned, pT_act, pT_dve = sem("turned"), sem("pT_act"), sem("pT_dve")
        o_ready, xout_ready, stored = sem("o_ready"), sem("xout_ready"), sem("stored")

        with nc.Block() as block:

            @block.sync
            def _(sp):
                def load(i):
                    shifted_loads(sp, xin, scratch[src], i, x_loaded)

                def load_rotary(i):
                    sp.dma_start(rotary[:, :, :, :],
                                 t_in["k_rotary"][bass.ds(i * BT, BT), :, :].rearrange("(s p) a d -> p s (a d)", p=P))\
                      .then_inc(rotary_loaded, 16)

                def load_res(i):
                    sp.dma_start(xres[:, :, :], token_rows(scratch[src], i, 1)).then_inc(res_loaded, 16)

                ring.open(sp)
                out_ring.open(sp)
                sp.sem_inc(stored, 16)
                load(0)
                load_rotary(0)
                load_res(0)
                sp.dma_start(maskf[:, :, :], t_in["k_mask_local"]).then_inc(setup_loaded, 16)
                for group in prefetch:
                    for d, a in group["loads"]:
                        sp.dma_start(whole(d), a).then_inc(group["loaded"], 16)

                def body(i, more):
                    if more:
                        sp.wait_ge(*ring.data("xT1", i))
                        load(i + 1)
                        sp.wait_ge(turn_ready, i + 1)
                        load_rotary(i + 1)
                    sp.wait_ge(xout_ready, i + 1)
                    if more:
                        load_res(i + 1)
                    sp.dma_start(token_rows(scratch[dst], i, 1), xout[:, :, :]).then_inc(stored, 16)

                blocks_loop(sp, body)
                sp.wait_ge(stored, 16 * (NB + 1))

            @block.gpsimd
            def _(pool):
                def tables(i):
                    for t, name in enumerate(("q_scale", "k_scale")):
                        for a, (table, scales) in enumerate(((2 * t, w[name]), (2 * t + 1, w[name + "_turned"]))):
                            r = pool.tensor_tensor(
                                turn[:, :, 2 * t + a, :].rearrange("p s (a d) -> p s a d", a=2),
                                rotary[:, :, table, :].unsqueeze(2).broadcast_to([P, SUBS, 2, D64 // 2]),
                                scales[:, :].rearrange("p (a d) -> p a d", a=2).unsqueeze(1)
                                            .broadcast_to([P, SUBS, 2, D64 // 2]), ALU.mult)
                    return r

                def rotate(i, s):
                    pool.wait_ge(parts_ready, nth(i, s))
                    pool.tensor_tensor(qk[:, :, :], rot[:, :, 0, :], rot[:, :, 1, :], ALU.add)
                    pool.drain()
                    pool.wait_ge(ss_ready, nth(i, s))
                    pool.tensor_tensor(rr[:, s % 2, :, :].rearrange("p a b -> p (a b)"), ss[:, :, :].rearrange("p a b -> p (a b)"),
                                       neghalf[:, :], ALU.pow).then_inc(rr_ready, 1)
                    pool.drain()
                    pool.tensor_tensor(qk[:, 1, :].rearrange("p (h d) -> p h d", h=H8),
                                       qk[:, 1, :].rearrange("p (h d) -> p h d", h=H8),
                                       rr[:, s % 2, 1, :].unsqueeze(2).broadcast_to([P, H8, D64]), ALU.mult).then_inc(qk_ready, 1)

                def body(i, more):
                    for s in range(SUBS):
                        if s == 0:
                            pool.wait_ge(rotary_loaded, 16 * (i + 1))
                            tables(i).then_inc(turn_ready, 1)
                        rotate(i, s)

                pool.memset(kT[:, :, 0, :], 0.0)
                pool.memset(v[:, 0, :], 0.0).then_inc(before_ready, 1)
                pool.wait_ge(w["loaded"], 16 * len(w["loads"]))
                for name in ("q_scale_turned", "k_scale_turned"):
                    r = pool.tensor_scalar(w[name][:, 0:D64 // 2], w[name][:, 0:D64 // 2], -1.0, None, ALU.mult)
                pool.drain()
                blocks_loop(pool, body)

            @block.tensor
            def _(pe):
                def channels(i, s, n):
                    tag = f"{'qkv'[n]}{s}"
                    pe.wait_ge(*ring.space(tag, i))
                    tokens, cols = slice(s * P, (s + 1) * P), slice(n * INNER, (n + 1) * INNER)
                    for c in range(NCH):
                        mm = split_product(pe, ring.bank(tag)[:, :], (xT_high[:, c, tokens], xT_low[:, c, tokens]),
                                           (wqkv_high[:, c, cols], wqkv_low[:, c, cols]), c == 0, c == NCH - 1)
                    mm.then_inc(ring.full(tag), 1)

                def turn_x(i):
                    pe.wait_ge(x_loaded, 32 * (i + 1))
                    turn_block(pe, ring, ("xT0", "xT1"), i, xin, ident)

                def turn_qk(i, s):
                    pe.wait_ge(qk_ready, nth(i, s))
                    for t, tag in enumerate((f"tq{s}", f"tk{s}")):
                        pe.wait_ge(*ring.space(tag, i))
                        for g in range(INNER // P):
                            mm = pe.transpose(ring.bank(tag)[:, g * P:(g + 1) * P], qk[:, t, g * P:(g + 1) * P], ident[:, :])
                        mm.then_inc(ring.full(tag), 1)

                def scores(i, s, previous):
                    if previous:
                        pe.wait_ge(pT_act, nth(*previous))
                        pe.wait_ge(pT_dve, nth(*previous))
                    pe.wait_ge(*ring.copied(f"tq{s}", i))
                    pe.wait_ge(*ring.copied(f"tk{s}", i))
                    if s == 0:
                        pe.wait_ge(mask_ready, i + 1)
                    for b in range(4):
                        pe.matmul(wide[:, b, :], identb[:, :], mask[:, int(s == 0), :, :].rearrange("p a b -> p (a b)"),
                                  start=True, stop=False)
                    for pair in (0, 2, 1, 3):
                        for odd in range(2):
                            h = 2 * pair + odd
                            b, half = place(h)
                            r = slice(D64 * odd, D64 * (odd + 1))
                            mm = pe.matmul(wide[:, b, half * 2 * P:(half + 1) * 2 * P], qT[r, pair, :],
                                           kT[r, pair, s:s + 2, :].rearrange("p a b -> p (a b)"),
                                           start=False, stop=half == 1)
                    mm.then_inc(scores_done, 1)

                def turn_probs(i, s):
                    pe.wait_ge(probs_ready, nth(i, s))
                    for b in range(4):
                        for g in range(4):
                            mm = pe.transpose(wide[:, b, g * P:(g + 1) * P],
                                              probs[:, b, g // 2, (g % 2) * P:(g % 2 + 1) * P], ident[:, :])
                    mm.then_inc(turned, 1)

                def values(i, s):
                    tag = f"pv{s}"
                    pe.wait_ge(pT_act, nth(i, s))
                    pe.wait_ge(pT_dve, nth(i, s))
                    pe.wait_ge(*ring.copied(f"v{s}", i))
                    pe.wait_ge(*out_ring.space(tag, i))
                    for h in range(H8):
                        b, half = place(h)
                        cols = slice(h * D64, (h + 1) * D64)
                        for k in range(2):
                            mm = pe.matmul(out_ring.bank(tag)[:, cols], pT[:, b, 2 * half + k, :], v[:, s + k, cols],
                                           start=k == 0, stop=k == 1)
                    mm.then_inc(out_ring.full(tag), 1)

                def turn_o(i, s):
                    tag = f"oT{s}"
                    pe.wait_ge(o_ready, nth(i, s))
                    pe.wait_ge(*out_ring.space(tag, i))
                    for g in range(INNER // P):
                        mm = pe.transpose(out_ring.bank(tag)[:, g * P:(g + 1) * P], o[:, g * P:(g + 1) * P], ident[:, :])
                    mm.then_inc(out_ring.full(tag), 1)

                def project(i, s):
                    tag = f"wo{s}"
                    pe.wait_ge(*out_ring.space(tag, i))
                    for g in range(INNER // P):
                        mm = pe.matmul(out_ring.bank(tag)[:, 0:C], oT[:, g, :], w["wo"][:, g, :],
                                       start=g == 0, stop=g == INNER // P - 1)
                    mm.then_inc(out_ring.full(tag), 1)

                def body(i, first, last):
                    for s in range(SUBS):
                        one, two = ahead(i, s, 1, last), ahead(i, s, 2, last)
                        before = (i, s - 1) if s else None if first else (i - 1, SUBS - 1)
                        if before:
                            values(*before)
                        if one:
                            turn_qk(*one)
                        if two:
                            if s == 2:
                                pe.wait_ge(x_low_ready, i + 2)
                            channels(*two, 0)
                        if before:
                            turn_o(*before)
                        if two:
                            channels(*two, 1)
                        if before:
                            project(*before)
                        turn_probs(i, s)
                        if two:
                            channels(*two, 2)
                        if s == 1 and not last:
                            turn_x(i + 1)
                        elif s == 1:
                            ring.skip(pe, NB, "xT0", "xT1")
                        if one:
                            scores(*one, (i, s))

                pe.wait_ge(w["loaded"], 16 * len(w["loads"]))
                pe.wait_ge(before_ready, 1)
                ring.skip(pe, -1, *order[:order.index("xT0")])
                turn_x(0)
                ring.skip(pe, -1, *order[order.index("xT1") + 1:])
                pe.wait_ge(w_split, 1)
                pe.wait_ge(x_low_ready, 1)
                for n in range(3):
                    channels(0, 0, n)
                turn_qk(0, 0)
                for n in range(3):
                    channels(0, 1, n)
                scores(0, 0, None)
                staggered(pe, body)
                values(NB - 1, SUBS - 1)
                turn_o(NB - 1, SUBS - 1)
                project(NB - 1, SUBS - 1)

            @block.scalar
            def _(act):
                def copy(i, tag, dst, src, ring=ring):
                    act.wait_ge(*ring.data(tag, i))
                    act.copy(dst, src).then_inc(ring.free(tag), 1)

                def copy_x(i):
                    for c in range(NCH):
                        act.wait_ge(*ring.data(f"xT{c}", i))
                        act.copy(xT_high[:, c, :], ring.bank(f"xT{c}")[:, :])
                        act.copy(xT[:, c, :], ring.bank(f"xT{c}")[:, :]).then_inc(ring.free(f"xT{c}"), 1)

                def copy_q(i, s):
                    copy(i, f"tq{s}", qT[:, :, :].rearrange("p a b -> p (a b)"), ring.bank(f"tq{s}")[:, :])

                def copy_v(i, s):
                    copy(i, f"v{s}", v[:, s + 1, :], ring.bank(f"v{s}")[:, :])

                def copy_o(i, s):
                    tag = f"oT{s}"
                    copy(i, tag, oT[:, :, :].rearrange("p a b -> p (a b)"), out_ring.bank(tag)[:, :], out_ring)

                def squares(i, s):
                    for t in range(2):
                        tag = f"{'qk'[t]}{s}"
                        act.wait_ge(*ring.data(tag, i))
                        r = act.activation(junk[:, t, :], ring.bank(tag)[:, :], ACT.Square)
                    r.then_inc(squared, 1)

                def exponentials(i, s, heads):
                    if 0 in heads:
                        act.wait_ge(max_ready, nth(i, s))
                    for h in heads:
                        b, half = place(h)
                        r = act.activation(probs[:, b, half, :], wide[:, b, half * 2 * P:(half + 1) * 2 * P], ACT.Exp,
                                           bias=nm[:, h:h + 1], scale=scale[:, h:h + 1], accum_out=den[:, h:h + 1])
                    if H8 - 1 in heads:
                        r.then_inc(probs_ready, 1)

                def keep_turned(i, s):
                    act.wait_ge(turned, nth(i, s))
                    act.copy(pT[:, 2:4, :, :].rearrange("p a b c -> p (a b c)"),
                             wide[:, 2:4, :].rearrange("p a b -> p (a b)")).then_inc(pT_act, 1)

                def body(i, first, last):
                    for s in range(SUBS):
                        one, two = ahead(i, s, 1, last), ahead(i, s, 2, last)
                        before = (i, s - 1) if s else None if first else (i - 1, SUBS - 1)
                        exponentials(i, s, range(H8 // 2))
                        if one:
                            copy_q(*one)
                        exponentials(i, s, range(H8 // 2, H8))
                        if before:
                            copy_o(*before)
                        if two:
                            squares(*two)
                        keep_turned(i, s)
                        if two:
                            copy_v(*two)
                        if s == 1 and not last:
                            copy_x(i + 1)
                        if s == SUBS - 1 and not last:
                            act.copy(v[:, 0, :], v[:, SUBS, :])

                act.wait_ge(w["loaded"], 16 * len(w["loads"]))
                act.copy(wqkv_high[:, :, :], w["wqkv"][:, :, :]).then_inc(w_rounded, 1)
                act.wait_ge(before_ready, 1)
                copy_x(0)
                squares(0, 0)
                copy_v(0, 0)
                copy_q(0, 0)
                squares(0, 1)
                copy_v(0, 1)
                staggered(act, body)
                copy_o(NB - 1, SUBS - 1)

            @block.vector
            def _(dve):
                def copy(i, tag, dst, src):
                    dve.wait_ge(*ring.data(tag, i))
                    dve.tensor_copy(dst, src).then_inc(ring.free(tag), 1)

                def keep_low(i):
                    for c in range(NCH):
                        dve.wait_ge(*ring.copied(f"xT{c}", i))
                        r = dve.tensor_tensor(xT_low[:, c, :], xT[:, c, :], xT_high[:, c, :].bitcast(F32), ALU.subtract)
                    r.then_inc(x_low_ready, 1)

                def rotate(i, s):
                    if s == 0:
                        dve.wait_ge(turn_ready, i + 1)
                    dve.wait_ge(squared, nth(i, s))
                    half = D64 // 2
                    for t in range(2):
                        tag = f"{'qk'[t]}{s}"
                        dve.wait_ge(*ring.data(tag, i))
                        x = ring.bank(tag)[:, :].rearrange("p (h d) -> p h d", h=H8)
                        cos = rot[:, t, 0, :].rearrange("p (h d) -> p h d", h=H8)
                        sin = rot[:, t, 1, :].rearrange("p (h d) -> p h d", h=H8)
                        dve.tensor_tensor(cos, x, turn[:, s, 2 * t, :].unsqueeze(1).broadcast_to([P, H8, D64]), ALU.mult)
                        for a in range(2):
                            here, there = slice(a * half, (a + 1) * half), slice((1 - a) * half, (2 - a) * half)
                            r = dve.tensor_tensor(
                                sin[:, :, here], x[:, :, there],
                                turn[:, s, 2 * t + 1, here].unsqueeze(1).broadcast_to([P, H8, half]), ALU.mult)
                        r.then_inc(ring.free(tag), 1)
                    dve.drain().then_inc(parts_ready, 1)

                def sums(i, s):
                    dve.tensor_reduce(ss[:, :, :], junk[:, :, :].rearrange("p t (h d) -> p t h d", h=H8), AX, ALU.add)
                    dve.drain()
                    dve.tensor_scalar(ss[:, :, :], ss[:, :, :], NORM_FLOOR, None, ALU.max).then_inc(ss_ready, 1)

                def maxima(i, s):
                    dve.wait_ge(scores_done, nth(i, s))
                    dve.tensor_reduce(mx[:, :].rearrange("p (pair odd) -> p odd pair", odd=2),
                                      wide[:, :, :].rearrange("p (o b) (a k) -> p o (b a) k", o=2, a=2), AX, ALU.max)
                    dve.tensor_scalar(scale[:, :], rr[:, s % 2, 0, :], QK_SCALE, None, ALU.mult)
                    dve.drain()
                    dve.scalar_tensor_tensor(out=nm[:, :], in0=mx[:, :], scalar=-1.0, in1=scale[:, :],
                                             op0=ALU.mult, op1=ALU.mult).then_inc(max_ready, 1)

                def keep_turned(i, s):
                    dve.wait_ge(turned, nth(i, s))
                    dve.tensor_copy(pT[:, 0:2, :, :].rearrange("p a b c -> p (a b c)"),
                                    wide[:, 0:2, :].rearrange("p a b -> p (a b)")).then_inc(pT_dve, 1)
                    dve.reciprocal(rden[:, :], den[:, :])
                    dve.drain()

                def outputs(i, s):
                    tag = f"pv{s}"
                    dve.wait_ge(*out_ring.data(tag, i))
                    dve.tensor_tensor(o[:, :].rearrange("p (h d) -> p h d", h=H8),
                                      out_ring.bank(tag)[:, :].rearrange("p (h d) -> p h d", h=H8),
                                      rden[:, :].unsqueeze(2).broadcast_to([P, H8, D64]), ALU.mult)\
                       .then_inc(out_ring.free(tag), 1)
                    dve.drain().then_inc(o_ready, 1)

                def keys(i, s):
                    tag = f"tk{s}"
                    copy(i, tag, kT[:, :, s + 1, :], ring.bank(tag)[:, :].rearrange("p (a b) -> p a b", a=H8 // 2))

                def add(i, s):
                    if s == 0:
                        dve.wait_ge(res_loaded, 16 * (i + 1))
                        dve.wait_ge(stored, 16 * (i + 1))
                    tag = f"wo{s}"
                    dve.wait_ge(*out_ring.data(tag, i))
                    dve.tensor_tensor(xout[:, s, :], out_ring.bank(tag)[:, 0:C], xres[:, s, :], ALU.add)\
                       .then_inc(out_ring.free(tag), 1)
                    if s == SUBS - 1:
                        dve.drain().then_inc(xout_ready, 1)

                def body(i, first, last):
                    for s in range(SUBS):
                        one, two = ahead(i, s, 1, last), ahead(i, s, 2, last)
                        before = (i, s - 1) if s else None if first else (i - 1, SUBS - 1)
                        maxima(i, s)
                        if s == 0:
                            dve.tensor_copy(mask[:, 1, :, :], mask[:, 0, :, :]).then_inc(mask_ready, 1)
                        if s == SUBS - 1 and not last:
                            dve.tensor_copy(kT[:, :, 0, :], kT[:, :, SUBS, :])
                        if before:
                            outputs(*before)
                        if one:
                            keys(*one)
                        if two:
                            rotate(*two)
                        keep_turned(i, s)
                        if two:
                            sums(*two)
                        if before:
                            add(*before)
                        if s == 1 and not last:
                            keep_low(i + 1)

                dve.wait_ge(setup_loaded, 16)
                dve.wait_ge(before_ready, 1)
                for n in range(2):
                    r = dve.tensor_copy(mask[:, n, :, :], maskf[:, n, :].unsqueeze(1).broadcast_to([P, 2, 2 * P]))
                r.then_inc(mask_ready, 1)
                dve.wait_ge(w_rounded, 1)
                dve.tensor_tensor(wqkv_low[:, :, :], w["wqkv"][:, :, :], wqkv_high[:, :, :].bitcast(F32), ALU.subtract)\
                   .then_inc(w_split, 1)
                keep_low(0)
                rotate(0, 0)
                sums(0, 0)
                keys(0, 0)
                rotate(0, 1)
                sums(0, 1)
                staggered(dve, body)
                outputs(NB - 1, SUBS - 1)
                add(NB - 1, SUBS - 1)


def local_ffn(nc, buffers, sem, banks, wide, shared, t_in, scratch, w, src, dst):
    ctx = ExitStack()
    with ctx:
        sb = buffers(ctx, "f_")
        ident, neghalf = shared["ident"], shared["neghalf"]
        xin = sb("xin", [P, SUBS, C])
        st = sb("st", [P, SUBS, 6])
        mv = sb("mv", [P, SUBS, 2])
        rs = sb("rs", [P, SUBS])
        xn = sb("xn", [P, SUBS, C])
        xT = sb("xT", [P, NCH, BT])
        xres = sb("xres", [P, SUBS, C])
        xb = sb("xb", [P, SUBS, C])
        xout = sb("xout", [P, SUBS, C])
        gate = sb("gate", [P, 2, BT])
        u = sb("u", [P, 2, BT])
        xT_high, xT_low = (sb("xT_" + n, [P, NCH, BT], F32R) for n in ("high", "low"))
        u_high, u_low = (sb("u_" + n, [P, HCH, BT], F32R) for n in ("high", "low"))
        w1_high, w1_low = (sb("w1_" + n, [P, NCH, 2, HCH * P], F32R) for n in ("high", "low"))
        w2_high, w2_low = (sb("w2_" + n, [P, HCH, C], F32R) for n in ("high", "low"))
        zeros = sb("zeros", [P, HCH * P - HID])

        order = []
        for m in range(HCH):
            order += [f"g{m}", f"a{m}"]
        order += ["xT0", "xT1"] + [f"y{s}" for s in range(SUBS)]
        ring = Ring(banks, sem, order, ("xT0", "xT1"))
        full = HID // P
        splits = [(w["w1"][:, :, t * HID:(t + 1) * HID], w1_high[:, :, t, 0:HID], w1_low[:, :, t, 0:HID])
                  for t in range(2)]
        splits.append((w["w2"][:, 0:full, :], w2_high[:, 0:full, :], w2_low[:, 0:full, :]))
        rest = HID - full * P
        splits.append((w["w2"][0:rest, full, :], w2_high[0:rest, full, :], w2_low[0:rest, full, :]))

        def chunks_low(i, m):
            return i * HCH + (m + 3)

        rows = [min(P, HID - m * P) for m in range(HCH)]

        x_loaded, res_loaded, stored = sem("x_loaded"), sem("res_loaded"), sem("stored")
        stats_ready, rs_ready, xn_ready = sem("stats_ready"), sem("rs_ready"), sem("xn_ready")
        xb_ready, xout_ready = sem("xb_ready"), sem("xout_ready")
        w_rounded, w_split = sem("w_rounded"), sem("w_split")
        x_low_ready, u_low_ready = sem("x_low_ready"), sem("u_low_ready")

        with nc.Block() as block:

            @block.sync
            def _(sp):
                def load(i):
                    shifted_loads(sp, xin, scratch[src], i, x_loaded)

                def load_res(i):
                    sp.dma_start(xres[:, :, :], token_rows(scratch[src], i, 1)).then_inc(res_loaded, 16)

                ring.open(sp)
                sp.sem_inc(stored, 16)
                sp.sem_inc(u_low_ready, 2)
                load(0)
                load_res(0)

                def body(i, more):
                    if more:
                        sp.wait_ge(xn_ready, i + 1)
                        load(i + 1)
                        sp.wait_ge(xb_ready, i + 1)
                        load_res(i + 1)
                    sp.wait_ge(xout_ready, i + 1)
                    rows_out = token_rows(scratch[dst], i, int(dst in PADDED))
                    sp.dma_start(rows_out, xout[:, :, :]).then_inc(stored, 16)

                blocks_loop(sp, body)
                sp.wait_ge(stored, 16 * (NB + 1))

            @block.gpsimd
            def _(pool):
                def front(i):
                    pool.wait_ge(stats_ready, i + 1)
                    inverse_root(pool, rs[:, :], mv[:, :, 1], shared["eps_ln"][:, :], neghalf[:, 0:SUBS]).then_inc(rs_ready, 1)

                def body(i, more):
                    pool.wait_ge(res_loaded, 16 * (i + 1))
                    pool.tensor_tensor(xb[:, :, :], xres[:, :, :], w["b2"][:, :].unsqueeze(1).broadcast_to([P, SUBS, C]),
                                       ALU.add).then_inc(xb_ready, 1)
                    for m, r in enumerate(rows):
                        if more and m == 3:
                            front(i + 1)
                        pool.wait_ge(*ring.copied(f"a{m}", i))
                        pool.tensor_tensor(u_low[0:r, m, :], u[0:r, m % 2, :], u_high[0:r, m, :].bitcast(F32),
                                           ALU.subtract).then_inc(u_low_ready, 1)
                    if more:
                        pool.wait_ge(xout_ready, i + 1)

                front(0)
                pool.wait_ge(w["loaded"], 16 * len(w["loads"]))
                blocks_loop(pool, body)

            @block.tensor
            def _(pe):
                def turn_x(i):
                    pe.wait_ge(xn_ready, i + 1)
                    turn_block(pe, ring, ("xT0", "xT1"), i, xn, ident)

                def body(i, more):
                    pe.wait_ge(x_low_ready, i + 1)
                    for m in range(HCH):
                        for t, tag in ((1, f"g{m}"), (0, f"a{m}")):
                            pe.wait_ge(*ring.space(tag, i))
                            for c in range(NCH):
                                cols = slice(m * P, (m + 1) * P)
                                mm = split_product(pe, ring.bank(tag)[:, :],
                                                   (w1_high[:, c, t, cols], w1_low[:, c, t, cols]),
                                                   (xT_high[:, c, :], xT_low[:, c, :]), c == 0, c == NCH - 1)
                            mm.then_inc(ring.full(tag), 1)
                    if more:
                        turn_x(i + 1)
                    else:
                        ring.skip(pe, NB, "xT0", "xT1")
                    for s in range(SUBS):
                        pe.wait_ge(*ring.space(f"y{s}", i))
                        for m, r in enumerate(rows):
                            if s == 0:
                                pe.wait_ge(u_low_ready, chunks_low(i, m))
                            cols = slice(s * P, (s + 1) * P)
                            mm = split_product(pe, ring.bank(f"y{s}")[:, 0:C],
                                               (u_high[0:r, m, cols], u_low[0:r, m, cols]),
                                               (w2_high[0:r, m, :], w2_low[0:r, m, :]), m == 0, m == HCH - 1)
                        mm.then_inc(ring.full(f"y{s}"), 1)

                ring.skip(pe, -1, *order[:order.index("xT0")])
                turn_x(0)
                ring.skip(pe, -1, *order[order.index("xT1") + 1:])
                pe.wait_ge(w_split, 1)
                blocks_loop(pe, body)

            @block.scalar
            def _(act):
                def copy_x(i):
                    for c in range(NCH):
                        tag = f"xT{c}"
                        act.wait_ge(*ring.data(tag, i))
                        for dst in (xT, xT_high):
                            r = act.activation(dst[:, c, :], ring.bank(tag)[:, :], ACT.Identity,
                                               bias=w["lb"][:, c:c + 1], scale=w["lg"][:, c:c + 1])
                        r.then_inc(ring.free(tag), 1)

                def body(i, more):
                    for m, r in enumerate(rows):
                        tag = f"g{m}"
                        if m >= 2:
                            act.wait_ge(*ring.copied(f"a{m - 2}", i))
                        act.wait_ge(*ring.data(tag, i))
                        act.activation(gate[0:r, m % 2, :], ring.bank(tag)[0:r, :], ACT.Gelu,
                                       bias=w["b1"][0:r, 1, m:m + 1]).then_inc(ring.free(tag), 1)
                    if more:
                        copy_x(i + 1)

                act.wait_ge(w["loaded"], 16 * len(w["loads"]))
                for whole_weights, high, low in splits:
                    act.copy(high, whole_weights).then_inc(w_rounded, 1)
                copy_x(0)
                blocks_loop(act, body)

            @block.vector
            def _(dve):
                def front_stats(i):
                    dve.wait_ge(x_loaded, 32 * (i + 1))
                    row_stats(dve, xin, st, mv).then_inc(stats_ready, 1)

                def front_norm(i):
                    dve.wait_ge(rs_ready, i + 1)
                    normalise(dve, xn, xin, mv, rs).then_inc(xn_ready, 1)

                def keep_low(i):
                    for c in range(NCH):
                        dve.wait_ge(*ring.copied(f"xT{c}", i))
                        r = dve.tensor_tensor(xT_low[:, c, :], xT[:, c, :], xT_high[:, c, :].bitcast(F32), ALU.subtract)
                    r.then_inc(x_low_ready, 1)

                def body(i, more):
                    for m, r in enumerate(rows):
                        dve.wait_ge(*ring.copied(f"g{m}", i))
                        dve.wait_ge(*ring.data(f"a{m}", i))
                        for dst in (u_high[0:r, m, :], u[0:r, m % 2, :]):
                            if dst.dtype == F32:
                                dve.wait_ge(u_low_ready, chunks_low(i, m) - 2)
                            d = dve.scalar_tensor_tensor(out=dst, in0=ring.bank(f"a{m}")[0:r, :],
                                                         scalar=w["b1"][0:r, 0, m:m + 1], in1=gate[0:r, m % 2, :],
                                                         op0=ALU.add, op1=ALU.mult)
                        d.then_inc(ring.free(f"a{m}"), 1)
                        if more and m == 1:
                            front_stats(i + 1)
                        if more and m == 3:
                            front_norm(i + 1)
                    if more:
                        keep_low(i + 1)
                    dve.wait_ge(xb_ready, i + 1)
                    dve.wait_ge(stored, 16 * (i + 1))
                    for s in range(SUBS):
                        dve.wait_ge(*ring.data(f"y{s}", i))
                        dve.tensor_tensor(xout[:, s, :], ring.bank(f"y{s}")[:, 0:C], xb[:, s, :], ALU.add)\
                           .then_inc(ring.free(f"y{s}"), 1)
                    dve.drain().then_inc(xout_ready, 1)

                dve.memset(zeros[:, :], 0.0)
                dve.wait_ge(w["loaded"], 16 * len(w["loads"]))
                for n, (whole_weights, high, low) in enumerate(splits):
                    dve.wait_ge(w_rounded, n + 1)
                    dve.tensor_tensor(low, whole_weights, high.bitcast(F32), ALU.subtract)
                dve.drain()
                for part in (w1_high, w1_low):
                    for c in range(NCH):
                        for t in range(2):
                            dve.tensor_copy(part[:, c, t, HID:HCH * P], zeros[:, :])
                dve.drain().then_inc(w_split, 1)
                front_stats(0)
                front_norm(0)
                keep_low(0)
                blocks_loop(dve, body)


POOL_D = 8
POOL_SUMS = POOL_D // 2


def linear_stage(nc, buffers, sem, banks, wide, shared, t_in, scratch, w, spare, out):
    ctx = ExitStack()
    with ctx:
        sb = buffers(ctx, "l_")
        ident, neghalf, eps = shared["ident"], shared["neghalf"], shared["eps_ln"]
        xin = sb("xin", [P, SUBS, C])
        st = sb("st", [P, SUBS, 6])
        mv = sb("mv", [P, SUBS, 2])
        rs = sb("rs", [P, SUBS])
        xn = sb("xn", [P, SUBS, C])
        xT = sb("xT", [P, NCH, BT])
        xb = sb("xb", [P, SUBS, C])
        x1, xl = spare
        base = sb("base", [P, C])
        z = sb("z", [P, 2 * C])
        neg = sb("neg", [P, 2 * C])
        ez = sb("ez", [P, 2 * C])
        f = sb("f", [P, 2, 2, C])
        v = sb("v", [P, 2, D16, H16])
        prod = sb("prod", [P, 2, D16, D16, H16])
        prod2 = sb("prod2", [P, D16, H16, D16])
        kv = sb("kv", [P, D16, D16])
        ksum = sb("ksum", [P, D16])
        dprod = sb("dprod", [P, H16, D16])
        den = sb("den", [P, 2, H16])
        y = sb("y", [P, C])
        yT = sb("yT", [P, NCH, P])
        x2 = sb("x2", [P, SUBS, C])
        st2 = sb("st2", [P, 6])
        mv2 = sb("mv2", [P, 2])
        rs2 = sb("rs2", [P, 1])
        xn2 = sb("xn2", [P, C])
        x2T = sb("x2T", [P, NCH, BT])
        hT = sb("hT", [P, MLP // P, 2 * P])
        rest = sb("rest", [P, SUBS, C])
        total = sb("total", [P, SUBS, C])

        order = []
        for s in range(SUBS):
            old, later = (s - 1) % SUBS, (s + 2) % SUBS
            order += [f"yT{old}"] + (["xT0", "xT1"] if s == 2 else [])
            order += [f"qk{later}", f"v{later}", f"wo{old}", f"num{s}", f"x2T{old}"]
        ring = Ring(banks, sem, order)
        mlp_order = []
        for pair in range(2):
            mlp_order += [f"h{pair}_{m}" for m in range(MLP // P)] + [f"p{2 * pair + k}" for k in range(2)]
        mlp_ring = Ring([wide[:, b, :] for b in range(4)], lambda name: sem("mlp_" + name), mlp_order)

        x_loaded, rest_loaded, stored = sem("x_loaded"), sem("rest_loaded"), sem("stored")
        stats_ready, rs_ready, xn_ready = sem("stats_ready"), sem("rs_ready"), sem("xn_ready")
        xb_ready, rest_ready, total_ready = sem("xb_ready"), sem("rest_ready"), sem("total_ready")
        z_ready, elu_ready, f_ready = sem("z_ready"), sem("elu_ready"), sem("f_ready")
        prod_pool, kv_ready = sem("prod_pool"), sem("kv_ready")
        prod2_pool, prod2_vector, y_ready = sem("prod2_pool"), sem("prod2_vector"), sem("y_ready")
        stats2_ready, rs2_ready, xn2_ready = sem("stats2_ready"), sem("rs2_ready"), sem("xn2_ready")

        def pipeline(eng, slot):
            def run(r, before, here, after):
                for s in range(SUBS):
                    def at(k, s=s):
                        turn, sub = divmod(s + k, SUBS)
                        return (r + turn, sub) if (before, here, after)[turn + 1] else None
                    slot(r, s, before, here, after, at)
            run(-1, False, False, True)
            run(0, False, True, True)
            with eng.Fori(1, NB - 1) as r:
                run(r, True, True, True)
            run(NB - 1, True, True, False)
            run(NB, True, False, False)

        def mlp_part(r, s, before, here):
            if s == SUBS - 1:
                return (r, 0, "in") if here else None
            return (r - 1, (0, 1, 1)[s], ("out", "in", "out")[s]) if before else None

        shape = [P, D16, D16, D16]

        def fkv(eng, s, lo, hi):
            fk = f[:, s % 2, 1, :].rearrange("p (d h) -> p d h", h=H16).unsqueeze(2).broadcast_to(shape)
            vt = v[:, s % 2, :, :].unsqueeze(1).broadcast_to(shape)
            return eng.tensor_tensor(prod[:, s % 2, lo:hi], fk[:, lo:hi], vt[:, lo:hi], ALU.mult)

        def fqkv(eng, s, lo, hi):
            fq = f[:, s % 2, 0, :].rearrange("p (h d) -> p d h", h=H16).unsqueeze(3).broadcast_to(shape)
            kvs = kv[:, :, :].unsqueeze(2).broadcast_to(shape)
            return eng.tensor_tensor(prod2[:, lo:hi], fq[:, lo:hi], kvs[:, lo:hi], ALU.mult)

        with nc.Block() as block:

            @block.sync
            def _(sp):
                def load_x(b):
                    sp.dma_start(xin[:, :, :], token_rows(scratch["xn1"], b, 1)).then_inc(x_loaded, 16)

                def load_rest(b):
                    sp.dma_start(x1[:, :, :], token_rows(scratch["x1"], b)).then_inc(rest_loaded, 16)
                    sp.dma_start(xl[:, :, :], token_rows(scratch["xl2"], b)).then_inc(rest_loaded, 16)

                ring.open(sp)
                mlp_ring.open(sp)
                sp.sem_inc(stored, 16)
                load_x(0)
                load_rest(0)

                def slot(r, s, before, here, after, at):
                    if s == 0 and here and after:
                        sp.wait_ge(xn_ready, r + 1)
                        sp.wait_ge(xb_ready, r + 1)
                        load_x(r + 1)
                    if s == 1 and before and here:
                        sp.wait_ge(rest_ready, nth(r - 1, SUBS - 1))
                        load_rest(r)
                    if s == 3 and before:
                        sp.wait_ge(total_ready, r)
                        sp.dma_start(token_rows(out, r - 1), total[:, :, :]).then_inc(stored, 16)

                pipeline(sp, slot)
                sp.wait_ge(stored, 16 * (NB + 1))

            @block.gpsimd
            def _(pool):
                def slot(r, s, before, here, after, at):
                    old, cur, nxt = at(-1), at(0), at(1)
                    if nxt:
                        pool.wait_ge(f_ready, nth(*nxt))
                        fkv(pool, nxt[1], D16 - POOL_D, D16).then_inc(prod_pool, 1)
                    if cur:
                        pool.wait_ge(kv_ready, nth(*cur))
                        fqkv(pool, s, D16 - POOL_D, D16)
                        pool.drain()
                        kept = prod2[:, D16 - POOL_D:D16 - POOL_D + POOL_SUMS]
                        pool.tensor_tensor(kept, kept, prod2[:, D16 - POOL_SUMS:D16], ALU.add).then_inc(prod2_pool, 1)
                    if old:
                        pool.wait_ge(stats2_ready, nth(*old))
                        inverse_root(pool, rs2[:, :], mv2[:, 1:2], eps[:, 0:1], neghalf[:, 0:1]).then_inc(rs2_ready, 1)
                    if s == 0 and here:
                        bias = w["bo"][:, :].unsqueeze(1).broadcast_to([P, SUBS, C])
                        pool.tensor_tensor(xb[:, :, :], xin[:, :, :], bias, ALU.add).then_inc(xb_ready, 1)
                    if s == 1 and after:
                        pool.wait_ge(stats_ready, r + 2)
                        inverse_root(pool, rs[:, :], mv[:, :, 1], eps[:, :], neghalf[:, 0:SUBS]).then_inc(rs_ready, 1)
                    if old:
                        b, o = old
                        if o == 0:
                            pool.wait_ge(rest_loaded, 32 * (b + 1))
                        pool.tensor_tensor(base[:, :], x1[:, o, :], xl[:, o, :], ALU.add)
                        pool.drain()
                        pool.tensor_tensor(base[:, :], base[:, :], w["projb"][:, :], ALU.add)
                        pool.drain()
                        pool.tensor_tensor(rest[:, o, :], base[:, :], x2[:, o, :], ALU.add).then_inc(rest_ready, 1)
                        pool.drain()

                pool.wait_ge(w["loaded"], 16 * len(w["loads"]))
                pipeline(pool, slot)

            @block.tensor
            def _(pe):
                def turn(use, tag, x):
                    pe.wait_ge(*ring.space(tag, use))
                    for c in range(NCH):
                        mm = pe.transpose(ring.bank(tag)[:, c * P:(c + 1) * P], x[:, c * P:(c + 1) * P], ident[:, :])
                    mm.then_inc(ring.full(tag), 1)

                def mlp(part, use, half):
                    i, pair, layer = part
                    if layer == "in":
                        if half == 0:
                            pe.wait_ge(*ring.copied(f"x2T{2 * pair + 1}", use))
                        for m in range(half * MLP // P // 2, (half + 1) * MLP // P // 2):
                            tag = f"h{pair}_{m}"
                            pe.wait_ge(*mlp_ring.space(tag, i))
                            for c in range(NCH):
                                mm = pe.matmul(mlp_ring.bank(tag)[:, 0:2 * P], w["fc"][:, c, m * P:(m + 1) * P],
                                               x2T[:, c, pair * 2 * P:(pair + 1) * 2 * P],
                                               start=c == 0, stop=c == NCH - 1)
                            mm.then_inc(mlp_ring.full(tag), 1)
                    else:
                        tag = f"p{2 * pair + half}"
                        pe.wait_ge(*mlp_ring.space(tag, i))
                        for m in range(MLP // P):
                            if half == 0:
                                pe.wait_ge(*mlp_ring.copied(f"h{pair}_{m}", i))
                            mm = pe.matmul(mlp_ring.bank(tag)[:, 0:C], hT[:, m, half * P:(half + 1) * P],
                                           w["proj"][:, m, :], start=m == 0, stop=m == MLP // P - 1)
                        mm.then_inc(mlp_ring.full(tag), 1)

                def slot(r, s, before, here, after, at):
                    old, cur, later, use = at(-1), at(0), at(2), r + 1
                    part = mlp_part(r, s, before, here)
                    o, n = (s - 1) % SUBS, (s + 2) % SUBS
                    if old:
                        pe.wait_ge(y_ready, nth(*old))
                        turn(use, f"yT{o}", y)
                    else:
                        ring.skip(pe, use, f"yT{o}")
                    if s == 2 and after:
                        pe.wait_ge(xn_ready, r + 2)
                        turn_block(pe, ring, ("xT0", "xT1"), use, xn, ident)
                        for tag in ("xT0", "xT1"):
                            pe.wait_ge(*ring.copied(tag, use))
                    elif s == 2:
                        ring.skip(pe, use, "xT0", "xT1")
                    if later:
                        for tag, lo, hi in ((f"qk{n}", 0, 2 * C), (f"v{n}", 2 * C, 3 * C)):
                            pe.wait_ge(*ring.space(tag, use))
                            for c in range(NCH):
                                mm = pe.matmul(ring.bank(tag)[:, 0:hi - lo], xT[:, c, n * P:(n + 1) * P],
                                               w["wqkv"][:, c, lo:hi], start=c == 0, stop=c == NCH - 1)
                            mm.then_inc(ring.full(tag), 1)
                    else:
                        ring.skip(pe, use, f"qk{n}", f"v{n}")
                    if old:
                        pe.wait_ge(*ring.space(f"wo{o}", use))
                        pe.wait_ge(*ring.copied(f"yT{o}", use))
                        for c in range(NCH):
                            mm = pe.matmul(ring.bank(f"wo{o}")[:, 0:C], yT[:, c, :], w["wo"][:, c, :],
                                           start=c == 0, stop=c == NCH - 1)
                        mm.then_inc(ring.full(f"wo{o}"), 1)
                    else:
                        ring.skip(pe, use, f"wo{o}")
                    if part:
                        mlp(part, use, 0)
                    if cur:
                        tag = f"num{s}"
                        pe.wait_ge(*ring.space(tag, use))
                        pe.wait_ge(prod2_vector, nth(*cur))
                        for d in range(D16 - POOL_SUMS):
                            if d == D16 - POOL_D:
                                pe.wait_ge(prod2_pool, nth(*cur))
                            mm = pe.matmul(ring.bank(tag)[:, 0:C], ident[:, :],
                                           prod2[:, d, :, :].rearrange("p h e -> p (h e)"), start=d == 0,
                                           stop=d == D16 - POOL_SUMS - 1)
                        mm.then_inc(ring.full(tag), 1)
                    else:
                        ring.skip(pe, use, f"num{s}")
                    if part:
                        mlp(part, use, 1)
                    if old:
                        pe.wait_ge(xn2_ready, nth(*old))
                        turn(use, f"x2T{o}", xn2)
                    else:
                        ring.skip(pe, use, f"x2T{o}")

                pe.wait_ge(w["loaded"], 16 * len(w["loads"]))
                pipeline(pe, slot)

            @block.scalar
            def _(act):
                def gelu(part, half):
                    i, pair, layer = part
                    if layer == "in":
                        for m in range(half * MLP // P // 2, (half + 1) * MLP // P // 2):
                            tag = f"h{pair}_{m}"
                            act.wait_ge(*mlp_ring.data(tag, i))
                            act.activation(hT[:, m, :], mlp_ring.bank(tag)[:, 0:2 * P], ACT.Gelu,
                                           bias=w["fcb"][:, m:m + 1]).then_inc(mlp_ring.free(tag), 1)

                def slot(r, s, before, here, after, at):
                    old, later, use = at(-1), at(2), r + 1
                    part = mlp_part(r, s, before, here)
                    o = (s - 1) % SUBS
                    if old:
                        tag = f"yT{o}"
                        act.wait_ge(*ring.data(tag, use))
                        act.copy(yT[:, :, :].rearrange("p a b -> p (a b)"), ring.bank(tag)[:, 0:C])\
                           .then_inc(ring.free(tag), 1)
                    if s == 2 and after:
                        for c in range(NCH):
                            tag = f"xT{c}"
                            act.wait_ge(*ring.data(tag, use))
                            act.activation(xT[:, c, :], ring.bank(tag)[:, :], ACT.Identity, bias=w["o1"][:, c:c + 1],
                                           scale=w["g1"][:, c:c + 1]).then_inc(ring.free(tag), 1)
                    if part:
                        gelu(part, 0)
                    if later:
                        act.wait_ge(z_ready, nth(*later))
                        act.activation(neg[:, :], z[:, :], ACT.Relu, scale=-1.0)
                        act.drain()
                        act.activation(ez[:, :], neg[:, :], ACT.Exp, scale=-1.0).then_inc(elu_ready, 1)
                    if part:
                        gelu(part, 1)
                    if old:
                        tag = f"x2T{o}"
                        act.wait_ge(*ring.data(tag, use))
                        for c in range(NCH):
                            a = act.activation(x2T[:, c, o * P:(o + 1) * P], ring.bank(tag)[:, c * P:(c + 1) * P],
                                               ACT.Identity, bias=w["o2"][:, c:c + 1], scale=w["g2"][:, c:c + 1])
                        a.then_inc(ring.free(tag), 1)

                act.wait_ge(w["loaded"], 16 * len(w["loads"]))
                pipeline(act, slot)

            @block.vector
            def _(dve):
                def weigh(b, s):
                    tag = f"num{s}"
                    dve.wait_ge(*ring.data(tag, b + 1))
                    dve.tensor_tensor(y[:, :].rearrange("p (h e) -> p h e", h=H16),
                                      ring.bank(tag)[:, 0:C].rearrange("p (h e) -> p h e", h=H16),
                                      den[:, s % 2, :].unsqueeze(2).broadcast_to([P, H16, D16]), ALU.mult)\
                       .then_inc(ring.free(tag), 1)
                    dve.drain().then_inc(y_ready, 1)

                def features(b, s):
                    fs, d = f[:, s % 2, :, :], den[:, s % 2, :]
                    dve.wait_ge(elu_ready, nth(b, s))
                    dve.scalar_tensor_tensor(fs.rearrange("p a b -> p (a b)"), z[:, :], 0.0, ez[:, :], ALU.max, ALU.add)
                    dve.drain().then_inc(f_ready, 1)
                    dve.tensor_reduce(ksum[:, :], fs[:, 1, :].rearrange("p (d h) -> p d h", h=H16), AX, ALU.add)
                    dve.drain()
                    dve.tensor_tensor(dprod[:, :, :], fs[:, 0, :].rearrange("p (h d) -> p h d", h=H16),
                                      ksum[:, :].unsqueeze(1).broadcast_to([P, H16, D16]), ALU.mult)
                    dve.drain()
                    dve.tensor_reduce(d, dprod[:, :, :], AX, ALU.add)
                    dve.drain()
                    dve.tensor_scalar(d, d, 1e-6, None, ALU.add)
                    dve.drain()
                    dve.reciprocal(d, d)

                def project_in(use, b, s):
                    dve.wait_ge(*ring.data(f"qk{s}", use))
                    dve.tensor_tensor(z[:, 0:C], ring.bank(f"qk{s}")[:, 0:C], w["bqkv"][:, 0:C], ALU.add)
                    dve.tensor_tensor(z[:, C:2 * C].rearrange("p (d h) -> p h d", h=H16),
                                      ring.bank(f"qk{s}")[:, C:2 * C].rearrange("p (h d) -> p h d", h=H16),
                                      w["bqkv"][:, C:2 * C].rearrange("p (h d) -> p h d", h=H16), ALU.add)\
                       .then_inc(ring.free(f"qk{s}"), 1)
                    dve.wait_ge(*ring.data(f"v{s}", use))
                    dve.tensor_tensor(v[:, s % 2, :, :].rearrange("p e h -> p h e"),
                                      ring.bank(f"v{s}")[:, 0:C].rearrange("p (h e) -> p h e", h=H16),
                                      w["bqkv"][:, 2 * C:3 * C].rearrange("p (h e) -> p h e", h=H16), ALU.add)\
                       .then_inc(ring.free(f"v{s}"), 1)
                    dve.drain().then_inc(z_ready, 1)

                def add(i, s):
                    if s == 0:
                        dve.wait_ge(stored, 16 * (i + 1))
                    dve.wait_ge(rest_ready, nth(i, s))
                    dve.wait_ge(*mlp_ring.data(f"p{s}", i))
                    dve.tensor_tensor(total[:, s, :], mlp_ring.bank(f"p{s}")[:, 0:C], rest[:, s, :], ALU.add)\
                       .then_inc(mlp_ring.free(f"p{s}"), 1)

                def slot(r, s, before, here, after, at):
                    old, cur, nxt, later, use = at(-1), at(0), at(1), at(2), r + 1
                    if old:
                        weigh(*old)
                    if nxt:
                        features(*nxt)
                    if s == 1 and before:
                        add(r - 1, 0)
                        add(r - 1, 1)
                    if s == 3 and before:
                        add(r - 1, 2)
                        add(r - 1, 3)
                        dve.drain().then_inc(total_ready, 1)
                    if cur:
                        dve.wait_ge(prod_pool, nth(*cur))
                        dve.tensor_reduce(kv[:, :, :].rearrange("p a b -> p (a b)"),
                                          prod[:, s % 2].rearrange("p d e h -> p (d e) h"), AX, ALU.add)
                        dve.drain().then_inc(kv_ready, 1)
                        fqkv(dve, s, 0, D16 - POOL_D).then_inc(prod2_vector, 1)
                    if later:
                        project_in(use, *later)
                    if s == 1 and after:
                        dve.wait_ge(x_loaded, 16 * (r + 2))
                        row_stats(dve, xin, st, mv).then_inc(stats_ready, 1)
                    if old:
                        o = old[1]
                        if o == 0:
                            dve.wait_ge(xb_ready, old[0] + 1)
                        dve.wait_ge(*ring.data(f"wo{o}", use))
                        dve.tensor_tensor(x2[:, o, :], ring.bank(f"wo{o}")[:, 0:C], xb[:, o, :], ALU.add)\
                           .then_inc(ring.free(f"wo{o}"), 1)
                        dve.drain()
                        dve.bn_stats(st2[:, :], x2[:, o, :])
                        dve.drain()
                        dve.bn_aggr(mv2[:, :], st2[:, :]).then_inc(stats2_ready, 1)
                    if nxt:
                        fkv(dve, nxt[1], 0, D16 - POOL_D)
                    if old:
                        dve.wait_ge(rs2_ready, nth(*old))
                        dve.tensor_scalar(xn2[:, :], x2[:, old[1], :], mv2[:, 0:1], rs2[:, 0:1], ALU.subtract, ALU.mult)\
                           .then_inc(xn2_ready, 1)
                    if s == 1 and after:
                        dve.wait_ge(rs_ready, r + 2)
                        normalise(dve, xn, xin, mv, rs).then_inc(xn_ready, 1)
                    dve.drain()

                dve.wait_ge(w["loaded"], 16 * len(w["loads"]))
                pipeline(dve, slot)


_INS = ['L0_attn_x', 'L0_attn_w_qkv', 'L0_attn_ln_w', 'L0_attn_w_proj', 'L0_ffn_gate_w', 'L0_ffn_gate_b', 'L0_ffn_w1',
        'L0_ffn_b1', 'L0_ffn_w2', 'L0_ffn_b2', 'L1_attn_ln1_w', 'L1_attn_ln1_b', 'L1_attn_wq', 'L1_attn_bq',
        'L1_attn_wk', 'L1_attn_bk', 'L1_attn_wv', 'L1_attn_bv', 'L1_attn_wo', 'L1_attn_bo', 'L1_attn_ln2_w',
        'L1_attn_ln2_b', 'L1_attn_fc_w', 'L1_attn_fc_b', 'L1_attn_proj_w', 'L1_attn_proj_b', 'L1_ffn_wqkv',
        'L1_ffn_q_scale', 'L1_ffn_k_scale', 'L1_ffn_wo', 'L1_ffn_ln_g', 'L1_ffn_ln_b', 'L1_ffn_w1', 'L1_ffn_b1',
        'L1_ffn_w2', 'L1_ffn_b2']


def shape_constants():
    import numpy as np

    masked = np.float32(-1e30)
    q, k = np.arange(P)[:, None], np.arange(P)[None, :]
    group = 64
    local = np.concatenate([q <= k, k <= q], axis=1)
    first = np.concatenate([np.zeros((P, P), bool), k <= q], axis=1)
    half = np.arange(0, D64, 2, dtype=np.float32)
    freq = (np.float32(1.0) / np.float32(10000.0) ** (half / np.float32(D64))).astype(np.float32)
    t = np.arange(NT, dtype=np.float32)
    angle = (t[:, None] * freq[None, :]).astype(np.float32)
    base = ((half + np.float32(0.4 * D64)) / np.float32(1.4 * D64)).astype(np.float32)
    power = ((t - NT // 2) / np.float32(P // 2)).astype(np.float32)
    scale = (base[None, :] ** power[:, None]).astype(np.float32)
    cos, sin = np.cos(angle), np.sin(angle)
    return {
        "k_ident": np.eye(P, dtype=np.float32),
        "k_iota": np.arange(NE, dtype=np.float32),
        "k_mask_group": np.where((k <= q) & (k // group == q // group), np.float32(0), masked),
        "k_mask_local": np.stack([np.where(m, np.float32(0), masked) for m in (local, first)], axis=1),
        "k_rotary": np.stack([cos * scale, sin * scale, cos / scale, sin / scale], axis=1).astype(np.float32),
    }


def kernel(**inputs):
    import numpy as _np
    import concourse.bacc as _bacc
    from concourse.bass_utils import run_bass_kernel_spmd as _run

    nc = _bacc.Bacc("TRN2", target_bir_lowering=False, num_devices=1)
    arrays, t_in = {}, {}
    for name in _INS:
        a = _np.ascontiguousarray(inputs[name])
        if name == 'L0_attn_x':
            name, a = 'x', a.reshape(NT, C)
        arrays[f"in_{name}"] = a
        t_in[name] = nc.dram_tensor(f"in_{name}", a.shape, mybir.dt.from_np(a.dtype), kind="ExternalInput").ap()
    for name, a in shape_constants().items():
        arrays[name] = a
        t_in[name] = nc.dram_tensor(name, a.shape, F32, kind="ExternalInput").ap()
    out = nc.dram_tensor("out_0_dram", (1, NT, C), F32, kind="ExternalOutput").ap()
    scratch = {name: nc.dram_tensor(f"s_{name}", (NT + (name in PADDED), C), F32).ap()
               for name in ("x1", "xl2") + PADDED}
    build(nc, t_in, out[0], scratch)
    r = _run(nc, [arrays], core_ids=[0])
    return r.results[0]["out_0_dram"]
```
